# Optimizing a Trainium2 kernel written in Bass

```python
import numpy as np
import jax
import jax.numpy as jnp

def _softmax(x, axis=-1):
    return jax.nn.softmax(x, axis=axis)

def _gelu(x):
    return jax.nn.gelu(x, approximate=True)

def _silu(x):
    return jax.nn.silu(x)

def _sigmoid(x):
    return jax.nn.sigmoid(x)

def _layernorm(x, axis=-1, eps=1e-05):
    m = jnp.mean(x, axis=axis, keepdims=True)
    v = jnp.var(x, axis=axis, keepdims=True)
    return (x - m) / jnp.sqrt(v + eps)

def _scatter_add(tgt, idx, src, axis=0):
    return tgt.at[idx].add(src)

def _segment_sum(src, seg, n):
    return jax.ops.segment_sum(src, seg, n)
kernel_name = 'mk_flamingo_gated_d2_seqx_r8_370c61'

def setup_inputs(seed: int=0):
    np.random.seed(seed)
    _w = jnp.asarray

    def _rec_inputs():
        import jax
        import jax.numpy as jnp
        _rk = jax.random.key(seed)
        x = -0.0002928 + 1 * jax.random.normal(jax.random.fold_in(_rk, 1), (64, 64, 128), jnp.float32)
        _lenS = 64 - jax.random.randint(jax.random.fold_in(_rk, 7), (64,), 0, max(1, 64 // 4) + 1, jnp.int32)
        _lenS2 = 64 - jax.random.randint(jax.random.fold_in(_rk, 8), (64,), 0, max(1, 64 // 4) + 1, jnp.int32)
        _ctx_1024P = jax.random.normal(jax.random.fold_in(_rk, 11), (64, 16, 128), jnp.float32)
        _ctx_1024c = jax.random.dirichlet(jax.random.fold_in(_rk, 511), 0.3 * jnp.ones((16,), jnp.float32), (64, 64))
        _ctx_1024t = jnp.einsum('bsk,bkd->bsd', _ctx_1024c, _ctx_1024P)
        _ctx_1024t = _ctx_1024t * jax.lax.rsqrt(jnp.mean(jnp.square(_ctx_1024t)) + 1e-12) * 0.953939
        ctx_1024 = -1.39393e-06 + 0.999914 * (_ctx_1024t + 0.3 * jax.random.normal(jax.random.fold_in(_rk, 611), (64, 64, 128), jnp.float32))
        _g = jax.random.normal(jax.random.fold_in(_rk, 9001), (2, 2), jnp.float32)
        _g = jnp.sign(_g) * jnp.maximum(jnp.abs(_g), 1.0) + (_g == 0) * 1.0
        g_xattn = _g[0]
        g_ffn = _g[1]
        return (x, ctx_1024, g_xattn, g_ffn)
    x, ctx_1024, g_xattn, g_ffn = _rec_inputs()

    def _L0_xattn_setup():
        import jax, jax.numpy as jnp
        import numpy as np
        B, T, D, H = (2, 256, 128, 16)
        DH = D // H
        key = jax.random.key(seed)
        ks = jax.random.split(key, 11)
        s = 1.0 / np.sqrt(D)
        return {'q': jax.random.normal(ks[0], (B, T, D), jnp.float32), 'k': jax.random.normal(ks[1], (B, T, D), jnp.float32), 'v': jax.random.normal(ks[2], (B, T, D), jnp.float32), 'wq_w': jax.random.normal(ks[3], (D, D), jnp.float32) * s, 'wq_b': jnp.zeros((D,), jnp.float32), 'wk_w': jax.random.normal(ks[4], (D, D), jnp.float32) * s, 'wk_b': jnp.zeros((D,), jnp.float32), 'wv_w': jax.random.normal(ks[5], (D, D), jnp.float32) * s, 'wv_b': jnp.zeros((D,), jnp.float32), 'wo_w': jax.random.normal(ks[6], (D, D), jnp.float32) * s, 'wo_b': jnp.zeros((D,), jnp.float32)}
    _L0_xattn_all = _L0_xattn_setup()
    _L0_xattn_in = {k: v for k, v in _L0_xattn_all.items() if k in ('wq_w', 'wq_b', 'wk_w', 'wk_b', 'wv_w', 'wv_b', 'wo_w', 'wo_b')}
    del _L0_xattn_all

    def _L0_ffn_setup():
        import jax, jax.numpy as jnp
        import numpy as np
        E = 8
        TOP_K = 2
        DIM = 128
        HID = 256
        key = jax.random.key(seed)
        k1, k2, k3, k4, k5 = jax.random.split(key, 5)
        s = 0.02
        x = jax.random.normal(k1, (2, 256, DIM), dtype=jnp.float32)
        Wg = jax.random.normal(k2, (DIM, E), dtype=jnp.float32) * s
        W1 = jax.random.normal(k3, (E, DIM, HID), dtype=jnp.float32) * s
        W2 = jax.random.normal(k4, (E, DIM, HID), dtype=jnp.float32) * s
        W3 = jax.random.normal(k5, (E, HID, DIM), dtype=jnp.float32) * s
        return {'x': x, 'Wg': Wg, 'W1': W1, 'W2': W2, 'W3': W3}
    _L0_ffn_all = _L0_ffn_setup()
    _L0_ffn_in = {k: v for k, v in _L0_ffn_all.items() if k in ('Wg', 'W1', 'W2', 'W3')}
    del _L0_ffn_all

    def _L1_xattn_setup():
        import jax, jax.numpy as jnp
        import numpy as np
        B, L_ENC, L_DEC, D = (16, 64, 128, 128)
        key = jax.random.key(seed)
        k1, k2, k3, k4, k5, k6 = jax.random.split(key, 6)
        encoder_hc = jax.random.normal(k1, (B, L_ENC, D), dtype=jnp.float32)
        decoder_hq = jax.random.normal(k2, (B, L_DEC, D), dtype=jnp.float32)
        w_sim = jax.random.normal(k3, (3 * D,), dtype=jnp.float32) * 0.02
        b_sim = jax.random.normal(k4, (1,), dtype=jnp.float32) * 0.02
        W_qv = jax.random.normal(k5, (4 * D, D), dtype=jnp.float32) * 0.02
        b_qv = jax.random.normal(k6, (D,), dtype=jnp.float32) * 0.02
        return {'encoder_hc': encoder_hc, 'decoder_hq': decoder_hq, 'w_sim': w_sim, 'b_sim': b_sim, 'W_qv': W_qv, 'b_qv': b_qv}
    _L1_xattn_all = _L1_xattn_setup()
    _L1_xattn_in = {k: v for k, v in _L1_xattn_all.items() if k in ('w_sim', 'b_sim', 'W_qv', 'b_qv')}
    del _L1_xattn_all

    def _L1_ffn_setup():
        import jax, jax.numpy as jnp
        import numpy as np
        E = 8
        K = 2
        R = 64
        ALPHA = 128.0
        SCALING = ALPHA / R
        key = jax.random.key(seed)
        k0, k1, k2, k3 = jax.random.split(key, 4)
        B, S, D = (4, 512, 128)
        x = jax.random.normal(k0, (B, S, D), jnp.float32)
        Wg = jax.random.normal(k1, (E, D), jnp.float32) * 0.02
        bg = jnp.zeros((E,), jnp.float32)
        W1 = jax.random.normal(k2, (E, R, D), jnp.float32) * (1.0 / np.sqrt(D))
        W2 = jax.random.normal(k3, (E, D, R), jnp.float32) * 0.02
        return {'x': x, 'Wg': Wg, 'bg': bg, 'W1': W1, 'W2': W2}
    _L1_ffn_all = _L1_ffn_setup()
    _L1_ffn_in = {k: v for k, v in _L1_ffn_all.items() if k in ('Wg', 'bg', 'W1', 'W2')}
    del _L1_ffn_all
    return {'x': x, 'ctx_1024': ctx_1024, 'g_xattn': g_xattn, 'g_ffn': g_ffn, 'L0_xattn_wq_w': _L0_xattn_in['wq_w'], 'L0_xattn_wq_b': _L0_xattn_in['wq_b'], 'L0_xattn_wk_w': _L0_xattn_in['wk_w'], 'L0_xattn_wk_b': _L0_xattn_in['wk_b'], 'L0_xattn_wv_w': _L0_xattn_in['wv_w'], 'L0_xattn_wv_b': _L0_xattn_in['wv_b'], 'L0_xattn_wo_w': _L0_xattn_in['wo_w'], 'L0_xattn_wo_b': _L0_xattn_in['wo_b'], 'L0_ffn_Wg': _L0_ffn_in['Wg'], 'L0_ffn_W1': _L0_ffn_in['W1'], 'L0_ffn_W2': _L0_ffn_in['W2'], 'L0_ffn_W3': _L0_ffn_in['W3'], 'L1_xattn_w_sim': _L1_xattn_in['w_sim'], 'L1_xattn_b_sim': _L1_xattn_in['b_sim'], 'L1_xattn_W_qv': _L1_xattn_in['W_qv'], 'L1_xattn_b_qv': _L1_xattn_in['b_qv'], 'L1_ffn_Wg': _L1_ffn_in['Wg'], 'L1_ffn_bg': _L1_ffn_in['bg'], 'L1_ffn_W1': _L1_ffn_in['W1'], 'L1_ffn_W2': _L1_ffn_in['W2']}

def reference(x, ctx_1024, g_xattn, g_ffn, L0_xattn_wq_w, L0_xattn_wq_b, L0_xattn_wk_w, L0_xattn_wk_b, L0_xattn_wv_w, L0_xattn_wv_b, L0_xattn_wo_w, L0_xattn_wo_b, L0_ffn_Wg, L0_ffn_W1, L0_ffn_W2, L0_ffn_W3, L1_xattn_w_sim, L1_xattn_b_sim, L1_xattn_W_qv, L1_xattn_b_qv, L1_ffn_Wg, L1_ffn_bg, L1_ffn_W1, L1_ffn_W2):
    import jax
    import jax.numpy as jnp

    def _L0_xattn_ref(q, k, v, wq_w, wq_b, wk_w, wk_b, wv_w, wv_b, wo_w, wo_b):
        import jax, jax.numpy as jnp
        import numpy as np
        B, T, D, H = (2, 256, 128, 16)
        DH = D // H
        b, t, d = q.shape
        wq = (q @ wq_w.T + wq_b).reshape(b, t, H, DH)
        wk = (k @ wk_w.T + wk_b).reshape(b, t, H, DH)
        wv = (v @ wv_w.T + wv_b).reshape(b, t, H, DH)
        scores = jnp.einsum('bthd,bshd->bhts', wq, wk) / jnp.sqrt(jnp.float32(DH))
        probs = jax.nn.softmax(scores, axis=-1)
        attn = jnp.einsum('bhts,bshd->bthd', probs, wv)
        attn = attn.reshape(b, t, d)
        return attn @ wo_w.T + wo_b

    def _L0_ffn_ref(x, Wg, W1, W2, W3):
        import jax, jax.numpy as jnp
        import numpy as np
        E = 8
        TOP_K = 2
        DIM = 128
        HID = 256
        B, T, C = x.shape
        xf = x.reshape(-1, C)
        logits = xf @ Wg
        top_w, top_i = jax.lax.top_k(logits, TOP_K)
        top_w = jax.nn.softmax(top_w, axis=-1)
        one_hot = jax.nn.one_hot(top_i, E, dtype=xf.dtype)
        combine = jnp.einsum('nk,nke->ne', top_w, one_hot)
        h = jnp.einsum('nc,ech->enh', xf, W1)
        g = jnp.einsum('nc,ech->enh', xf, W2)
        y = jnp.einsum('enh,ehc->enc', jax.nn.silu(h) * g, W3)
        out = jnp.einsum('enc,ne->nc', y, combine)
        return out.reshape(B, T, C)

    def _L1_xattn_ref(encoder_hc, decoder_hq, w_sim, b_sim, W_qv, b_qv):
        import jax, jax.numpy as jnp
        import numpy as np
        B, L_ENC, L_DEC, D = (16, 64, 128, 128)
        d = encoder_hc.shape[-1]
        w1, w2, w3 = (w_sim[:d], w_sim[d:2 * d], w_sim[2 * d:])
        Sim = (encoder_hc @ w1)[:, :, None] + (decoder_hq @ w2)[:, None, :] + jnp.einsum('bid,bjd->bij', encoder_hc * w3, decoder_hq) + b_sim[0]
        A = jax.nn.softmax(Sim, axis=2)
        hq_hat = jnp.einsum('bij,bjd->bid', A, decoder_hq)
        Batt = jax.nn.softmax(jnp.max(Sim, axis=2), axis=1)
        hc_bar = jnp.einsum('bi,bid->bd', Batt, encoder_hc)[:, None, :]
        hc_hat = jnp.broadcast_to(hc_bar, encoder_hc.shape)
        feats = jnp.concatenate([encoder_hc, hq_hat, encoder_hc * hq_hat, encoder_hc * hc_hat], axis=-1)
        hcq = feats @ W_qv + b_qv
        return hcq

    def _L1_ffn_ref(x, Wg, bg, W1, W2):
        import jax, jax.numpy as jnp
        import numpy as np
        E = 8
        K = 2
        R = 64
        ALPHA = 128.0
        SCALING = ALPHA / R
        orig_shape = x.shape
        D = orig_shape[-1]
        xf = x.reshape(-1, D)
        logits = xf @ Wg.T + bg
        top_gates, top_idx = jax.lax.top_k(logits, K)
        top_gates = jax.nn.softmax(top_gates, axis=-1)
        h = jax.nn.gelu(jnp.einsum('nd,erd->enr', xf, W1), approximate=False)
        eout = SCALING * jnp.einsum('enr,edr->ned', h, W2)
        sel = jnp.take_along_axis(eout, top_idx[:, :, None], axis=1)
        out = jnp.sum(top_gates[:, :, None] * sel, axis=1)
        return out.reshape(orig_shape)
    x = x + jnp.tanh(g_xattn[0]) * _L0_xattn_ref(_layernorm(x, axis=-1), ctx_1024, ctx_1024, L0_xattn_wq_w, L0_xattn_wq_b, L0_xattn_wk_w, L0_xattn_wk_b, L0_xattn_wv_w, L0_xattn_wv_b, L0_xattn_wo_w, L0_xattn_wo_b)
    x = x + jnp.tanh(g_ffn[0]) * _L0_ffn_ref(_layernorm(x, axis=-1), L0_ffn_Wg, L0_ffn_W1, L0_ffn_W2, L0_ffn_W3)
    x = x + jnp.tanh(g_xattn[1]) * _L1_xattn_ref(_layernorm(x, axis=-1), ctx_1024, L1_xattn_w_sim, L1_xattn_b_sim, L1_xattn_W_qv, L1_xattn_b_qv)
    x = x + jnp.tanh(g_ffn[1]) * _L1_ffn_ref(_layernorm(x, axis=-1), L1_ffn_Wg, L1_ffn_bg, L1_ffn_W1, L1_ffn_W2)
    return x

_drawn_inputs = setup_inputs


def setup_inputs(seed=0):
    import zlib

    import numpy as np

    out = dict(_drawn_inputs(seed))
    spreads = {'g_ffn': (-1.0, 0.6),
     'L0_xattn_wq_b': (0.0, 0.36),
     'L0_xattn_wk_b': (0.0, 2.0),
     'L0_xattn_wv_b': (0.0, 0.1),
     'L0_xattn_wo_b': (0.0, 0.1),
     'L1_ffn_bg': (0.0, 0.302)}
    factors = {'L0_ffn_Wg': 8.0,
     'L0_ffn_W1': 8.0,
     'L0_ffn_W2': 7.874,
     'L0_ffn_W3': 7.968,
     'L1_xattn_w_sim': 7.428,
     'L1_xattn_b_qv': 7.847}
    for name, (base, spread) in spreads.items():
        noise = np.random.default_rng([zlib.crc32(name.encode()), seed]).standard_normal(out[name].shape)
        drawn = base * np.exp(spread * noise) if base else spread * noise
        out[name] = jnp.asarray(drawn.astype(out[name].dtype))
    for name, factor in factors.items():
        out[name] = (out[name] * factor).astype(out[name].dtype)
    return out
```

```python
from contextlib import ExitStack

import numpy as np

import concourse.bass as bass
from concourse import mybir

F32 = mybir.dt.float32
BF16 = mybir.dt.bfloat16
U32 = mybir.dt.uint32
ACT = mybir.ActivationFunctionType
ALU = mybir.AluOpType
AX = mybir.AxisListType.X

P = 128
D = 128
L = 64
NH = 16
DH = D // NH
NG = 4
HG = NH // NG
E = 8
HID = 256
R = 64
SCALING = 2.0
EPS = 1e-5
WRITTEN = {1: "a_x", 2: "b_acc", 3: "c_x"}
WRITES = {1: 1, 2: E, 3: 1}
FAR = -1e30
TOKENS = 64 * L
CH = TOKENS // P
UA = CH // 2
U4 = CH // 4

BQ, BK, BV, W1S, W2S, W3S = range(6)
C_ID, C_KM, C_VM, C_IO, C_BI = 0, 128, 132, 134, 142
C_N = 144
R_BO, R_BQV, R_BG, R_BS = 0, 128, 256, 264
R_N = 265


def constants():
    c = np.zeros((P, C_N), np.float32)
    p = np.arange(P)
    c[:, C_ID:C_ID + P] = np.eye(P)
    c[p, C_KM + (p % 32) // DH] = 1
    c[p, C_VM + p // L] = 1
    c[:, C_IO:C_IO + E] = np.arange(E)
    c[p, C_BI + p // L] = 1
    far = np.zeros((2, P + 4 * P), np.float32)
    far[0, :L] = FAR
    far[1, L:P] = FAR
    k = np.arange(4 * P) % P
    far[0, P:] = k >= L
    far[1, P:] = k < L
    return c, far


def flamingo(nc, x, ctx_tok, ctx_t, wq, wk, wv, wo, cols, rows, gates, consts, far,
             f0_wg, f0_w1, f0_w2, f0_w3, wqv, f1_wg, f1_w1, f1_w2, out):
    with ExitStack() as stack:
        def sb(name, shape, dt=F32):
            return stack.enter_context(nc.sbuf_tensor(name, shape, dt))

        def sem(name):
            return stack.enter_context(nc.semaphore(name))

        xs = sb("xs", [P, CH, D])
        ln = sb("ln", [P, CH, 2])
        cst = sb("cst", [P, C_N])
        colv = sb("colv", [P, 6])
        rowv = sb("rowv", [1, R_N])
        gate = sb("gate", [P, 4])
        tg = sb("tg", [P, 4])
        ones = sb("ones", [1, P])
        farf = sb("farf", [2, 5 * P])
        farb = sb("farb", [2, 5 * P], BF16)
        half = sb("half", [P, 4])
        stat = sb("stat", [P, 4, 6])
        mv = sb("mv", [P, 4, 2])
        ve = sb("ve", [P, 4])

        wq_s, wk_s, wv_s, wo_s = (sb(n, [P, D]) for n in ("wq_s", "wk_s", "wv_s", "wo_s"))
        wv_eo = sb("wv_eo", [P, 2, D])
        bqs = sb("bqs", [P, 1])
        bkm = sb("bkm", [P, HG])
        row0 = sb("row0", [1, D])
        row1 = sb("row1", [1, D])
        xn = sb("xn", [P, 2, 4, D])
        cT = sb("cT", [P, 2, 4 * P])
        ctk = sb("ctk", [P, 2, 4, D])
        xT = sb("xT", [P, 2, 4 * P])
        QT = sb("QT", [P, 2 * P])
        Kb = sb("Kb", [P, HG, 2 * P])
        Vb = sb("Vb", [P, 2, 4, NH // 2, 18])
        Pr = sb("Pr", [P, 2, NG, 512])
        PT = sb("PT", [P, NG, 512])
        mx = sb("mx", [P, NG, 8])
        rec = sb("rec", [P, NH, 2])
        att = sb("att", [P, 2 * D])
        attT = sb("attT", [P, 2 * P])

        f0g_s = sb("f0g_s", [P, E])
        f0w1_s = sb("f0w1_s", [P, E, HID])
        f0w2_s = sb("f0w2_s", [P, E, HID])
        f0w3_s = sb("f0w3_s", [P, E, 2, D])
        sil = sb("sil", [P, 4, 512])
        act = sb("act", [P, 4, 512])
        lg = sb("lg", [P, 4, E])
        top = sb("top", [P, 4, 8])
        idx = sb("idx", [P, 4, 8], U32)
        idf = sb("idf", [P, 4, 8])
        dif = sb("dif", [P, 4])
        pe2 = sb("pe2", [P, 4])
        den = sb("den", [P, 4])
        w1g = sb("w1g", [P, 4])
        w2g = sb("w2g", [P, 4])
        oh1 = sb("oh1", [P, 4, E])
        oh2 = sb("oh2", [P, 4, E])
        cmb = sb("cmb", [P, 4, E])

        wqv_s = sb("wqv_s", [P, 4, D])
        wqv_g = sb("wqv_g", [P, 4, D])
        e3 = sb("e3", [P, 4 * P])
        rmx = sb("rmx", [P, 4])
        nmx = sb("nmx", [P, 4])
        Pc = sb("Pc", [P, 2, 4, P])
        sm = sb("sm", [P, 2, 4])
        rsm = sb("rsm", [P, 4])
        mcol = sb("mcol", [P, 4])
        bm = sb("bm", [4, 2])
        brow = sb("brow", [4, 2, L])
        bs = sb("bs", [4, 2])
        br = sb("br", [4, 2])
        wrow = sb("wrow", [4, P])
        wbd = sb("wbd", [P, 4, 2])
        hc = sb("hc", [P, 8])
        PcT = sb("PcT", [P, 4 * P])
        hqT = sb("hqT", [P, 4 * P])
        ehq = sb("ehq", [P, 4 * P])
        ehc = sb("ehc", [P, 2, 4 * P])

        f1g_s = sb("f1g_s", [P, E])
        f1w1_s = sb("f1w1_s", [P, E * R])
        f1w2_s = sb("f1w2_s", [P, 4, D])
        hg = sb("hg", [P, 2, E * R])
        hgg = sb("hgg", [P, 2, E * R])
        hT = sb("hT", [P, 2, 4 * P])

        ident = cst[:, C_ID:C_ID + P]
        iota = cst[:, C_IO:C_IO + E]

        bank = [stack.enter_context(nc.psum_tensor(f"bank{i}", [P, 512], F32)) for i in range(8)]

        ld_x = [sem(f"ld_x{i}") for i in range(4)]
        ld_small, ld_attn, ld_f0, ld_c, ld_f1 = (
            sem(n) for n in ("ld_small", "ld_attn", "ld_f0", "ld_c", "ld_f1"))
        ld_cT = [sem(f"ld_cT{i}") for i in range(2)]
        ld_cC = [sem(f"ld_cC{i}") for i in range(2)]
        fill, prep, prep_pe, prep_act, prep_b0 = (
            sem(n) for n in ("fill", "prep", "prep_pe", "prep_act", "prep_b0"))
        names = {}

        def S(name):
            if name not in names:
                names[name] = sem(name)
            return names[name]

        START_AT_ONE = {
            "vector": ("a_x", "a_nrm", "b_act", "b_acc", "c_x", "d_hgg", "d_x", "mv0", "mv1", "mv2", "mv3"),
            "scalar": ("a_pts", "d_gelu", "d_hts"),
            "tensor": ("a_pv", "b_y", "d_ht", "d_y"),
            "gpsimd": ("ln0", "ln1", "ln2", "ln3"),
        }

        def start_at_one(eng, which):
            for name in START_AT_ONE[which]:
                eng.sem_inc(S(name), 1)

        block = stack.enter_context(nc.Block())
        x_v = x.rearrange("(t p) c -> p t c", p=P)
        out_v = out.rearrange("(t p) c -> p t c", p=P)
        ctx_v = ctx_tok.rearrange("(t p) c -> p t c", p=P)

        def wait_alone(eng, semaphore, value):
            if not isinstance(value, int):
                eng.compute_val(value)
            eng.wait_ge(ld_small, 80)
            eng.wait_ge(semaphore, value)

        def skewed(eng, units, body):
            with eng.Fori(0, units // 2 - 1) as i:
                body(i * 2, 0, True, True)
                body(i * 2 + 1, 1, True, True)
            body(units - 2, 0, True, False)
            body(units - 1, 1, False, False)

        @block.sync
        def _(sp):
            sp.dma_start(cst[:], consts).then_inc(ld_small, 16)
            sp.dma_start(colv[:], cols).then_inc(ld_small, 16)
            sp.dma_start(rowv[:], rows).then_inc(ld_small, 16)
            sp.dma_start(gate[:], gates.partition_broadcast(P)).then_inc(ld_small, 16)
            sp.dma_start(farf[:], far).then_inc(ld_small, 16)
            for i in range(4):
                sp.dma_start(xs[:, 8 * i:8 * i + 8, :], x_v[:, 8 * i:8 * i + 8, :]).then_inc(ld_x[i], 16)
                if i == 0:
                    for s in range(2):
                        sp.dma_start(cT[:, s, 0:2 * P], ctx_t[:, 2 * P * s:2 * P * (s + 1)]).then_inc(ld_cT[s], 16)
            with sp.Fori(0, UA // 2 - 1) as i:
                u = i * 2
                for s in range(2):
                    sp.wait_ge(S("a_qk"), u + (s + 1))
                    sp.dma_start(cT[:, s, 0:2 * P], ctx_t[:, bass.ds((u + (s + 2)) * (2 * P), 2 * P)]).then_inc(ld_cT[s], 16)
            sp.wait_ge(S("a_qk"), UA)
            for s in range(2):
                sp.dma_start(cT[:, s, :], ctx_t[:, 4 * P * s:4 * P * (s + 1)]).then_inc(ld_cC[s], 16)
                sp.dma_start(ctk[:, s], ctx_v[:, 4 * s:4 * s + 4, :]).then_inc(ld_cC[s], 16)
            with sp.Fori(0, U4 // 2 - 1) as i:
                u = i * 2
                for s in range(2):
                    sp.wait_ge(S("c_hq"), u + (s + 1))
                    sp.dma_start(cT[:, s, :], ctx_t[:, bass.ds((u + (s + 2)) * (4 * P), 4 * P)]).then_inc(ld_cC[s], 16)
                    sp.dma_start(ctk[:, s], ctx_v[:, bass.ds((u + (s + 2)) * 4, 4), :]).then_inc(ld_cC[s], 16)
            with sp.Fori(0, U4, 1) as u:
                sp.wait_ge(S("d_x"), 1 + u * 4 + 4)
                sp.dma_start(out_v[:, bass.ds(u * 4, 4), :], xs[:, bass.ds(u * 4, 4), :]).then_inc(S("stored"), 16)
            sp.wait_ge(S("stored"), 16 * U4)

        @block.gpsimd
        def _(pool):
            start_at_one(pool, "gpsimd")
            for c, value in enumerate((EPS, 1.0, -0.5, float(np.e))):
                nc.gpsimd.memset(half[:, c:c + 1], value).then_inc(fill, 1)
            nc.gpsimd.memset(ones[:], 1.0).then_inc(fill, 1)
            nc.gpsimd.memset(wv_eo[:], 0.0).then_inc(fill, 1)
            pool.dma_start(f0g_s[:], f0_wg).then_inc(ld_f0, 16)
            pool.dma_start(f0w1_s[:], f0_w1).then_inc(ld_f0, 16)
            pool.dma_start(f0w2_s[:], f0_w2).then_inc(ld_f0, 16)
            pool.dma_start(f0w3_s[:], f0_w3).then_inc(ld_f0, 16)
            pool.dma_start(wqv_s[:], wqv).then_inc(ld_c, 16)
            pool.dma_start(f1g_s[:], f1_wg).then_inc(ld_f1, 16)
            pool.dma_start(f1w1_s[:], f1_w1).then_inc(ld_f1, 16)
            pool.dma_start(f1w2_s[:], f1_w2).then_inc(ld_f1, 16)
            pool.wait_ge(fill, 6)

            def rstd(k, u, n):
                pool.wait_ge(S(f"mv{k}"), 1 + u * n + n)
                nc.gpsimd.tensor_tensor(ve[:, 0:n], mv[:, 0:n, 1], half[:, 0:1].to_broadcast([P, n]), ALU.add).then_inc(S(f"ve{k}"), 1)
                pool.wait_ge(S(f"ve{k}"), u + 1)
                nc.gpsimd.tensor_copy(ln[:, bass.ds(u * n, n), 0], mv[:, 0:n, 0]).then_inc(S(f"lm{k}"), 1)
                nc.gpsimd.tensor_tensor(ln[:, bass.ds(u * n, n), 1], ve[:, 0:n], half[:, 2:3].to_broadcast([P, n]), ALU.pow).then_inc(S(f"ln{k}"), 1)

            def second_weight(k, u):
                pool.wait_ge(S(f"dif{k}"), u + 1)
                nc.gpsimd.tensor_tensor(pe2[:], half[:, 3:4].to_broadcast([P, 4]), dif[:], ALU.pow).then_inc(S(f"pe{k}"), 1)

            with pool.Fori(0, U4) as u:
                rstd(0, u, 4)
            with pool.Fori(0, UA) as u:
                rstd(1, u, 2)
            with pool.Fori(0, U4) as u:
                second_weight(1, u)
                rstd(2, u, 4)
            with pool.Fori(0, U4) as u:
                rstd(3, u, 4)
            with pool.Fori(0, U4) as u:
                second_weight(3, u)

        @block.scalar
        def _(a):
            start_at_one(a, "scalar")
            for w_s, w in ((wq_s, wq), (wk_s, wk), (wv_s, wv), (wo_s, wo)):
                a.dma_start(w_s[:], w).then_inc(ld_attn, 16)
            a.wait_ge(ld_small, 80)
            nc.scalar.activation(tg[:], gate[:], ACT.Tanh).then_inc(prep_act, 1)
            nc.scalar.activation(bqs[:], colv[:, BQ:BQ + 1], ACT.Copy, scale=float(DH) ** -0.5).then_inc(prep_act, 1)

            def a_xts(u):
                a.wait_ge(S("a_xt"), u + 1)
                nc.scalar.activation(xT[:, 0, 0:2 * P], bank[4][:, 0:2 * P], ACT.Copy).then_inc(S("a_xts"), 1)

            def a_qks(u):
                a.wait_ge(S("a_qk"), u + 1)
                nc.scalar.activation(QT[:], bank[4][:, 0:2 * P], ACT.Identity, bias=bqs[:], scale=float(DH) ** -0.5)
                for j in range(HG):
                    last = nc.scalar.activation(Kb[:, j, :], bank[4][:, 2 * P:4 * P], ACT.Identity,
                                                bias=bkm[:, j:j + 1], scale=cst[:, C_KM + j:C_KM + j + 1])
                last.then_inc(S("a_qks"), 1)

            def a_exp(u, s, g):
                a.wait_ge(S("a_sub"), u * 4 + (g + 1))
                nc.scalar.activation(Pr[:, s, g, :], Pr[:, s, g, :], ACT.Exp).then_inc(S("a_exp"), 1)

            def a_pts(u, g):
                a.wait_ge(S("a_pt"), u * 4 + (g + 1))
                if g == 0:
                    a.wait_ge(S("a_pv"), 1 + u)
                nc.scalar.activation(PT[:, g, :], bank[6 + g % 2][:], ACT.Copy).then_inc(S("a_pts"), 1)

            def a_ats(u):
                a.wait_ge(S("a_at"), u + 1)
                nc.scalar.activation(attT[:], bank[4][:, 0:2 * P], ACT.Copy).then_inc(S("a_ats"), 1)

            a.wait_ge(prep, 3)
            a_xts(0)
            a_qks(0)
            for g in range(NG):
                a_exp(0, 0, g)

            def body_a(u, s, nxt, nxt2):
                a_pts(u, 0)
                a_pts(u, 1)
                if nxt:
                    a_xts(u + 1)
                a_pts(u, 2)
                if nxt:
                    a_qks(u + 1)
                a_pts(u, 3)
                if nxt:
                    a_exp(u + 1, 1 - s, 0)
                    a_exp(u + 1, 1 - s, 1)
                a_ats(u)
                if nxt:
                    a_exp(u + 1, 1 - s, 2)
                    a_exp(u + 1, 1 - s, 3)

            skewed(a, UA, body_a)

            def b_xts(u):
                a.wait_ge(S("b_xt"), u + 1)
                nc.scalar.activation(xT[:, 0, :], bank[6][:], ACT.Copy).then_inc(S("b_xts"), 1)

            def body_b(u, nxt):
                for q in range(2 * E):
                    a.wait_ge(S("b_hg"), u * 16 + (q + 1))
                    a.wait_ge(S("b_act"), 1 + u * 16 + max(q - 3, 0))
                    nc.scalar.activation(sil[:, q % 4, :], bank[q % 2][:], ACT.Silu).then_inc(S("b_sil"), 1)
                if nxt:
                    b_xts(u + 1)

            b_xts(0)
            with a.Fori(0, U4 - 1) as u:
                body_b(u, True)
            body_b(U4 - 1, False)

            def c_xts(u, s):
                a.wait_ge(S("c_xt"), u + 1)
                nc.scalar.activation(xT[:, s, :], bank[0][:], ACT.Copy).then_inc(S("c_xts"), 1)

            def c_exp(u, s):
                a.wait_ge(S("c_nmx"), u + 1)
                for k in range(4):
                    last = nc.scalar.activation(Pc[:, s, k, :], bank[1][:, P * k:P * (k + 1)], ACT.Exp,
                                                bias=nmx[:, k:k + 1], accum_out=sm[:, s, k:k + 1])
                last.then_inc(S("c_exp"), 1)

            def c_bexp(u):
                a.wait_ge(S("c_bsub"), u + 1)
                nc.scalar.activation(brow[:], brow[:], ACT.Exp).then_inc(S("c_bexp"), 1)

            def c_pts(u):
                a.wait_ge(S("c_pt"), u + 1)
                nc.scalar.activation(PcT[:], bank[3][:], ACT.Copy).then_inc(S("c_pts"), 1)

            def c_hqs(u):
                a.wait_ge(S("c_hq"), u + 1)
                nc.scalar.activation(hqT[:], bank[4][:], ACT.Copy).then_inc(S("c_hqs"), 1)

            def body_c(u, s, nxt, nxt2):
                if nxt:
                    c_xts(u + 1, 1 - s)
                c_pts(u)
                c_hqs(u)
                if nxt:
                    c_exp(u + 1, 1 - s)
                    c_bexp(u + 1)

            c_xts(0, 0)
            c_exp(0, 0)
            c_bexp(0)
            skewed(a, U4, body_c)

            def d_xts(u, s):
                a.wait_ge(S("d_xt"), u + 1)
                nc.scalar.activation(xT[:, s, :], bank[0][:], ACT.Copy).then_inc(S("d_xts"), 1)

            def d_gelu(u, k):
                a.wait_ge(S("d_h"), u * 4 + (k + 1))
                a.wait_ge(S("d_hgg"), 1 + u * 4 + max(k - 1, 0))
                nc.scalar.activation(hg[:, k % 2, :], bank[1 + k % 2][:], ACT.Gelu).then_inc(S("d_gelu"), 1)

            def d_hts(u, k):
                a.wait_ge(S("d_ht"), 1 + u * 4 + (k + 1))
                a.wait_ge(S("d_y"), 1 + u * 4 + max(k - 1, 0))
                nc.scalar.activation(hT[:, k % 2, :], bank[3 + k % 2][:], ACT.Copy).then_inc(S("d_hts"), 1)

            def body_d(u, s, nxt, nxt2):
                d_gelu(u, 0)
                d_gelu(u, 1)
                d_hts(u, 0)
                if nxt:
                    d_xts(u + 1, 1 - s)
                d_gelu(u, 2)
                d_hts(u, 1)
                d_gelu(u, 3)
                d_hts(u, 2)
                d_hts(u, 3)

            d_xts(0, 0)
            skewed(a, U4, body_d)

        @block.vector
        def _(v):
            start_at_one(v, "vector")
            v.wait_ge(ld_small, 80)
            v.wait_ge(prep_act, 2)
            nc.vector.tensor_scalar(bkm[:], cst[:, C_KM:C_KM + HG], colv[:, BK:BK + 1], None, ALU.mult).then_inc(prep, 1)
            nc.vector.tensor_scalar(row1[:], rowv[:, R_BQV:R_BQV + D], tg[0:1, 1:2], None, ALU.mult).then_inc(prep, 1)
            for s in range(2):
                last = nc.vector.tensor_copy(Vb[:, s, :, :, 16:18],
                                             cst[:, C_VM:C_VM + 2].unsqueeze(1).unsqueeze(1).to_broadcast([P, 4, NH // 2, 2]))
            last.then_inc(prep, 1)
            nc.vector.tensor_copy(farb[:], farf[:]).then_inc(prep, 1)
            v.wait_ge(ld_attn, 64)
            v.wait_ge(fill, 6)
            nc.vector.tensor_scalar(wo_s[:], wo_s[:], tg[:, 0:1], None, ALU.mult).then_inc(prep, 1)
            nc.vector.tensor_scalar(rowv[:, R_BO:R_BO + D], rowv[:, R_BO:R_BO + D], tg[0:1, 0:1], None, ALU.mult).then_inc(prep, 1)
            for e in range(2):
                last = nc.vector.tensor_copy(wv_eo[:, e, :].rearrange("p (h e d) -> p h e d", e=2, d=DH)[:, :, e, :],
                                             wv_s[:].rearrange("p (h e d) -> p h e d", e=2, d=DH)[:, :, e, :])
            last.then_inc(prep, 1)
            v.wait_ge(ld_c, 16)
            nc.vector.tensor_scalar(wqv_g[:], wqv_s[:], tg[:, 1:2], None, ALU.mult).then_inc(prep, 1)
            v.wait_ge(prep_pe, 1)
            nc.vector.tensor_copy(row0[:], bank[7][0:1, 0:D]).then_inc(prep_b0, 1)

            def stats(k, u, n):
                wait_alone(v, S(f"mv{k}"), 1 + u * n)
                if k:
                    wait_alone(v, S(WRITTEN[k]), 1 + (u + 1) * WRITES[k])
                for c in range(n):
                    nc.vector.bn_stats(stat[:, c, :], xs[:, u * n + c, :]).then_inc(S(f"bn{k}"), 1)
                wait_alone(v, S(f"ln{k}"), 1 + u)
                wait_alone(v, S(f"bn{k}"), u * n + n)
                for c in range(n):
                    nc.vector.bn_aggr(mv[:, c, :], stat[:, c, :]).then_inc(S(f"mv{k}"), 1)

            def norm(u, s, n, done):
                for c in range(n):
                    last = nc.vector.tensor_scalar(xn[:, s, c, :], xs[:, u * n + c, :], ln[:, u * n + c, 0:1],
                                                   ln[:, u * n + c, 1:2], ALU.subtract, ALU.mult)
                last.then_inc(S(done), 1)

            for i in range(4):
                v.wait_ge(ld_x[i], 16)
                for u in range(2 * i, 2 * i + 2):
                    stats(0, u, 4)

            v.wait_ge(S("ln0"), 1 + U4)

            def a_vs(u, s):
                v.wait_ge(S("a_v"), u + 1)
                nc.vector.tensor_copy(Vb[:, s, :, :, 0:16],
                                      bank[5][:].rearrange("p (b h d) -> p b h d", b=4, d=16)).then_inc(S("a_vs"), 1)

            def a_sub(u, s, g):
                v.wait_ge(S("a_s"), u * 4 + (g + 1))
                sc = bank[g][:].rearrange("p (m k) -> p m k", k=L)
                nc.vector.tensor_reduce(mx[:, g, :], sc, AX, ALU.max).then_inc(S("a_max"), 1)
                v.wait_ge(S("a_max"), u * 4 + (g + 1))
                nc.vector.tensor_tensor(Pr[:, s, g, :].rearrange("p (m k) -> p m k", k=L), sc,
                                        mx[:, g, :].unsqueeze(2).to_broadcast([P, 8, L]), ALU.subtract).then_inc(S("a_sub"), 1)

            def a_nrm(u):
                v.wait_ge(S("a_pv"), 1 + u + 1)
                o = bank[5][:, 0:NH * 18].rearrange("p (m c) -> p m c", c=18)
                nc.vector.reciprocal(rec[:], o[:, :, 16:18]).then_inc(S("a_rec"), 1)
                v.wait_ge(S("a_rec"), u + 1)
                nc.vector.tensor_tensor(att[:].rearrange("p (m e d) -> p m e d", e=2, d=DH),
                                        o[:, :, 0:16].rearrange("p m (e d) -> p m e d", e=2),
                                        rec[:].unsqueeze(3).to_broadcast([P, NH, 2, DH]), ALU.mult).then_inc(S("a_nrm"), 1)

            def a_x(u):
                v.wait_ge(S("a_y"), u + 1)
                xu = xs[:, bass.ds(u * 2, 2), :] if not isinstance(u, int) else xs[:, 2 * u:2 * u + 2, :]
                nc.vector.tensor_tensor(xu, bank[4][:, 2 * P:4 * P].rearrange("p (c d) -> p c d", d=D), xu, ALU.add).then_inc(S("a_x"), 1)
                stats(1, u, 2)

            norm(0, 0, 2, "a_ln")
            norm(1, 1, 2, "a_ln")
            a_vs(0, 0)
            for g in range(NG):
                a_sub(0, 0, g)

            def body_a(u, s, nxt, nxt2):
                if nxt:
                    a_vs(u + 1, 1 - s)
                if nxt2:
                    norm(u + 2, s, 2, "a_ln")
                if nxt:
                    a_sub(u + 1, 1 - s, 0)
                    a_sub(u + 1, 1 - s, 1)
                a_nrm(u)
                if nxt:
                    a_sub(u + 1, 1 - s, 2)
                    a_sub(u + 1, 1 - s, 3)
                a_x(u)

            skewed(v, UA, body_a)

            def choose(k, u, scores):
                v.wait_ge(S(f"lgp{k}"), u + 1)
                nc.vector.tensor_copy(lg[:], scores).then_inc(S(f"lgs{k}"), 1)
                wait_alone(v, S(f"lgs{k}"), u + 1)
                for c in range(4):
                    nc.vector.max(top[:, c, :], lg[:, c, :]).then_inc(S(f"top{k}"), 1)
                v.wait_ge(S(f"top{k}"), u * 4 + 4)
                nc.vector.tensor_tensor(dif[:], top[:, :, 1], top[:, :, 0], ALU.subtract).then_inc(S(f"dif{k}"), 1)
                for c in range(4):
                    nc.vector.max_index(idx[:, c, :], top[:, c, :], lg[:, c, :]).then_inc(S(f"idx{k}"), 1)
                v.wait_ge(S(f"idx{k}"), u * 4 + 4)
                nc.vector.tensor_copy(idf[:], idx[:]).then_inc(S(f"idf{k}"), 1)
                v.wait_ge(S(f"idf{k}"), u + 1)
                for o, h in ((oh1, 0), (oh2, 1)):
                    nc.vector.tensor_tensor(o[:], iota.unsqueeze(1).to_broadcast([P, 4, E]),
                                            idf[:, :, h:h + 1].to_broadcast([P, 4, E]), ALU.is_equal).then_inc(S(f"oh{k}"), 1)

            def weigh(k, u, g, factor):
                v.wait_ge(S(f"pe{k}"), u + 1)
                nc.vector.tensor_scalar(den[:], pe2[:], 1.0, None, ALU.add).then_inc(S(f"den{k}"), 1)
                v.wait_ge(S(f"den{k}"), u * 2 + 1)
                nc.vector.reciprocal(den[:], den[:]).then_inc(S(f"den{k}"), 1)
                v.wait_ge(S(f"den{k}"), u * 2 + 2)
                nc.vector.tensor_scalar(w1g[:], den[:], tg[:, g:g + 1], factor, ALU.mult, ALU.mult).then_inc(S(f"w{k}"), 1)
                v.wait_ge(S(f"w{k}"), u * 2 + 1)
                nc.vector.tensor_tensor(w2g[:], w1g[:], pe2[:], ALU.mult).then_inc(S(f"w{k}"), 1)
                v.wait_ge(S(f"oh{k}"), u * 4 + 2)
                nc.vector.tensor_tensor(oh1[:], oh1[:], w1g[:].unsqueeze(2).to_broadcast([P, 4, E]), ALU.mult).then_inc(S(f"oh{k}"), 1)
                v.wait_ge(S(f"w{k}"), u * 2 + 2)
                nc.vector.tensor_tensor(oh2[:], oh2[:], w2g[:].unsqueeze(2).to_broadcast([P, 4, E]), ALU.mult).then_inc(S(f"oh{k}"), 1)
                v.wait_ge(S(f"oh{k}"), u * 4 + 4)
                nc.vector.tensor_tensor(cmb[:], oh1[:], oh2[:], ALU.add).then_inc(S(f"cmb{k}"), 1)

            v.wait_ge(S("ln1"), 1 + UA)
            norm(0, 0, 4, "b_ln")

            def b_act(u, q):
                v.wait_ge(S("b_sil"), u * 16 + (q + 1))
                v.wait_ge(S("b_y"), 1 + u * 8 + max(q // 2 - 1, 0))
                nc.vector.tensor_tensor(act[:, q % 4, :], sil[:, q % 4, :], bank[2 + q % 2][:], ALU.mult).then_inc(S("b_act"), 1)

            def b_acc(u, e):
                v.wait_ge(S("b_y"), 1 + u * 8 + (e + 1))
                v.wait_ge(S("b_acc"), 1 + u * 8 + e)
                if e == 0:
                    v.wait_ge(S("cmb1"), u + 1)
                for c in range(4):
                    last = nc.vector.scalar_tensor_tensor(
                        xs[:, u * 4 + c, :], bank[4 + e % 2][:, P * c:P * (c + 1)], cmb[:, c, e:e + 1],
                        xs[:, u * 4 + c, :], ALU.mult, ALU.add)
                last.then_inc(S("b_acc"), 1)

            def body_b(u, nxt):
                b_act(u, 0)
                choose(1, u, bank[7][:, 0:4 * E].rearrange("p (c e) -> p c e", e=E))
                b_act(u, 1)
                weigh(1, u, 2, 1.0)
                b_act(u, 2)
                for e in range(E):
                    if e < E - 1:
                        b_act(u, 2 * e + 3)
                    b_acc(u, e)
                    if e < E - 2:
                        b_act(u, 2 * e + 4)
                    if e == 3 and nxt:
                        norm(u + 1, 0, 4, "b_ln")
                stats(2, u, 4)

            with v.Fori(0, U4 - 1) as u:
                body_b(u, True)
            body_b(U4 - 1, False)

            v.wait_ge(S("ln2"), 1 + U4)

            def c_e3(u, s):
                v.wait_ge(S("c_xts"), u + 1)
                nc.vector.tensor_scalar(e3[:], xT[:, s, :], colv[:, W3S:W3S + 1], colv[:, W2S:W2S + 1],
                                        ALU.mult, ALU.add).then_inc(S("c_e3"), 1)

            def c_max(u):
                v.wait_ge(S("c_s"), u + 1)
                nc.vector.tensor_reduce(rmx[:], bank[1][:].rearrange("p (c k) -> p c k", k=P), AX, ALU.max).then_inc(S("c_rmx"), 1)
                v.wait_ge(S("c_rmx"), u + 1)
                nc.vector.tensor_scalar(nmx[:], rmx[:], -1.0, None, ALU.mult).then_inc(S("c_nmx"), 1)
                nc.vector.tensor_tensor(mcol[:], bank[2][:, 0:4], rmx[:], ALU.add).then_inc(S("c_mcol"), 1)

            def c_bsub(u):
                v.wait_ge(S("c_mt"), u + 1)
                m = bank[2][0:4, P:2 * P].rearrange("p (b l) -> p b l", l=L)
                nc.vector.tensor_reduce(bm[:], m, AX, ALU.max).then_inc(S("c_bm"), 1)
                v.wait_ge(S("c_bm"), u + 1)
                nc.vector.tensor_tensor(brow[:], m, bm[:].unsqueeze(2).to_broadcast([4, 2, L]), ALU.subtract).then_inc(S("c_bsub"), 1)

            def c_brow(u):
                v.wait_ge(S("c_bexp"), u + 1)
                nc.vector.tensor_reduce(bs[:], brow[:], AX, ALU.add).then_inc(S("c_bs"), 1)
                v.wait_ge(S("c_bs"), u * 2 + 1)
                nc.vector.reciprocal(br[:], bs[:]).then_inc(S("c_bs"), 1)
                v.wait_ge(S("c_bs"), u * 2 + 2)
                nc.vector.tensor_tensor(wrow[:].rearrange("p (b l) -> p b l", l=L), brow[:],
                                        br[:].unsqueeze(2).to_broadcast([4, 2, L]), ALU.mult).then_inc(S("c_wrow"), 1)

            def c_wbd(u):
                v.wait_ge(S("c_wt"), u + 1)
                nc.vector.tensor_tensor(wbd[:], bank[2][:, 4:8].unsqueeze(2).to_broadcast([P, 4, 2]),
                                        cst[:, C_BI:C_BI + 2].unsqueeze(1).to_broadcast([P, 4, 2]), ALU.mult).then_inc(S("c_wbd"), 1)

            def c_ehc(u, s):
                v.wait_ge(S("c_hc"), u + 1)
                nc.vector.tensor_copy(hc[:], bank[2][:, 8:16]).then_inc(S("c_hcs"), 1)
                v.wait_ge(S("c_hcs"), u + 1)
                nc.vector.tensor_tensor(ehc[:, s, :].rearrange("p (b l) -> p b l", l=L),
                                        xT[:, s, :].rearrange("p (b l) -> p b l", l=L),
                                        hc[:].unsqueeze(2).to_broadcast([P, 8, L]), ALU.mult).then_inc(S("c_ehc"), 1)

            def c_nrm(u, s):
                v.wait_ge(S("c_exp"), u + 1)
                nc.vector.reciprocal(rsm[:], sm[:, s, :]).then_inc(S("c_rsm"), 1)
                v.wait_ge(S("c_rsm"), u + 1)
                nc.vector.tensor_tensor(Pc[:, s], Pc[:, s], rsm[:].unsqueeze(2).to_broadcast([P, 4, P]), ALU.mult).then_inc(S("c_nrm"), 1)

            def c_ehq(u, s):
                v.wait_ge(S("c_hqs"), u + 1)
                nc.vector.tensor_tensor(ehq[:], hqT[:], xT[:, s, :], ALU.mult).then_inc(S("c_ehq"), 1)

            def c_x(u):
                v.wait_ge(S("c_y"), u + 1)
                xu = xs[:, bass.ds(u * 4, 4), :] if not isinstance(u, int) else xs[:, 4 * u:4 * u + 4, :]
                nc.vector.tensor_tensor(xu, bank[5][:].rearrange("p (c d) -> p c d", d=D), xu, ALU.add).then_inc(S("c_x"), 1)
                stats(3, u, 4)

            norm(0, 0, 4, "c_ln")
            norm(1, 1, 4, "c_ln")
            c_e3(0, 0)
            c_max(0)
            c_bsub(0)
            c_brow(0)
            c_nrm(0, 0)
            c_wbd(0)
            c_ehc(0, 0)

            def body_c(u, s, nxt, nxt2):
                if nxt:
                    c_e3(u + 1, 1 - s)
                c_ehq(u, s)
                if nxt:
                    c_max(u + 1)
                    c_bsub(u + 1)
                    c_brow(u + 1)
                    c_nrm(u + 1, 1 - s)
                    c_wbd(u + 1)
                    c_ehc(u + 1, 1 - s)
                if nxt2:
                    norm(u + 2, s, 4, "c_ln")
                c_x(u)

            skewed(v, U4, body_c)

            v.wait_ge(S("ln3"), 1 + U4)

            def d_gate(u, k):
                v.wait_ge(S("d_gelu"), 1 + u * 4 + (k + 1))
                if k == 0:
                    v.wait_ge(S("cmb3"), u + 1)
                v.wait_ge(S("d_ht"), 1 + u * 4 + max(k - 1, 0))
                nc.vector.tensor_tensor(hgg[:, k % 2, :].rearrange("p (e r) -> p e r", r=R),
                                        hg[:, k % 2, :].rearrange("p (e r) -> p e r", r=R),
                                        cmb[:, k, :].unsqueeze(2).to_broadcast([P, E, R]), ALU.mult).then_inc(S("d_hgg"), 1)

            def d_acc(u, k):
                v.wait_ge(S("d_y"), 1 + u * 4 + (k + 1))
                xk = xs[:, u * 4 + k, :]
                nc.vector.tensor_tensor(xk, bank[5 + k % 2][:, 0:D], xk, ALU.add).then_inc(S("d_x"), 1)

            def d_choose(u):
                choose(3, u, bank[7][:, 0:4 * E].rearrange("p (c e) -> p c e", e=E))

            norm(0, 0, 4, "d_ln")
            norm(1, 1, 4, "d_ln")
            d_choose(0)

            def body_d(u, s, nxt, nxt2):
                weigh(3, u, 3, SCALING)
                d_gate(u, 0)
                d_gate(u, 1)
                d_acc(u, 0)
                if nxt2:
                    norm(u + 2, s, 4, "d_ln")
                d_gate(u, 2)
                d_acc(u, 1)
                d_gate(u, 3)
                if nxt:
                    d_choose(u + 1)
                d_acc(u, 2)
                d_acc(u, 3)

            skewed(v, U4, body_d)

        @block.tensor
        def _(pe):
            start_at_one(pe, "tensor")
            mm = nc.tensor.matmul

            pe.wait_ge(prep, 7)
            mm(bank[7][0:1, 0:D], colv[:, BV:BV + 1], wo_s[:], start=True, stop=False)
            mm(bank[7][0:1, 0:D], ones[0:1, 0:1], rowv[0:1, R_BO:R_BO + D], start=False, stop=True).then_inc(prep_pe, 1)

            def transposes(done, dst, src, n):
                for c in range(n):
                    last = nc.tensor.transpose(dst[:, P * c:P * (c + 1)], src(c), ident)
                last.then_inc(S(done), 1)

            def a_xt(u, s):
                pe.wait_ge(S("a_ln"), u + 1)
                transposes("a_xt", bank[4], lambda c: xn[:, s, c, :], 2)

            def a_v(u, s, arrived):
                pe.wait_ge(ld_cT[s], arrived)
                for b in range(4):
                    for e in range(2):
                        last = mm(bank[5][L * e:L * (e + 1), P * b:P * (b + 1)], cT[:, s, L * b:L * (b + 1)],
                                  wv_eo[:, e, :], start=True, stop=True)
                last.then_inc(S("a_v"), 1)

            def a_qk(u, s):
                pe.wait_ge(S("a_xts"), u + 1)
                mm(bank[4][:, 0:2 * P], wq_s[:], xT[:, 0, 0:2 * P], start=True, stop=True)
                mm(bank[4][:, 2 * P:4 * P], wk_s[:], cT[:, s, 0:2 * P], start=True, stop=True).then_inc(S("a_qk"), 1)

            def a_s(u, g):
                for p in range(2):
                    for b in range(2):
                        t = P * p + L * b
                        last = mm(bank[g][L * b:L * (b + 1), 256 * p:256 * (p + 1)], QT[32 * g:32 * (g + 1), t:t + L],
                                  Kb[32 * g:32 * (g + 1), :, t:t + L], start=True, stop=True)
                last.then_inc(S("a_s"), 1)

            def a_s2(u, g):
                pe.wait_ge(S("a_sub"), u * 4 + (g - 3))
                a_s(u, g)

            def a_pt(u, s, g):
                pe.wait_ge(S("a_exp"), u * 4 + (g + 1))
                pe.wait_ge(S("a_pts"), 1 + u * 4 + max(g - 1, 0))
                transposes("a_pt", bank[6 + g % 2], lambda c: Pr[:, s, g, P * c:P * (c + 1)], 4)

            def a_pv(u, s, g):
                pe.wait_ge(S("a_pts"), 1 + u * 4 + (g + 1))
                for p in range(2):
                    for h in range(2):
                        for b in range(2):
                            m = (p * 8 + 2 * g + h) * 18
                            c = P * (2 * p + h) + L * b
                            last = mm(bank[5][L * b:L * (b + 1), m:m + 18], PT[:, g, c:c + L],
                                      Vb[:, s, 2 * p + b, 2 * g + h, :], start=True, stop=True)
                if g == NG - 1:
                    last.then_inc(S("a_pv"), 1)

            def a_at(u):
                pe.wait_ge(S("a_nrm"), 1 + u + 1)
                transposes("a_at", bank[4], lambda c: att[:, D * c:D * (c + 1)], 2)

            def a_y(u):
                pe.wait_ge(S("a_ats"), u + 1)
                for c in range(2):
                    o = bank[4][:, P * (2 + c):P * (3 + c)]
                    mm(o, attT[:, P * c:P * (c + 1)], wo_s[:], start=True, stop=False)
                    last = mm(o, ones[:], row0[:], start=False, stop=True)
                last.then_inc(S("a_y"), 1)

            a_xt(0, 0)
            a_v(0, 0, 16)
            a_qk(0, 0)
            pe.wait_ge(S("a_qks"), 1)
            for g in range(NG):
                a_s(0, g)
            pe.wait_ge(prep_b0, 1)

            def body_a(u, s, nxt, nxt2):
                a_pt(u, s, 0)
                a_pt(u, s, 1)
                if nxt:
                    pe.wait_ge(S("a_x"), 1 + u)
                    pe.wait_ge(S("a_qks"), u + 1)
                    a_xt(u + 1, 1 - s)
                    pe.wait_ge(S("a_nrm"), 1 + u)
                    pe.wait_ge(S("a_vs"), u + 1)
                    a_v(u + 1, 1 - s, (u - s) * 8 + (16 if s == 0 else 32))
                a_pt(u, s, 2)
                if nxt:
                    a_qk(u + 1, 1 - s)
                a_pt(u, s, 3)
                if nxt:
                    pe.wait_ge(S("a_vs"), u + 2)
                a_pv(u, s, 0)
                a_pv(u, s, 1)
                if nxt:
                    pe.wait_ge(S("a_qks"), u + 2)
                    a_s2(u + 1, 0)
                a_pv(u, s, 2)
                if nxt:
                    a_s2(u + 1, 1)
                a_pv(u, s, 3)
                if nxt:
                    a_s2(u + 1, 2)
                a_at(u)
                if nxt:
                    a_s2(u + 1, 3)
                a_y(u)

            skewed(pe, UA, body_a)

            pe.wait_ge(S("a_x"), 1 + UA)
            pe.wait_ge(S("a_pts"), 1 + NG * UA)
            pe.wait_ge(ld_f0, 64)

            def b_xt(u):
                pe.wait_ge(S("b_ln"), u + 1)
                transposes("b_xt", bank[6], lambda c: xn[:, 0, c, :], 4)

            def b_hg(u, q):
                e, t = divmod(q, 2)
                pe.wait_ge(S("b_act"), 1 + u * 16 + max(q - 1, 0))
                mm(bank[q % 2][:], f0w1_s[:, e, P * t:P * (t + 1)], xT[:, 0, :], start=True, stop=True)
                mm(bank[2 + q % 2][:], f0w2_s[:, e, P * t:P * (t + 1)], xT[:, 0, :], start=True, stop=True).then_inc(S("b_hg"), 1)

            def b_y(u, e):
                pe.wait_ge(S("b_act"), 1 + u * 16 + (2 * e + 2))
                pe.wait_ge(S("b_acc"), 1 + u * 8 + max(e - 1, 0))
                for c in range(4):
                    for t in range(2):
                        last = mm(bank[4 + e % 2][:, P * c:P * (c + 1)], act[:, (2 * e + t) % 4, P * c:P * (c + 1)],
                                  f0w3_s[:, e, t, :], start=t == 0, stop=t == 1)
                last.then_inc(S("b_y"), 1)

            def body_b(u, nxt):
                pe.wait_ge(S("b_xts"), u + 1)
                b_hg(u, 0)
                for c in range(4):
                    last = mm(bank[7][:, E * c:E * (c + 1)], xT[:, 0, P * c:P * (c + 1)], f0g_s[:], start=True, stop=True)
                last.then_inc(S("lgp1"), 1)
                b_hg(u, 1)
                b_hg(u, 2)
                for e in range(E):
                    for q in (2 * e + 3, 2 * e + 4):
                        if q < 2 * E:
                            b_hg(u, q)
                        if e == E - 2 and q == 2 * e + 4 and nxt:
                            b_xt(u + 1)
                    b_y(u, e)

            b_xt(0)
            with pe.Fori(0, U4 - 1) as u:
                body_b(u, True)
            body_b(U4 - 1, False)

            pe.wait_ge(S("b_acc"), 1 + E * U4)
            pe.wait_ge(prep, 8)

            def c_xt(u, s):
                pe.wait_ge(S("c_ln"), u + 1)
                transposes("c_xt", bank[0], lambda c: xn[:, s, c, :], 4)

            def c_s(u, s, arrived):
                pe.wait_ge(ld_cC[s], arrived)
                pe.wait_ge(S("c_e3"), u + 1)
                mm(bank[1][:], farb[:, 0:P], farb[:, P:5 * P], start=True, stop=False, skip_group_check=True)
                for c in range(4):
                    mm(bank[1][:, P * c:P * (c + 1)], e3[:, P * c:P * (c + 1)], cT[:, s, P * c:P * (c + 1)],
                       start=False, stop=True, skip_group_check=True)
                for c in range(4):
                    last = mm(bank[2][:, c:c + 1], xT[:, s, P * c:P * (c + 1)], colv[:, W1S:W1S + 1], start=True, stop=False)
                    last = mm(bank[2][:, c:c + 1], ones[:], rowv[0:1, R_BS:R_BS + 1], start=False, stop=True)
                last.then_inc(S("c_s"), 1)

            def c_mt(u):
                pe.wait_ge(S("c_mcol"), u + 1)
                nc.tensor.transpose(bank[2][0:4, P:2 * P], mcol[:], ident).then_inc(S("c_mt"), 1)

            def c_wt(u):
                wait_alone(pe, S("c_wrow"), u + 1)
                nc.tensor.transpose(bank[2][:, 4:8], wrow[:], cst[0:4, C_ID:C_ID + 4]).then_inc(S("c_wt"), 1)

            def c_hc(u, s):
                pe.wait_ge(S("c_wbd"), u + 1)
                for c in range(4):
                    last = mm(bank[2][:, 8 + 2 * c:10 + 2 * c], xn[:, s, c, :], wbd[:, c, :], start=True, stop=True)
                last.then_inc(S("c_hc"), 1)

            def c_pt(u, s):
                pe.wait_ge(S("c_nrm"), u + 1)
                transposes("c_pt", bank[3], lambda c: Pc[:, s, c, :], 4)

            def c_hq(u, s):
                pe.wait_ge(S("c_pts"), u + 1)
                for c in range(4):
                    last = mm(bank[4][:, P * c:P * (c + 1)], ctk[:, s, c, :], PcT[:, P * c:P * (c + 1)], start=True, stop=True)
                last.then_inc(S("c_hq"), 1)

            def c_y(u, s, c):
                if c == 0:
                    pe.wait_ge(S("c_ehq"), u + 1)
                    pe.wait_ge(S("c_ehc"), u + 1)
                    pe.wait_ge(S("c_x"), 1 + u)
                o = bank[5][:, P * c:P * (c + 1)]
                tok = slice(P * c, P * (c + 1))
                for i, f in enumerate((xT[:, s, tok], hqT[:, tok], ehq[:, tok], ehc[:, s, tok])):
                    mm(o, f, wqv_g[:, i, :], start=i == 0, stop=False)
                last = mm(o, ones[:], row1[:], start=False, stop=True)
                if c == 3:
                    last.then_inc(S("c_y"), 1)

            c_xt(0, 0)
            c_s(0, 0, 32)
            c_mt(0)
            c_wt(0)
            c_hc(0, 0)

            def body_c(u, s, nxt, nxt2):
                if nxt:
                    c_xt(u + 1, 1 - s)
                c_pt(u, s)
                c_hq(u, s)
                if nxt:
                    c_s(u + 1, 1 - s, (u - s) * 16 + (32 if s == 0 else 64))
                c_y(u, s, 0)
                if nxt:
                    c_mt(u + 1)
                c_y(u, s, 1)
                if nxt:
                    c_wt(u + 1)
                c_y(u, s, 2)
                c_y(u, s, 3)
                if nxt:
                    c_hc(u + 1, 1 - s)

            skewed(pe, U4, body_c)

            pe.wait_ge(S("c_x"), 1 + U4)
            pe.wait_ge(ld_f1, 48)

            def d_xt(u, s):
                pe.wait_ge(S("d_ln"), u + 1)
                transposes("d_xt", bank[0], lambda c: xn[:, s, c, :], 4)

            def d_lg(u, s):
                pe.wait_ge(S("d_xts"), u + 1)
                for c in range(4):
                    o = bank[7][:, E * c:E * (c + 1)]
                    mm(o, xT[:, s, P * c:P * (c + 1)], f1g_s[:], start=True, stop=False)
                    last = mm(o, ones[:], rowv[0:1, R_BG:R_BG + E], start=False, stop=True)
                last.then_inc(S("lgp3"), 1)

            def d_h(u, s, k):
                pe.wait_ge(S("d_gelu"), 1 + u * 4 + max(k - 1, 0))
                mm(bank[1 + k % 2][:], xT[:, s, P * k:P * (k + 1)], f1w1_s[:], start=True, stop=True).then_inc(S("d_h"), 1)

            def d_ht(u, k):
                pe.wait_ge(S("d_hgg"), 1 + u * 4 + (k + 1))
                pe.wait_ge(S("d_hts"), 1 + u * 4 + max(k - 1, 0))
                transposes("d_ht", bank[3 + k % 2], lambda c: hgg[:, k % 2, P * c:P * (c + 1)], 4)

            def d_y(u, k):
                pe.wait_ge(S("d_hts"), 1 + u * 4 + (k + 1))
                pe.wait_ge(S("d_x"), 1 + u * 4 + max(k - 1, 0))
                for c in range(4):
                    last = mm(bank[5 + k % 2][:, 0:D], hT[:, k % 2, P * c:P * (c + 1)], f1w2_s[:, c, :],
                              start=c == 0, stop=c == 3)
                last.then_inc(S("d_y"), 1)

            d_xt(0, 0)
            d_lg(0, 0)

            def body_d(u, s, nxt, nxt2):
                d_h(u, s, 0)
                d_h(u, s, 1)
                d_ht(u, 0)
                if nxt:
                    d_xt(u + 1, 1 - s)
                d_h(u, s, 2)
                d_ht(u, 1)
                d_y(u, 0)
                d_h(u, s, 3)
                d_ht(u, 2)
                d_y(u, 1)
                if nxt:
                    d_lg(u + 1, 1 - s)
                d_ht(u, 3)
                d_y(u, 2)
                d_y(u, 3)

            skewed(pe, U4, body_d)


def kernel(**inputs):
    import concourse.bacc as bacc
    from concourse.bass_utils import run_bass_kernel_spmd

    a = {k: np.asarray(v) for k, v in inputs.items()}
    consts, far = constants()
    lay = np.ascontiguousarray
    sim = a["L1_xattn_w_sim"].reshape(3, D)
    arrays = {
        "x": a["x"].reshape(TOKENS, D),
        "ctx_tok": a["ctx_1024"].reshape(TOKENS, D),
        "ctx_t": lay(a["ctx_1024"].reshape(TOKENS, D).T),
        "wq": lay(a["L0_xattn_wq_w"].T),
        "wk": lay(a["L0_xattn_wk_w"].T),
        "wv": lay(a["L0_xattn_wv_w"].T),
        "wo": lay(a["L0_xattn_wo_w"].T),
        "cols": lay(np.stack([a["L0_xattn_wq_b"], a["L0_xattn_wk_b"], a["L0_xattn_wv_b"], sim[0], sim[1], sim[2]], 1)),
        "rows": lay(np.concatenate([a["L0_xattn_wo_b"], a["L1_xattn_b_qv"], a["L1_ffn_bg"], a["L1_xattn_b_sim"]])[None]),
        "gates": lay(np.concatenate([a["g_xattn"], a["g_ffn"]])),
        "consts": consts,
        "far": far,
        "f0_wg": a["L0_ffn_Wg"],
        "f0_w1": lay(a["L0_ffn_W1"].transpose(1, 0, 2)),
        "f0_w2": lay(a["L0_ffn_W2"].transpose(1, 0, 2)),
        "f0_w3": lay(a["L0_ffn_W3"].reshape(E, 2, P, D).transpose(2, 0, 1, 3)),
        "wqv": lay(a["L1_xattn_W_qv"].reshape(4, D, D).transpose(1, 0, 2)),
        "f1_wg": lay(a["L1_ffn_Wg"].T),
        "f1_w1": lay(a["L1_ffn_W1"].reshape(E * R, D).T),
        "f1_w2": lay(a["L1_ffn_W2"].transpose(0, 2, 1).reshape(4, P, D).transpose(1, 0, 2)),
    }
    nc = bacc.Bacc("TRN2", target_bir_lowering=False, num_devices=1)
    args = {n: nc.dram_tensor(n + "_dram", v.shape, mybir.dt.from_np(v.dtype), kind="ExternalInput").ap()
            for n, v in arrays.items()}
    args["out"] = nc.dram_tensor("out_dram", (TOKENS, D), F32, kind="ExternalOutput").ap()
    flamingo(nc, **args)
    r = run_bass_kernel_spmd(nc, [{n + "_dram": v for n, v in arrays.items()}], core_ids=[0])
    return r.results[0]["out_dram"].reshape(a["x"].shape)
```

```python
from contextlib import ExitStack

import numpy as np

import concourse.bass as bass
from concourse import mybir

F32 = mybir.dt.float32
BF16 = mybir.dt.bfloat16
U32 = mybir.dt.uint32
ACT = mybir.ActivationFunctionType
ALU = mybir.AluOpType
AX = mybir.AxisListType.X

P = 128
D = 128
L = 64
NH = 16
DH = D // NH
NG = 4
HG = NH // NG
E = 8
HID = 256
R = 64
SCALING = 2.0
TOKENS = 64 * L
EPS = 1e-5
REGION = TOKENS + P
PACK = 6
RK = 2 * P + 2 * E
NB = 2 * TOKENS // P + E
WRITTEN = {1: "a_x", 2: "c_sum", 3: "c_x"}
WRITES = {1: 1, 2: 2, 3: 1}
FAR = -1e30
CH = TOKENS // P
UA = CH // 2
U4 = CH // 4
stats_units = {0: 0, 1: U4, 2: U4 + UA, 3: 0}
gated = {1: 0, 3: UA}

BQ, BK, BV, W1S, W2S, W3S = range(6)
C_ID, C_KM, C_VM, C_IO, C_BI, C_UP, C_RG, C_TR, C_J = 0, 128, 132, 134, 142, 144, 272, 280, 344
C_N = C_J + NB
R_BO, R_BQV, R_BG = 0, 128, 256
R_N = 264


def constants():
    c = np.zeros((P, C_N), np.float32)
    p = np.arange(P)
    c[:, C_ID:C_ID + P] = np.eye(P)
    c[p, C_KM + (p % 32) // DH] = 1
    c[p, C_VM + p // L] = 1
    c[:, C_IO:C_IO + E] = np.arange(E)
    c[p, C_BI + p // L] = 1
    c[:, C_UP:C_UP + P] = p[:, None] < p[None, :]
    c[:, C_RG:C_RG + E] = np.arange(E) * REGION
    c[:, C_TR:C_TR + E * E] = (np.arange(E)[:, None] >= np.arange(E)[None, :]).reshape(-1)
    c[:, C_J:C_J + NB] = np.arange(NB)
    far = np.zeros((2, P + 4 * P), np.float32)
    far[0, :L] = FAR
    far[1, L:P] = FAR
    k = np.arange(4 * P) % P
    far[0, P:] = k >= L
    far[1, P:] = k < L
    return c, far


def flamingo(nc, x, ctx_tok, ctx_t, wq, wk, wv, wo, cols, rows, gates, consts, far,
             f0_wg, f0_w12, f0_w3, wqv, f1_wg, f1_w1, f1_w2, out):
    with ExitStack() as stack:
        def sb(name, shape, dt=F32):
            return stack.enter_context(nc.sbuf_tensor(name, shape, dt))

        def sem(name):
            return stack.enter_context(nc.semaphore(name))

        xs = sb("xs", [P, CH, D])
        ln = sb("ln", [P, CH, 2])
        cst = sb("cst", [P, C_N])
        colv = sb("colv", [P, 6])
        rowv = sb("rowv", [1, R_N])
        gate = sb("gate", [P, 5])
        tg = sb("tg", [P, 4])
        ones = sb("ones", [1, P])
        farf = sb("farf", [2, 5 * P])
        farb = sb("farb", [2, 5 * P], BF16)
        half = sb("half", [P, 4])
        stat = sb("stat", [P, 2, 4, 6])
        mv = sb("mv", [P, 2, 4, 2])
        ve = sb("ve", [P, 2, 4])

        wq_s, wk_s, wv_s, wo_s = (sb(n, [P, D]) for n in ("wq_s", "wk_s", "wv_s", "wo_s"))
        wv_eo = sb("wv_eo", [P, 2, D])
        bqs = sb("bqs", [P, 1])
        bkm = sb("bkm", [P, HG])
        row0 = sb("row0", [1, D])
        row1 = sb("row1", [1, D])
        xn = sb("xn", [P, 2, 4, D])
        cT = sb("cT", [P, 2, 4 * P])
        ctk = sb("ctk", [P, 2, 4, D])
        xT = sb("xT", [P, 2, 4 * P])
        QT = sb("QT", [P, 2, NG, 2 * P])
        Kb = sb("Kb", [P, 2, HG, 2 * P])
        Vb = sb("Vb", [P, 2, 4, NH // 2, 18])
        Pr = sb("Pr", [P, 2, NG, 512])
        PT = sb("PT", [P, NG, 512])
        mx = sb("mx", [P, NG, 8])
        rec = sb("rec", [P, NH, 2])
        att = sb("att", [P, 2 * D])
        attT = sb("attT", [P, 2 * P])

        f0g_s = sb("f0g_s", [P, E])
        f0w12_s = sb("f0w12_s", [P, E, 2 * HID])
        f0w3_s = sb("f0w3_s", [P, E, 2, D])
        sil = sb("sil", [P, 2, HID])
        act = sb("act", [P, 2, HID])
        aT = sb("aT", [P, 2, 2, P])
        xb = sb("xb", [P, 4, D])
        xbT = sb("xbT", [P, 2, P])
        yb = sb("yb", [P, 4, D])
        zero = sb("zero", [P, D])
        xr = sb("xr", [P, 2, 2, D])
        upb = sb("upb", [P, P], BF16)
        onb = sb("onb", [P, P], BF16)
        chosen = sb("chosen", [P, 2, E], BF16)
        run = sb("run", [P, E])
        pos = sb("pos", [P, 2, E])
        ohp = sb("ohp", [P, 2, 2, E])
        row = sb("row", [P, 4])
        rowu = sb("rowu", [P, 2, 4], U32)
        kept_row = sb("kept_row", [P, UA, 4])
        kept_e = sb("kept_e", [P, UA, 4])
        kept_w = sb("kept_w", [P, UA, 4])
        back = sb("back", [P, UA, 4], U32)
        cnt = sb("cnt", [P, E], U32)
        cntf = sb("cntf", [P, E])
        nbf = sb("nbf", [P, E])
        trn = sb("trn", [P, E, E])
        cs = sb("cs", [P, E])
        shift = sb("shift", [P, E])
        ge = sb("ge", [1, NB, E])
        ej = sb("ej", [1, NB + PACK - 1])
        word = sb("word", [1, NB])
        cn = sb("cn", [1, NB])
        table = sb("table", [1, 2, NB], U32)
        tail = sb("tail", [1, E], U32)
        eqd = sb("eqd", [P, 4 * UA, E])
        bkf = sb("bkf", [P, 4 * UA])
        gidx = sb("gidx", [P, 2, 8], U32)
        yg = sb("yg", [P, 2, 8, D])
        lg = sb("lg", [P, 4, E])
        top = sb("top", [P, 4, 8])
        idx = sb("idx", [P, 4, 8], U32)
        idf = sb("idf", [P, 4, 8])
        dif = sb("dif", [P, 4])
        pe2 = sb("pe2", [P, 4])
        den = sb("den", [P, 4])
        w1g = sb("w1g", [P, 4])
        w2g = sb("w2g", [P, 4])
        oh = sb("oh", [P, 2, 4, E])
        cmb = sb("cmb", [P, 4, E])

        wqv_s = sb("wqv_s", [P, 4, D])
        wqv_g = sb("wqv_g", [P, 4, D])
        e3 = sb("e3", [P, 4 * P])
        rmx = sb("rmx", [P, 4])
        nmx = sb("nmx", [P, 4])
        Pc = sb("Pc", [P, 2, 4, P])
        sm = sb("sm", [P, 2, 4])
        rsm = sb("rsm", [P, 4])
        mcol = sb("mcol", [P, 4])
        bm = sb("bm", [4, 2])
        brow = sb("brow", [4, 2, L])
        bs = sb("bs", [4, 2])
        br = sb("br", [4, 2])
        wrow = sb("wrow", [4, P])
        wbd = sb("wbd", [P, 4, 2])
        hc = sb("hc", [P, 8])
        PcT = sb("PcT", [P, 4 * P])
        hqT = sb("hqT", [P, 4 * P])
        ehq = sb("ehq", [P, 4 * P])
        w1c = sb("w1c", [P, 4, 4])
        ehc = sb("ehc", [P, 2, 4 * P])

        f1g_s = sb("f1g_s", [P, E])
        f1w1_s = sb("f1w1_s", [P, E * R])
        f1w2_s = sb("f1w2_s", [P, 4, D])
        hg = sb("hg", [P, 2, E * R])
        hgg = sb("hgg", [P, 2, E * R])
        hT = sb("hT", [P, 2, 4 * P])

        ident = cst[:, C_ID:C_ID + P]
        iota = cst[:, C_IO:C_IO + E]

        bank = [stack.enter_context(nc.psum_tensor(f"bank{i}", [P, 512], F32)) for i in range(8)]

        sent = nc.dram_tensor("sent", (E * REGION + E * P, D), F32, kind="Internal").ap()
        done = nc.dram_tensor("done", (NB * P, D), F32, kind="Internal").ap()

        ld_x = [sem(f"ld_x{i}") for i in range(4)]
        ld_small, ld_attn, ld_f0g, ld_f0, ld_c, ld_f1 = (
            sem(n) for n in ("ld_small", "ld_attn", "ld_f0g", "ld_f0", "ld_c", "ld_f1"))
        ld_cT = [sem(f"ld_cT{i}") for i in range(2)]
        ld_cC = [sem(f"ld_cC{i}") for i in range(2)]
        sent_s = [sem(f"sent{i}") for i in range(2)]
        zeroed = sem("zeroed")
        ld_b = [sem(f"ld_b{i}") for i in range(4)]
        st_b = [sem(f"st_b{i}") for i in range(4)]
        back_s = [sem(f"back{i}") for i in range(2)]
        fill, prep, prep_pe, prep_act, prep_b0 = (
            sem(n) for n in ("fill", "prep", "prep_pe", "prep_act", "prep_b0"))
        names = {}

        def S(name):
            if name not in names:
                names[name] = sem(name)
            return names[name]

        START_AT_ONE = {
            "vector": ("a_x", "a_nrm", "c_x", "c_sum", "d_hgg", "d_x", "mv0", "mv1", "mv2", "mv3"),
            "scalar": ("a_pts", "d_gelu", "d_hts"),
            "tensor": ("a_pv", "d_ht", "d_y"),
            "gpsimd": ("ln0", "ln1", "ln2", "ln3"),
        }

        def start_at_one(eng, which):
            for name in START_AT_ONE[which]:
                eng.sem_inc(S(name), 1)

        block = stack.enter_context(nc.Block())
        x_v = x.rearrange("(t p) c -> p t c", p=P)
        out_v = out.rearrange("(t p) c -> p t c", p=P)
        ctx_v = ctx_tok.rearrange("(t p) c -> p t c", p=P)

        def wait_alone(eng, semaphore, value):
            if not isinstance(value, int):
                eng.compute_val(value)
            eng.wait_ge(ld_small, 80)
            eng.wait_ge(semaphore, value)

        def skewed(eng, units, first, ahead, body):
            turns = (units - first - ahead) // 2
            with eng.Fori(0, turns) as i:
                for s in range(2):
                    body(i * 2 + (first + s), s, ahead)
            for u in range(first + 2 * turns, units):
                body(u, (u - first) % 2, units - 1 - u)

        def has(u, units=UA):
            return not isinstance(u, int) or 0 <= u < units

        def pipelined(eng, it, first, loop, behind, end):
            for u in range(first, loop):
                it(u, u % 2)
            with eng.Fori(0, (behind - loop) // 2) as i:
                for k in range(2):
                    it(i * 2 + (loop + k), (loop + k) % 2)
            for u in range(behind, end):
                it(u, u % 2)

        def wait(eng, semaphore, value):
            if not isinstance(value, int) or value > 0:
                eng.wait_ge(semaphore, value)

        def blocks(eng, step, turn=lambda t, n: None):
            turn(0, 8)
            for t in range(8):
                step(t, t % 4, t, 4)
            with eng.Fori(0, NB // 4 - 2) as i:
                turn(i * 4 + 5, 6)
                for q in range(4):
                    step(i * 4 + (8 + q), q, 8, 4)
            turn(NB - 3, 3)
            for t in range(NB, NB + 3):
                step(t, t % 4, 8, NB - 1 - t)

        @block.sync
        def _(sp):
            sp.dma_start(cst[:], consts).then_inc(ld_small, 16)
            sp.dma_start(colv[:], cols).then_inc(ld_small, 16)
            sp.dma_start(rowv[:], rows).then_inc(ld_small, 16)
            sp.dma_start(gate[:], gates.partition_broadcast(P)).then_inc(ld_small, 16)
            sp.dma_start(farf[:], far).then_inc(ld_small, 16)
            for i in range(4):
                sp.dma_start(xs[:, 8 * i:8 * i + 8, :], x_v[:, 8 * i:8 * i + 8, :]).then_inc(ld_x[i], 16)
                if i == 0:
                    for s in range(2):
                        sp.dma_start(cT[:, s, 0:2 * P], ctx_t[:, 2 * P * s:2 * P * (s + 1)]).then_inc(ld_cT[s], 16)
            with sp.Fori(0, UA // 2 - 1) as i:
                u = i * 2
                for s in range(2):
                    sp.wait_ge(S("a_v"), u + (s + 1))
                    sp.dma_start(cT[:, s, 0:2 * P], ctx_t[:, bass.ds((u + (s + 2)) * (2 * P), 2 * P)]).then_inc(ld_cT[s], 16)
            sp.wait_ge(fill, 11)
            for e in range(E):
                sp.dma_start(sent[E * REGION + P * e:E * REGION + P * (e + 1), :], zero[:]).then_inc(zeroed, 16)
            sp.wait_ge(S("tail"), 1)
            for e in range(E):
                r = sp.value_load(tail[0:1, e:e + 1], min_val=e * REGION, max_val=e * REGION + TOKENS)
                sp.dma_start(sent[bass.ds(r, P), :], zero[:]).then_inc(zeroed, 16)
            sp.wait_ge(zeroed, 32 * E)
            sp.wait_ge(S("table"), 2)
            for i in range(2):
                sp.wait_ge(sent_s[i], 64 * UA // 2)

            def b_load(t, k):
                r = sp.value_load(table[0:1, 1, bass.ds(t, 1)], min_val=0, max_val=E * REGION + (E - 1) * P)
                sp.dma_start(xb[:, k, :], sent[bass.ds(r, P), :]).then_inc(ld_b[k], 16)

            def b_store(t, k):
                sp.wait_ge(S("b_ys"), t + 1)
                sp.dma_start(done[bass.ds(t * P, P), :], yb[:, k, :]).then_inc(st_b[k], 16)

            for t in range(4):
                b_load(t, t)
            for t in range(4, 8):
                sp.wait_ge(S("b_xt"), t - 3)
                b_load(t, t % 4)
                if t >= 6:
                    b_store(t - 6, t - 6)
            with sp.Fori(0, NB // 4 - 2) as i:
                for k in range(4):
                    sp.wait_ge(S("b_xt"), i * 4 + (8 + k - 3))
                    b_load(i * 4 + (8 + k), k)
                    b_store(i * 4 + (8 + k - 6), (k + 2) % 4)
            for t in range(NB - 6, NB):
                b_store(t, t % 4)

            sp.wait_ge(S("a_v"), UA)
            for s in range(2):
                sp.dma_start(cT[:, s, :], ctx_t[:, 4 * P * s:4 * P * (s + 1)]).then_inc(ld_cC[s], 16)
                sp.dma_start(ctk[:, s], ctx_v[:, 4 * s:4 * s + 4, :]).then_inc(ld_cC[s], 16)
            with sp.Fori(0, U4 // 2 - 1) as i:
                u = i * 2
                for s in range(2):
                    sp.wait_ge(S("c_hq"), u + (s + 1))
                    sp.dma_start(cT[:, s, :], ctx_t[:, bass.ds((u + (s + 2)) * (4 * P), 4 * P)]).then_inc(ld_cC[s], 16)
                    sp.dma_start(ctk[:, s], ctx_v[:, bass.ds((u + (s + 2)) * 4, 4), :]).then_inc(ld_cC[s], 16)
            with sp.Fori(0, U4, 1) as u:
                sp.wait_ge(S("d_x"), 1 + u * 4 + 4)
                sp.dma_start(out_v[:, bass.ds(u * 4, 4), :], xs[:, bass.ds(u * 4, 4), :]).then_inc(S("stored"), 16)
            sp.wait_ge(S("stored"), 16 * U4)

        @block.gpsimd
        def _(pool):
            start_at_one(pool, "gpsimd")
            for c, value in enumerate((EPS, 1.0, -0.5, float(np.e))):
                nc.gpsimd.memset(half[:, c:c + 1], value).then_inc(fill, 1)
            nc.gpsimd.memset(ones[:], 1.0).then_inc(fill, 1)
            nc.gpsimd.memset(wv_eo[:], 0.0).then_inc(fill, 1)
            nc.gpsimd.memset(zero[:], 0.0).then_inc(fill, 1)
            nc.gpsimd.memset(onb[:], 1.0).then_inc(fill, 1)
            nc.gpsimd.memset(chosen[:], 0.0).then_inc(fill, 1)
            nc.gpsimd.memset(QT[:], 0.0).then_inc(fill, 1)
            nc.gpsimd.memset(w1c[:], 0.0).then_inc(fill, 1)
            pool.dma_start(f0g_s[:], f0_wg).then_inc(ld_f0g, 16)
            pool.dma_start(f0w12_s[:], f0_w12).then_inc(ld_f0, 16)
            pool.dma_start(f0w3_s[:], f0_w3).then_inc(ld_f0, 16)
            pool.dma_start(wqv_s[:], wqv).then_inc(ld_c, 16)
            pool.dma_start(f1g_s[:], f1_wg).then_inc(ld_f1, 16)
            pool.dma_start(f1w1_s[:], f1_w1).then_inc(ld_f1, 16)
            pool.dma_start(f1w2_s[:], f1_w2).then_inc(ld_f1, 16)
            pool.wait_ge(fill, 11)

            def rstd(k, u, n):
                pool.wait_ge(S(f"mv{k}"), 1 + u * n + n)
                h = k % 2
                nc.gpsimd.tensor_tensor(ve[:, h, 0:n], mv[:, h, 0:n, 1], half[:, 0:1].to_broadcast([P, n]), ALU.add).then_inc(S(f"ve{k // 3}"), 1)
                pool.wait_ge(S(f"ve{k // 3}"), stats_units[k] + u + 1)
                nc.gpsimd.tensor_copy(ln[:, bass.ds(u * n, n), 0], mv[:, h, 0:n, 0])
                nc.gpsimd.tensor_tensor(ln[:, bass.ds(u * n, n), 1], ve[:, h, 0:n], half[:, 2:3].to_broadcast([P, n]), ALU.pow).then_inc(S(f"ln{k}"), 1)

            def second_weight(k, u, n):
                pool.wait_ge(S("dif"), gated[k] + u + 1)
                nc.gpsimd.tensor_tensor(pe2[:, 0:n], half[:, 3:4].to_broadcast([P, n]), dif[:, 0:n], ALU.pow).then_inc(S("second"), 1)

            def send(u, s):
                wait_alone(pool, S("r_row"), u + 1)
                for k in range(2):
                    for c in range(2):
                        nc.gpsimd.indirect_dma_start(sent, bass.IndirectOffsetOnAxis(ap=rowu[:, s, 2 * k + c:2 * k + c + 1], axis=0),
                                                     xr[:, s, c, :], None).then_inc(sent_s[s], 16)

            def fetch(u, s):
                if not isinstance(u, int) or u >= 2:
                    wait_alone(pool, S("c_sum"), u * 2 - 1)
                nc.gpsimd.tensor_copy(gidx[:, s, :].rearrange("p (a j) -> p a j", a=2), back[:, bass.ds(u * 2, 2), :]).then_inc(S("c_idx"), 1)
                wait_alone(pool, S("c_idx"), u + 1)
                for j in range(8):
                    nc.gpsimd.indirect_dma_start(yg[:, s, j, :], None, done,
                                                 bass.IndirectOffsetOnAxis(ap=gidx[:, s, j:j + 1], axis=0)).then_inc(back_s[s], 16)

            with pool.Fori(0, U4) as u:
                rstd(0, u, 4)
            rstd(1, 0, 2)

            def body_a(u, s, left):
                if left:
                    rstd(1, u + 1, 2)
                second_weight(1, u, 2)
                send(u, s)

            skewed(pool, UA, 0, 2, body_a)
            pool.wait_ge(S("back"), 1)
            for k in range(4):
                pool.wait_ge(st_b[k], 16 * (NB // 4))

            def it_c(u, s):
                if has(u + 4, U4):
                    fetch(u + 4, s)
                if has(u - 1, U4):
                    rstd(3, u - 1, 4)
                if has(u + 3, U4):
                    rstd(2, u + 3, 4)

            pipelined(pool, it_c, -4, 1, U4 - 5, U4 + 1)
            with pool.Fori(0, U4) as u:
                second_weight(3, u, 4)

        @block.scalar
        def _(a):
            start_at_one(a, "scalar")
            for w_s, w in ((wq_s, wq), (wk_s, wk), (wv_s, wv), (wo_s, wo)):
                a.dma_start(w_s[:], w).then_inc(ld_attn, 16)
            a.wait_ge(ld_small, 80)
            nc.scalar.activation(tg[:], gate[:, 0:4], ACT.Tanh).then_inc(prep_act, 1)
            nc.scalar.activation(bqs[:], colv[:, BQ:BQ + 1], ACT.Copy, scale=float(DH) ** -0.5).then_inc(prep_act, 1)

            def a_xts(u):
                a.wait_ge(S("a_xt"), u + 1)
                nc.scalar.activation(xT[:, 0, 0:2 * P], bank[4][:, 0:2 * P], ACT.Copy).then_inc(S("a_xts"), 1)

            def a_qks(u, s):
                a.wait_ge(S("a_qk"), u + 1)
                for g in range(NG):
                    rows_g = slice(32 * g, 32 * (g + 1))
                    nc.scalar.activation(QT[rows_g, s, g, :], bank[4][rows_g, 0:2 * P], ACT.Identity, bias=bqs[rows_g], scale=float(DH) ** -0.5)
                for j in range(HG):
                    last = nc.scalar.activation(Kb[:, s, j, :], bank[4][:, 2 * P:4 * P], ACT.Identity,
                                                bias=bkm[:, j:j + 1], scale=cst[:, C_KM + j:C_KM + j + 1])
                last.then_inc(S("a_qks"), 1)

            def a_exp(u, s, g):
                a.wait_ge(S("a_sub"), u * 4 + (g + 1))
                nc.scalar.activation(Pr[:, s, g, :], Pr[:, s, g, :], ACT.Exp).then_inc(S("a_exp"), 1)

            def a_pts(u, g):
                a.wait_ge(S("a_pt"), u * 4 + (g + 1))
                if g == 0:
                    a.wait_ge(S("a_pv"), 1 + u)
                nc.scalar.activation(PT[:, g, :], bank[6 + g % 2][:], ACT.Copy).then_inc(S("a_pts"), 1)

            def a_ats(u):
                a.wait_ge(S("a_at"), u + 1)
                nc.scalar.activation(attT[:], bank[2][:, 0:2 * P], ACT.Copy).then_inc(S("a_ats"), 1)

            a.wait_ge(prep, 3)
            a.wait_ge(fill, 11)
            def r_xts(v):
                a.wait_ge(S("r_xt"), v + 1)
                nc.scalar.activation(xT[:, 1, 0:2 * P], bank[3][:, 0:2 * P], ACT.Copy).then_inc(S("r_xts"), 1)

            def it_a(u, s):
                if has(u):
                    a_pts(u, 0)
                    a_pts(u, 1)
                if has(u - 1):
                    a_ats(u - 1)
                if has(u + 2):
                    a_xts(u + 2)
                if has(u - 2):
                    r_xts(u - 2)
                if has(u):
                    a_pts(u, 2)
                    a_pts(u, 3)
                if has(u + 1):
                    a_exp(u + 1, 1 - s, 0)
                    a_exp(u + 1, 1 - s, 1)
                if has(u + 2):
                    a_qks(u + 2, s)
                if has(u + 1):
                    a_exp(u + 1, 1 - s, 2)
                    a_exp(u + 1, 1 - s, 3)

            pipelined(a, it_a, -3, 3, UA - 3, UA + 3)

            def b_step(t, q, first, last):
                k = q % 2
                if last >= 0:
                    a.wait_ge(S("b_xt"), t + 1)
                    nc.scalar.activation(xbT[:, k, :], bank[k][:, 0:P], ACT.Copy).then_inc(S("b_xts"), 1)
                if first >= 1 and last >= -1:
                    a.wait_ge(S("b_hg"), t)
                    if first >= 3:
                        a.wait_ge(S("b_act"), t - 2)
                    nc.scalar.activation(sil[:, 1 - k, :], bank[3 - k][:, 0:HID], ACT.Silu).then_inc(S("b_sil"), 1)
                if first >= 2 and last >= -2:
                    a.wait_ge(S("b_at"), t - 1)
                    if first >= 4:
                        a.wait_ge(S("b_y"), t - 3)
                    nc.scalar.activation(aT[:, k], bank[4 + k][:, 0:2 * P].rearrange("p (j n) -> p j n", n=P), ACT.Copy).then_inc(S("b_ats"), 1)

            blocks(a, b_step)

            def c_xts(u, s):
                wait(a, S("c_y"), u - 1)
                nc.scalar.activation(xT[:, s, :], bank[0][:], ACT.Copy).then_inc(S("c_xts"), 1)

            def c_e3(u):
                a.wait_ge(S("c_xt"), u + 1)
                nc.scalar.activation(e3[:], bank[0][:], ACT.Identity, bias=colv[:, W2S:W2S + 1],
                                     scale=colv[:, W3S:W3S + 1]).then_inc(S("c_e3"), 1)

            def c_exp(u, s):
                a.wait_ge(S("c_nmx"), u + 1)
                for k in range(4):
                    last = nc.scalar.activation(Pc[:, s, k, :], bank[1][:, P * k:P * (k + 1)], ACT.Exp,
                                                bias=nmx[:, k:k + 1], accum_out=sm[:, s, k:k + 1])
                last.then_inc(S("c_exp"), 1)

            def c_nrm(u, s):
                a.wait_ge(S("c_rsm"), u + 1)
                for k in range(4):
                    last = nc.scalar.activation(Pc[:, s, k, :], Pc[:, s, k, :], ACT.Copy, scale=rsm[:, k:k + 1])
                last.then_inc(S("c_nrm"), 1)

            def c_bexp(u):
                a.wait_ge(S("c_bsub"), u + 1)
                nc.scalar.activation(brow[:], brow[:], ACT.Exp).then_inc(S("c_bexp"), 1)

            def c_pts(u):
                a.wait_ge(S("c_pt"), u + 1)
                nc.scalar.activation(PcT[:], bank[3][:], ACT.Copy).then_inc(S("c_pts"), 1)

            def c_hqs(u):
                a.wait_ge(S("c_hq"), u + 1)
                nc.scalar.activation(hqT[:], bank[4][:], ACT.Copy).then_inc(S("c_hqs"), 1)

            def it_c(u, s):
                if has(u + 1, U4):
                    c_xts(u + 1, 1 - s)
                if has(u, U4):
                    c_hqs(u)
                if has(u + 1, U4):
                    c_exp(u + 1, 1 - s)
                if has(u + 2, U4):
                    c_e3(u + 2)
                if has(u + 1, U4):
                    c_nrm(u + 1, 1 - s)
                    c_bexp(u + 1)
                    c_pts(u + 1)

            pipelined(a, it_c, -3, 1, U4 - 3, U4 + 1)

            def d_xts(u, s):
                a.wait_ge(S("d_xt"), u + 1)
                nc.scalar.activation(xT[:, s, :], bank[0][:], ACT.Copy).then_inc(S("d_xts"), 1)

            def d_gelu(u, k):
                a.wait_ge(S("d_h"), u * 4 + (k + 1))
                a.wait_ge(S("d_hgg"), 1 + u * 4 + max(k - 1, 0))
                nc.scalar.activation(hg[:, k % 2, :], bank[1 + k % 2][:], ACT.Gelu).then_inc(S("d_gelu"), 1)

            def d_hts(u, k):
                a.wait_ge(S("d_ht"), 1 + u * 4 + (k + 1))
                a.wait_ge(S("d_y"), 1 + u * 4 + max(k - 1, 0))
                nc.scalar.activation(hT[:, k % 2, :], bank[3 + k % 2][:], ACT.Copy).then_inc(S("d_hts"), 1)

            def body_d(u, s, left):
                d_gelu(u, 0)
                d_gelu(u, 1)
                d_hts(u, 0)
                if left:
                    d_xts(u + 1, 1 - s)
                d_gelu(u, 2)
                d_hts(u, 1)
                d_gelu(u, 3)
                d_hts(u, 2)
                d_hts(u, 3)

            d_xts(0, 0)
            skewed(a, U4, 0, 2, body_d)

        @block.vector
        def _(v):
            start_at_one(v, "vector")
            v.wait_ge(ld_small, 80)
            v.wait_ge(prep_act, 2)
            nc.vector.tensor_scalar(bkm[:], cst[:, C_KM:C_KM + HG], colv[:, BK:BK + 1], None, ALU.mult).then_inc(prep, 1)
            nc.vector.tensor_scalar(row1[:], rowv[:, R_BQV:R_BQV + D], tg[0:1, 1:2], None, ALU.mult).then_inc(prep, 1)
            for s in range(2):
                last = nc.vector.tensor_copy(Vb[:, s, :, :, 16:18],
                                             cst[:, C_VM:C_VM + 2].unsqueeze(1).unsqueeze(1).to_broadcast([P, 4, NH // 2, 2]))
            last.then_inc(prep, 1)
            nc.vector.tensor_copy(farb[:], farf[:]).then_inc(prep, 1)
            nc.vector.tensor_copy(upb[:], cst[:, C_UP:C_UP + P]).then_inc(S("r_prep"), 1)
            nc.vector.tensor_copy(run[:], cst[:, C_RG:C_RG + E]).then_inc(S("r_run"), 1)
            v.wait_ge(ld_attn, 64)
            v.wait_ge(fill, 11)
            nc.vector.tensor_scalar(wo_s[:], wo_s[:], tg[:, 0:1], None, ALU.mult).then_inc(prep, 1)
            nc.vector.tensor_scalar(rowv[:, R_BO:R_BO + D], rowv[:, R_BO:R_BO + D], tg[0:1, 0:1], None, ALU.mult).then_inc(prep, 1)
            for e in range(2):
                last = nc.vector.tensor_copy(wv_eo[:, e, :].rearrange("p (h e d) -> p h e d", e=2, d=DH)[:, :, e, :],
                                             wv_s[:].rearrange("p (h e d) -> p h e d", e=2, d=DH)[:, :, e, :])
            last.then_inc(prep, 1)
            nc.vector.tensor_copy(w1c[:].rearrange("p c m -> p (c m)")[:, 0:16:5], colv[:, W1S:W1S + 1].to_broadcast([P, 4])).then_inc(prep, 1)
            v.wait_ge(ld_c, 16)
            nc.vector.tensor_scalar(wqv_g[:], wqv_s[:], tg[:, 1:2], None, ALU.mult).then_inc(prep, 1)
            v.wait_ge(prep_pe, 1)
            nc.vector.tensor_copy(row0[:], bank[7][0:1, 0:D]).then_inc(prep_b0, 1)

            def sums(k, u, n):
                wait_alone(v, S(f"mv{k}"), 1 + u * n)
                if k:
                    wait_alone(v, S(WRITTEN[k]), 1 + (u + 1) * WRITES[k])
                for c in range(n):
                    nc.vector.bn_stats(stat[:, k % 2, c, :], xs[:, u * n + c, :]).then_inc(S(f"bn{k // 3}"), 1)

            def moments(k, u, n):
                wait_alone(v, S(f"ln{k}"), 1 + u)
                wait_alone(v, S(f"bn{k // 3}"), CH * (k % 3) + u * n + n)
                for c in range(n):
                    nc.vector.bn_aggr(mv[:, k % 2, c, :], stat[:, k % 2, c, :]).then_inc(S(f"mv{k}"), 1)

            def stats(k, u, n):
                sums(k, u, n)
                moments(k, u, n)

            def norm(u, n, dst, signal, k=0):
                if k:
                    v.wait_ge(S(f"ln{k}"), 2 + u)
                for c in range(n):
                    last = nc.vector.tensor_scalar(dst[:, c, :], xs[:, u * n + c, :], ln[:, u * n + c, 0:1],
                                                   ln[:, u * n + c, 1:2], ALU.subtract, ALU.mult)
                last.then_inc(S(signal), 1)

            for i in range(4):
                v.wait_ge(ld_x[i], 16)
                for u in range(2 * i, 2 * i + 2):
                    stats(0, u, 4)

            v.wait_ge(S("ln0"), 1 + U4)

            def a_vs(u, s):
                v.wait_ge(S("a_v"), u + 1)
                nc.vector.tensor_copy(Vb[:, s, :, :, 0:16],
                                      bank[5][:].rearrange("p (b h d) -> p b h d", b=4, d=16)).then_inc(S("a_vs"), 1)

            def scores(g):
                return bank[g % 2][:].rearrange("p (m k) -> p m k", k=L)

            def a_max(u, g):
                v.wait_ge(S("a_s"), u * 4 + (g + 1))
                nc.vector.tensor_reduce(mx[:, g, :], scores(g), AX, ALU.max).then_inc(S("a_max"), 1)

            def a_sub(u, s, g):
                v.wait_ge(S("a_max"), u * 4 + (g + 1))
                nc.vector.tensor_tensor(Pr[:, s, g, :].rearrange("p (m k) -> p m k", k=L), scores(g),
                                        mx[:, g, :].unsqueeze(2).to_broadcast([P, 8, L]), ALU.subtract).then_inc(S("a_sub"), 1)

            def a_rec(u):
                v.wait_ge(S("a_pv"), 1 + u + 1)
                nc.vector.reciprocal(rec[:], bank[5][:, 0:NH * 18].rearrange("p (m c) -> p m c", c=18)[:, :, 16:18]).then_inc(S("a_rec"), 1)

            def a_nrm(u):
                v.wait_ge(S("a_rec"), u + 1)
                o = bank[5][:, 0:NH * 18].rearrange("p (m c) -> p m c", c=18)
                nc.vector.tensor_tensor(att[:].rearrange("p (m e d) -> p m e d", e=2, d=DH),
                                        o[:, :, 0:16].rearrange("p m (e d) -> p m e d", e=2),
                                        rec[:].unsqueeze(3).to_broadcast([P, NH, 2, DH]), ALU.mult).then_inc(S("a_nrm"), 1)

            def a_x(u):
                v.wait_ge(S("a_y"), u + 1)
                xu = xs[:, bass.ds(u * 2, 2), :] if not isinstance(u, int) else xs[:, 2 * u:2 * u + 2, :]
                nc.vector.tensor_tensor(xu, bank[2][:, 2 * P:4 * P].rearrange("p (c d) -> p c d", d=D), xu, ALU.add).then_inc(S("a_x"), 1)


            def logits(k, u, n, scores):
                v.wait_ge(S("lgp"), gated[k] + u + 1)
                nc.vector.tensor_copy(lg[:, 0:n, :], scores).then_inc(S("lgs"), 1)

            def largest(k, u, n):
                wait_alone(v, S("lgs"), gated[k] + u + 1)
                for c in range(n):
                    nc.vector.max(top[:, c, :], lg[:, c, :]).then_inc(S("top"), 1)

            def experts(k, u, n):
                v.wait_ge(S("top"), gated[k] * 2 + u * n + n)
                nc.vector.tensor_tensor(dif[:, 0:n], top[:, 0:n, 1], top[:, 0:n, 0], ALU.subtract).then_inc(S("dif"), 1)
                for c in range(n):
                    nc.vector.max_index(idx[:, c, :], top[:, c, :], lg[:, c, :]).then_inc(S("idx"), 1)

            def as_float(k, u, n):
                v.wait_ge(S("idx"), gated[k] * 2 + u * n + n)
                nc.vector.tensor_copy(idf[:, 0:n, :], idx[:, 0:n, :]).then_inc(S("idf"), 1)

            def one_hot(k, u, n):
                v.wait_ge(S("idf"), gated[k] + u + 1)
                for h in range(2):
                    nc.vector.tensor_tensor(oh[:, h, 0:n, :], iota.unsqueeze(1).to_broadcast([P, n, E]),
                                            idf[:, 0:n, h:h + 1].to_broadcast([P, n, E]), ALU.is_equal).then_inc(S("oh"), 1)

            def denominator(k, u, n):
                v.wait_ge(S("second"), gated[k] + u + 1)
                nc.vector.tensor_scalar(den[:, 0:n], pe2[:, 0:n], 1.0, None, ALU.add).then_inc(S("den"), 1)

            def inverse(k, u, n):
                v.wait_ge(S("den"), gated[k] * 2 + u * 2 + 1)
                nc.vector.reciprocal(den[:, 0:n], den[:, 0:n]).then_inc(S("den"), 1)

            def first_weight(k, u, n, g, factor, w1):
                v.wait_ge(S("den"), gated[k] * 2 + u * 2 + 2)
                nc.vector.tensor_scalar(w1, den[:, 0:n], tg[:, g:g + 1], factor, ALU.mult, ALU.mult).then_inc(S("w"), 1)

            def second_weight(k, u, n, w1, w2):
                v.wait_ge(S("w"), gated[k] * 2 + u * 2 + 1)
                nc.vector.tensor_tensor(w2, w1, pe2[:, 0:n], ALU.mult).then_inc(S("w"), 1)

            def r_ln(w, s):
                if not isinstance(w, int) or w >= 2:
                    v.wait_ge(sent_s[s], (w - s) * 32)
                norm(w, 2, xr[:, s], "r_ln", 1)

            def r_mask(w):
                v.wait_ge(S("oh"), w * 2 + 2)
                nc.vector.tensor_tensor(chosen[:], oh[:, 0, 0:2, :], oh[:, 1, 0:2, :], ALU.add).then_inc(S("r_m"), 1)

            def r_pos(w):
                v.wait_ge(S("r_rank"), w + 1)
                v.wait_ge(S("r_run"), w + 1)
                nc.vector.tensor_tensor(pos[:], bank[3][:, RK:RK + 2 * E].rearrange("p (c e) -> p c e", e=E),
                                        run[:].unsqueeze(1).to_broadcast([P, 2, E]), ALU.add).then_inc(S("r_pos"), 1)

            def r_own(w):
                v.wait_ge(S("r_pos"), w + 1)
                nc.vector.tensor_tensor(ohp[:], oh[:, :, 0:2, :], pos[:].unsqueeze(1).to_broadcast([P, 2, 2, E]), ALU.mult).then_inc(S("r_ohp"), 1)
                nc.vector.tensor_tensor(run[:], bank[3][:, RK + 2 * E:RK + 3 * E], run[:], ALU.add).then_inc(S("r_run"), 1)

            def r_sum(w):
                v.wait_ge(S("r_ohp"), w + 1)
                nc.vector.tensor_reduce(row[:], ohp[:].rearrange("p k c e -> p (k c) e"), AX, ALU.add).then_inc(S("r_red"), 1)

            def r_keep(w, s):
                v.wait_ge(S("r_red"), w + 1)
                nc.vector.tensor_copy(rowu[:, s, :], row[:]).then_inc(S("r_row"), 1)
                nc.vector.tensor_copy(kept_row[:, bass.ds(w, 1), :], row[:].unsqueeze(1)).then_inc(S("r_kept"), 1)
                nc.vector.tensor_copy(kept_e[:, bass.ds(w, 1), :].rearrange("p a (k c) -> p a k c", k=2),
                                      idf[:, 0:2, 0:2].rearrange("p c k -> p k c").unsqueeze(1)).then_inc(S("r_kept"), 1)

            def kept_weight(w, k):
                return kept_w[:, bass.ds(w, 1), 2 * k:2 * k + 2].rearrange("p a c -> p (a c)")

            def it_a(u, s):
                if has(u + 3):
                    wait(v, S("a_xt"), u + 2)
                    norm(u + 3, 2, xn[:, 1 - s], "a_ln")
                if has(u - 3):
                    r_pos(u - 3)
                if has(u - 2):
                    r_ln(u - 2, s)
                if has(u - 3):
                    r_own(u - 3)
                if has(u):
                    a_vs(u, s)
                if has(u - 3):
                    r_sum(u - 3)
                if has(u + 1):
                    a_max(u + 1, 0)
                if has(u - 3):
                    r_keep(u - 3, 1 - s)
                if has(u + 1):
                    a_sub(u + 1, 1 - s, 0)
                if has(u - 3):
                    denominator(1, u - 3, 2)
                if has(u + 1):
                    a_max(u + 1, 1)
                if has(u - 3):
                    inverse(1, u - 3, 2)
                if has(u + 1):
                    a_sub(u + 1, 1 - s, 1)
                if has(u - 3):
                    first_weight(1, u - 3, 2, 2, 1.0, kept_weight(u - 3, 0))
                if has(u - 1):
                    a_x(u - 1)
                if has(u - 3):
                    second_weight(1, u - 3, 2, kept_weight(u - 3, 0), kept_weight(u - 3, 1))
                if has(u - 2):
                    logits(1, u - 2, 2, bank[3][:, 2 * P:2 * P + 2 * E].rearrange("p (c e) -> p c e", e=E))
                if has(u - 1):
                    sums(1, u - 1, 2)
                if has(u - 2):
                    largest(1, u - 2, 2)
                if has(u - 1):
                    moments(1, u - 1, 2)
                if has(u + 1):
                    a_max(u + 1, 2)
                if has(u - 2):
                    experts(1, u - 2, 2)
                if has(u + 1):
                    a_sub(u + 1, 1 - s, 2)
                if has(u - 2):
                    as_float(1, u - 2, 2)
                if has(u + 1):
                    a_max(u + 1, 3)
                if has(u - 2):
                    one_hot(1, u - 2, 2)
                if has(u + 1):
                    a_sub(u + 1, 1 - s, 3)
                if has(u - 2):
                    r_mask(u - 2)
                if has(u):
                    a_rec(u)
                    a_nrm(u)

            pipelined(v, it_a, -3, 3, UA - 3, UA + 3)

            n_table = [0]

            def then(ins):
                n_table[0] += 1
                ins.then_inc(S("steps"), 1)
                v.wait_ge(S("steps"), n_table[0])

            v.wait_ge(S("r_run"), UA + 1)
            nc.vector.tensor_copy(tail[:], run[0:1, :]).then_inc(S("tail"), 1)
            then(nc.vector.tensor_tensor(cntf[:], run[:], cst[:, C_RG:C_RG + E], ALU.subtract))
            then(nc.vector.tensor_scalar(cnt[:], cntf[:], float(P - 1), None, ALU.add))
            then(nc.vector.tensor_scalar(cnt[:], cnt[:], 7, None, ALU.logical_shift_right))
            then(nc.vector.tensor_copy(nbf[:], cnt[:]))
            then(nc.vector.tensor_tensor(trn[:], nbf[:].unsqueeze(1).to_broadcast([P, E, E]),
                                         cst[:, C_TR:C_TR + E * E].rearrange("p (e f) -> p e f", f=E), ALU.mult))
            then(nc.vector.tensor_reduce(cs[:], trn[:], AX, ALU.add))
            blk = cst[0:1, C_J:C_J + NB]
            then(nc.vector.tensor_tensor(ge[:], blk.unsqueeze(2).to_broadcast([1, NB, E]),
                                         cs[0:1, :].unsqueeze(1).to_broadcast([1, NB, E]), ALU.is_ge))
            then(nc.vector.memset(ej[:], 0.0))
            then(nc.vector.tensor_reduce(ej[:, 0:NB], ge[:], AX, ALU.add))
            then(nc.vector.tensor_tensor(ge[:], ge[:], nbf[0:1, :].unsqueeze(1).to_broadcast([1, NB, E]), ALU.mult))
            then(nc.vector.tensor_reduce(cn[:], ge[:], AX, ALU.add))
            then(nc.vector.tensor_tensor(cn[:], blk, cn[:], ALU.subtract))
            then(nc.vector.tensor_scalar(cn[:], cn[:], float(P), None, ALU.mult))
            nc.vector.scalar_tensor_tensor(table[:, 1, :], ej[:, 0:NB], float(REGION), cn[:], ALU.mult, ALU.add).then_inc(S("table"), 1)
            v.wait_ge(S("table"), 1)
            then(nc.vector.tensor_scalar(ej[:], ej[:], float(E - 1), None, ALU.min))
            then(nc.vector.tensor_copy(word[:], ej[:, PACK - 1:PACK - 1 + NB]))
            for k in range(PACK - 2, 0, -1):
                then(nc.vector.scalar_tensor_tensor(word[:], word[:], float(E), ej[:, k:k + NB], ALU.mult, ALU.add))
            nc.vector.scalar_tensor_tensor(table[:, 0, :], word[:], float(E), ej[:, 0:NB], ALU.mult, ALU.add).then_inc(S("table"), 1)
            then(nc.vector.tensor_tensor(cs[:], cs[:], nbf[:], ALU.subtract))
            then(nc.vector.scalar_tensor_tensor(shift[:], cs[:], float(P), cst[:, C_RG:C_RG + E], ALU.mult, ALU.subtract))
            v.wait_ge(S("r_kept"), 2 * UA)
            then(nc.vector.tensor_tensor(eqd[:], kept_e[:].rearrange("p a j -> p (a j)").unsqueeze(2).to_broadcast([P, 4 * UA, E]),
                                         iota.unsqueeze(1).to_broadcast([P, 4 * UA, E]), ALU.is_equal))
            then(nc.vector.tensor_tensor(eqd[:], eqd[:], shift[:].unsqueeze(1).to_broadcast([P, 4 * UA, E]), ALU.mult))
            then(nc.vector.tensor_reduce(bkf[:], eqd[:], AX, ALU.add))
            nc.vector.tensor_tensor(back[:].rearrange("p a j -> p (a j)"), kept_row[:].rearrange("p a j -> p (a j)"),
                                    bkf[:], ALU.add).then_inc(S("back"), 1)

            def b_step(t, q, first, last):
                k = q % 2
                if first >= 1 and last >= -1:
                    v.wait_ge(S("b_sil"), t)
                    if first >= 3:
                        v.wait_ge(S("b_at"), t - 2)
                    nc.vector.tensor_tensor(act[:, 1 - k, :], sil[:, 1 - k, :], bank[3 - k][:, HID:2 * HID], ALU.mult).then_inc(S("b_act"), 1)
                if first >= 3:
                    v.wait_ge(S("b_y"), t - 2)
                    slot = (q + 1) % 4
                    if first >= 7:
                        v.wait_ge(st_b[slot], (t - (3 + slot)) * 4)
                    nc.vector.tensor_copy(yb[:, slot, :], bank[7 - k][:, 0:D]).then_inc(S("b_ys"), 1)

            blocks(v, b_step)

            def comb(u, s, k, a):
                if k == 0 and a == 0:
                    v.wait_ge(back_s[s], (u - s) * 64 + 128)
                if k == 1 and a == 0:
                    v.wait_ge(S("c_sum"), 1 + u * 2 + 1)
                for c in range(2):
                    xk = xs[:, u * 4 + (2 * a + c), :]
                    last = nc.vector.scalar_tensor_tensor(xk, yg[:, s, 4 * a + 2 * k + c, :],
                                                          kept_w[:, u * 2 + a, 2 * k + c:2 * k + c + 1], xk, ALU.mult, ALU.add)
                if a == 1:
                    last.then_inc(S("c_sum"), 1)

            def c_rmx(u):
                v.wait_ge(S("c_s"), u + 1)
                nc.vector.tensor_reduce(rmx[:], bank[1][:].rearrange("p (c k) -> p c k", k=P), AX, ALU.max).then_inc(S("c_rmx"), 1)

            def c_nmx(u):
                v.wait_ge(S("c_rmx"), u + 1)
                nc.vector.tensor_scalar(nmx[:], rmx[:], -1.0, None, ALU.mult).then_inc(S("c_nmx"), 1)
                nc.vector.tensor_scalar(mcol[:], rmx[:], gate[:, 4:5], None, ALU.add).then_inc(S("c_mcol"), 1)

            def maxima():
                return bank[2][0:4, P:2 * P].rearrange("p (b l) -> p b l", l=L)

            def c_bm(u):
                v.wait_ge(S("c_mt"), u + 1)
                nc.vector.tensor_reduce(bm[:], maxima(), AX, ALU.max).then_inc(S("c_bm"), 1)

            def c_bsub(u):
                v.wait_ge(S("c_bm"), u + 1)
                nc.vector.tensor_tensor(brow[:], maxima(), bm[:].unsqueeze(2).to_broadcast([4, 2, L]), ALU.subtract).then_inc(S("c_bsub"), 1)

            def c_bs(u):
                v.wait_ge(S("c_bexp"), u + 1)
                nc.vector.tensor_reduce(bs[:], brow[:], AX, ALU.add).then_inc(S("c_bs"), 1)

            def c_br(u):
                v.wait_ge(S("c_bs"), u * 2 + 1)
                nc.vector.reciprocal(br[:], bs[:]).then_inc(S("c_bs"), 1)

            def c_wrow(u):
                v.wait_ge(S("c_bs"), u * 2 + 2)
                nc.vector.tensor_tensor(wrow[:].rearrange("p (b l) -> p b l", l=L), brow[:],
                                        br[:].unsqueeze(2).to_broadcast([4, 2, L]), ALU.mult).then_inc(S("c_wrow"), 1)

            def c_wbd(u):
                v.wait_ge(S("c_wt"), u + 1)
                nc.vector.tensor_tensor(wbd[:], bank[2][:, 4:8].unsqueeze(2).to_broadcast([P, 4, 2]),
                                        cst[:, C_BI:C_BI + 2].unsqueeze(1).to_broadcast([P, 4, 2]), ALU.mult).then_inc(S("c_wbd"), 1)

            def c_hcs(u):
                v.wait_ge(S("c_hc"), u + 1)
                nc.vector.tensor_copy(hc[:], bank[2][:, 8:16]).then_inc(S("c_hcs"), 1)

            def c_ehc(u, s):
                v.wait_ge(S("c_hcs"), u + 1)
                nc.vector.tensor_tensor(ehc[:, s, :].rearrange("p (b l) -> p b l", l=L),
                                        xT[:, s, :].rearrange("p (b l) -> p b l", l=L),
                                        hc[:].unsqueeze(2).to_broadcast([P, 8, L]), ALU.mult).then_inc(S("c_ehc"), 1)

            def c_rsm(u, s):
                v.wait_ge(S("c_exp"), u + 1)
                nc.vector.reciprocal(rsm[:], sm[:, s, :]).then_inc(S("c_rsm"), 1)

            def c_ehq(u, s):
                v.wait_ge(S("c_hqs"), u + 1)
                nc.vector.tensor_tensor(ehq[:], hqT[:], xT[:, s, :], ALU.mult).then_inc(S("c_ehq"), 1)

            def c_x(u, s):
                v.wait_ge(S("c_y"), u + 1)
                xu = xs[:, bass.ds(u * 4, 4), :] if not isinstance(u, int) else xs[:, 4 * u:4 * u + 4, :]
                nc.vector.tensor_tensor(xu, bank[5 + s][:].rearrange("p (c d) -> p c d", d=D), xu, ALU.add).then_inc(S("c_x"), 1)

            def it_c(u, s):
                this, nxt, got, was = has(u, U4), has(u + 1, U4), has(u + 3, U4), has(u - 1, U4)
                if this:
                    c_ehq(u, s)
                if was:
                    c_x(u - 1, 1 - s)
                if nxt:
                    c_rmx(u + 1)
                    c_nmx(u + 1)
                if has(u + 2, U4):
                    wait(v, S("c_hc"), u + 1)
                    norm(u + 2, 4, xn[:, s], "c_ln", 2)
                if was:
                    sums(3, u - 1, 4)
                if nxt:
                    c_rsm(u + 1, 1 - s)
                    c_bm(u + 1)
                if got:
                    comb(u + 3, 1 - s, 0, 0)
                if nxt:
                    c_bsub(u + 1)
                if got:
                    comb(u + 3, 1 - s, 0, 1)
                if nxt:
                    c_bs(u + 1)
                if was:
                    moments(3, u - 1, 4)
                if nxt:
                    c_br(u + 1)
                if got:
                    comb(u + 3, 1 - s, 1, 0)
                if nxt:
                    c_wrow(u + 1)
                if got:
                    comb(u + 3, 1 - s, 1, 1)
                if nxt:
                    c_wbd(u + 1)
                if got:
                    sums(2, u + 3, 4)
                if nxt:
                    c_hcs(u + 1)
                if got:
                    moments(2, u + 3, 4)
                if nxt:
                    c_ehc(u + 1, 1 - s)

            pipelined(v, it_c, -3, 1, U4 - 3, U4 + 1)

            def d_gate(u, k):
                v.wait_ge(S("d_gelu"), 1 + u * 4 + (k + 1))
                if k == 0:
                    v.wait_ge(S("cmb"), u + 1)
                v.wait_ge(S("d_ht"), 1 + u * 4 + max(k - 1, 0))
                nc.vector.tensor_tensor(hgg[:, k % 2, :].rearrange("p (e r) -> p e r", r=R),
                                        hg[:, k % 2, :].rearrange("p (e r) -> p e r", r=R),
                                        cmb[:, k, :].unsqueeze(2).to_broadcast([P, E, R]), ALU.mult).then_inc(S("d_hgg"), 1)

            def d_acc(u, k):
                v.wait_ge(S("d_y"), 1 + u * 4 + (k + 1))
                xk = xs[:, u * 4 + k, :]
                nc.vector.tensor_tensor(xk, bank[5 + k % 2][:, 0:D], xk, ALU.add).then_inc(S("d_x"), 1)

            def d_choose(u):
                logits(3, u, 4, bank[7][:, 0:4 * E].rearrange("p (c e) -> p c e", e=E))
                for step in (largest, experts, as_float, one_hot):
                    step(3, u, 4)

            def d_weigh(u):
                denominator(3, u, 4)
                inverse(3, u, 4)
                first_weight(3, u, 4, 3, SCALING, w1g[:])
                second_weight(3, u, 4, w1g[:], w2g[:])
                v.wait_ge(S("oh"), UA * 2 + u * 2 + 2)
                v.wait_ge(S("w"), UA * 2 + u * 2 + 2)
                for h, w in enumerate((w1g, w2g)):
                    nc.vector.tensor_tensor(oh[:, h], oh[:, h], w[:].unsqueeze(2).to_broadcast([P, 4, E]), ALU.mult).then_inc(S("ohw"), 1)
                v.wait_ge(S("ohw"), u * 2 + 2)
                nc.vector.tensor_tensor(cmb[:], oh[:, 0], oh[:, 1], ALU.add).then_inc(S("cmb"), 1)

            norm(0, 4, xn[:, 0], "d_ln", 3)
            norm(1, 4, xn[:, 1], "d_ln", 3)
            d_choose(0)

            def body_d(u, s, left):
                d_weigh(u)
                d_gate(u, 0)
                d_gate(u, 1)
                d_acc(u, 0)
                if left >= 2:
                    norm(u + 2, 4, xn[:, s], "d_ln", 3)
                d_gate(u, 2)
                d_acc(u, 1)
                d_gate(u, 3)
                if left:
                    d_choose(u + 1)
                d_acc(u, 2)
                d_acc(u, 3)

            skewed(v, U4, 0, 2, body_d)

        @block.tensor
        def _(pe):
            start_at_one(pe, "tensor")
            mm = nc.tensor.matmul

            pe.wait_ge(prep, 7)
            mm(bank[7][0:1, 0:D], colv[:, BV:BV + 1], wo_s[:], start=True, stop=False)
            mm(bank[7][0:1, 0:D], ones[0:1, 0:1], rowv[0:1, R_BO:R_BO + D], start=False, stop=True).then_inc(prep_pe, 1)

            def transposes(done, dst, src, n):
                for c in range(n):
                    last = nc.tensor.transpose(dst[:, P * c:P * (c + 1)], src(c), ident)
                last.then_inc(S(done), 1)

            def a_xt(u, s):
                pe.wait_ge(S("a_ln"), u + 1)
                wait(pe, S("a_qks"), u)
                transposes("a_xt", bank[4], lambda c: xn[:, s, c, :], 2)

            def a_v(u, s):
                pe.wait_ge(S("a_nrm"), 1 + u)
                for b in range(4):
                    for e in range(2):
                        last = mm(bank[5][L * e:L * (e + 1), P * b:P * (b + 1)], cT[:, s, L * b:L * (b + 1)],
                                  wv_eo[:, e, :], start=True, stop=True)
                last.then_inc(S("a_v"), 1)

            def a_qk(u, s):
                pe.wait_ge(S("a_xts"), u + 1)
                pe.wait_ge(ld_cT[s], (u - s) * 8 + 16)
                mm(bank[4][:, 0:2 * P], wq_s[:], xT[:, 0, 0:2 * P], start=True, stop=True)
                mm(bank[4][:, 2 * P:4 * P], wk_s[:], cT[:, s, 0:2 * P], start=True, stop=True).then_inc(S("a_qk"), 1)

            def a_s(u, s, g):
                if g == 0:
                    pe.wait_ge(S("a_qks"), u + 1)
                wait(pe, S("a_sub"), u * 4 + (g - 1))
                for p in range(2):
                    for b in range(2):
                        t = P * p + L * b
                        last = mm(bank[g % 2][L * b:L * (b + 1), 256 * p:256 * (p + 1)], QT[:, s, g, t:t + L],
                                  Kb[:, s, :, t:t + L], start=True, stop=True)
                last.then_inc(S("a_s"), 1)

            def a_pt(u, s, g):
                pe.wait_ge(S("a_exp"), u * 4 + (g + 1))
                wait(pe, S("a_pts"), u * 4 + g)
                transposes("a_pt", bank[6 + g % 2], lambda c: Pr[:, s, g, P * c:P * (c + 1)], 4)

            def a_pv(u, s, g):
                pe.wait_ge(S("a_pts"), 1 + u * 4 + (g + 1))
                if g == 0:
                    pe.wait_ge(S("a_vs"), u + 1)
                for p in range(2):
                    for h in range(2):
                        for b in range(2):
                            m = (p * 8 + 2 * g + h) * 18
                            c = P * (2 * p + h) + L * b
                            last = mm(bank[5][L * b:L * (b + 1), m:m + 18], PT[:, g, c:c + L],
                                      Vb[:, s, 2 * p + b, 2 * g + h, :], start=True, stop=True)
                if g == NG - 1:
                    last.then_inc(S("a_pv"), 1)

            def a_at(u):
                pe.wait_ge(S("a_nrm"), 1 + u + 1)
                pe.wait_ge(S("a_x"), 1 + u)
                transposes("a_at", bank[2], lambda c: att[:, D * c:D * (c + 1)], 2)

            def a_y(u):
                pe.wait_ge(S("a_ats"), u + 1)
                for c in range(2):
                    o = bank[2][:, P * (2 + c):P * (3 + c)]
                    mm(o, attT[:, P * c:P * (c + 1)], wo_s[:], start=True, stop=False)
                    last = mm(o, ones[:], row0[:], start=False, stop=True)
                last.then_inc(S("a_y"), 1)

            pe.wait_ge(prep_b0, 1)

            def r_x(w, s):
                pe.wait_ge(S("r_ln"), w + 1)
                pe.wait_ge(S("r_run"), w + 1)
                transposes("r_xt", bank[3], lambda c: xr[:, s, c, :], 2)

            def r_lg(w):
                pe.wait_ge(S("r_xts"), w + 1)
                for c in range(2):
                    last = mm(bank[3][:, 2 * P + E * c:2 * P + E * (c + 1)], xT[:, 1, P * c:P * (c + 1)], f0g_s[:], start=True, stop=True)
                last.then_inc(S("lgp"), 1)

            def r_rank(w):
                pe.wait_ge(S("r_m"), w + 1)
                of = [bank[3][:, RK + E * c:RK + E * (c + 1)] for c in range(3)]
                mm(of[0], upb[:], chosen[:, 0, :], start=True, stop=True)
                mm(of[1], onb[:], chosen[:, 0, :], start=True, stop=False)
                mm(of[1], upb[:], chosen[:, 1, :], start=False, stop=True)
                mm(of[2], onb[:], chosen[:, 0, :], start=True, stop=False)
                mm(of[2], onb[:], chosen[:, 1, :], start=False, stop=True).then_inc(S("r_rank"), 1)

            pe.wait_ge(S("r_prep"), 1)
            pe.wait_ge(ld_f0g, 16)

            def it_a(u, s):
                if has(u):
                    a_pt(u, s, 0)
                    a_pt(u, s, 1)
                    a_v(u, s)
                if has(u + 1):
                    a_s(u + 1, 1 - s, 0)
                if has(u - 1):
                    a_at(u - 1)
                if has(u + 2):
                    a_xt(u + 2, s)
                if has(u + 1):
                    a_s(u + 1, 1 - s, 1)
                if has(u - 2):
                    r_x(u - 2, s)
                if has(u):
                    a_pt(u, s, 2)
                    a_pt(u, s, 3)
                if has(u - 1):
                    a_y(u - 1)
                if has(u - 2):
                    r_lg(u - 2)
                if has(u):
                    a_pv(u, s, 0)
                    a_pv(u, s, 1)
                if has(u + 2):
                    a_qk(u + 2, s)
                if has(u + 1):
                    a_s(u + 1, 1 - s, 2)
                if has(u):
                    a_pv(u, s, 2)
                if has(u + 1):
                    a_s(u + 1, 1 - s, 3)
                if has(u):
                    a_pv(u, s, 3)
                if has(u - 2):
                    r_rank(u - 2)

            pipelined(pe, it_a, -3, 3, UA - 3, UA + 3)

            pe.wait_ge(S("table"), 2)
            pe.wait_ge(ld_f0, 32)

            experts_of = {}

            def load_experts(t, n):
                experts_of.clear()
                for j in range(0, n, PACK):
                    w = pe.value_load(table[0:1, 0, bass.ds(t + j, 1)], min_val=0, max_val=E ** PACK - 1)
                    for k in range(min(PACK, n - j)):
                        experts_of[(t if isinstance(t, int) else -3) + j + k] = (w >> (3 * k)) & (E - 1)

            def expert(t, q, behind):
                return experts_of[(t if isinstance(t, int) else q) - behind]

            def b_step(t, q, first, last):
                k = q % 2
                if last >= 0:
                    pe.wait_ge(ld_b[q], (t - q) * 4 + 16)
                    if first >= 2:
                        pe.wait_ge(S("b_xts"), t - 1)
                    transposes("b_xt", bank[k], lambda c: xb[:, q, :], 1)
                if first >= 1 and last >= -1:
                    e = expert(t, q, 1)
                    pe.wait_ge(S("b_xts"), t)
                    if first >= 3:
                        pe.wait_ge(S("b_act"), t - 2)
                    mm(bank[3 - k][:], xbT[:, 1 - k, :], f0w12_s[:, bass.ds(e, 1), :].rearrange("p e n -> p (e n)"),
                       start=True, stop=True).then_inc(S("b_hg"), 1)
                if first >= 2 and last >= -2:
                    pe.wait_ge(S("b_act"), t - 1)
                    if first >= 4:
                        pe.wait_ge(S("b_ats"), t - 3)
                    transposes("b_at", bank[4 + k], lambda c: act[:, k, P * c:P * (c + 1)], 2)
                if first >= 3:
                    e = expert(t, q, 3)
                    pe.wait_ge(S("b_ats"), t - 2)
                    if first >= 5:
                        pe.wait_ge(S("b_ys"), t - 4)
                    for j in range(2):
                        last_mm = mm(bank[7 - k][:, 0:D], aT[:, 1 - k, j, :],
                                     f0w3_s[:, bass.ds(e, 1), j, :].rearrange("p e n -> p (e n)"), start=j == 0, stop=j == 1)
                    last_mm.then_inc(S("b_y"), 1)

            blocks(pe, b_step, load_experts)

            pe.wait_ge(S("b_ys"), NB)
            pe.wait_ge(prep, 9)

            def c_xt(u, s):
                pe.wait_ge(S("c_ln"), u + 1)
                transposes("c_xt", bank[0], lambda c: xn[:, s, c, :], 4)

            def c_s(u, s):
                pe.wait_ge(ld_cC[s], (u - s) * 16 + 32)
                pe.wait_ge(S("c_e3"), u + 1)
                mm(bank[1][:], farb[:, 0:P], farb[:, P:5 * P], start=True, stop=False, skip_group_check=True)
                for c in range(4):
                    last = mm(bank[1][:, P * c:P * (c + 1)], e3[:, P * c:P * (c + 1)], cT[:, s, P * c:P * (c + 1)],
                              start=False, stop=True, skip_group_check=True)
                last.then_inc(S("c_s"), 1)

            def c_own(u, s):
                pe.wait_ge(S("c_xts"), u + 1)
                wait(pe, S("c_hcs"), u)
                for c in range(4):
                    mm(bank[2][0:4, P:2 * P], w1c[:, c, :], xT[:, s, P * c:P * (c + 1)], start=c == 0, stop=False)

            def c_mt(u):
                pe.wait_ge(S("c_mcol"), u + 1)
                mm(bank[2][0:4, P:2 * P], mcol[:], ident, start=False, stop=True).then_inc(S("c_mt"), 1)

            def c_wt(u):
                wait_alone(pe, S("c_wrow"), u + 1)
                nc.tensor.transpose(bank[2][:, 4:8], wrow[:], cst[0:4, C_ID:C_ID + 4]).then_inc(S("c_wt"), 1)

            def c_hc(u, s):
                pe.wait_ge(S("c_wbd"), u + 1)
                for c in range(4):
                    last = mm(bank[2][:, 8 + 2 * c:10 + 2 * c], xn[:, s, c, :], wbd[:, c, :], start=True, stop=True)
                last.then_inc(S("c_hc"), 1)

            def c_pt(u, s):
                pe.wait_ge(S("c_nrm"), u + 1)
                transposes("c_pt", bank[3], lambda c: Pc[:, s, c, :], 4)

            def c_hq(u, s):
                pe.wait_ge(S("c_pts"), u + 1)
                wait(pe, S("c_hqs"), u)
                for c in range(4):
                    last = mm(bank[4][:, P * c:P * (c + 1)], ctk[:, s, c, :], PcT[:, P * c:P * (c + 1)], start=True, stop=True)
                last.then_inc(S("c_hq"), 1)

            def c_y(u, s, c):
                if c == 0:
                    pe.wait_ge(S("c_ehq"), u + 1)
                    pe.wait_ge(S("c_ehc"), u + 1)
                    wait(pe, S("c_x"), u)
                o = bank[5 + s][:, P * c:P * (c + 1)]
                tok = slice(P * c, P * (c + 1))
                for i, f in enumerate((xT[:, s, tok], hqT[:, tok], ehq[:, tok], ehc[:, s, tok])):
                    mm(o, f, wqv_g[:, i, :], start=i == 0, stop=False)
                last = mm(o, ones[:], row1[:], start=False, stop=True)
                if c == 3:
                    last.then_inc(S("c_y"), 1)

            def it_c(u, s):
                this, nxt = has(u, U4), has(u + 1, U4)
                if nxt:
                    c_s(u + 1, 1 - s)
                    c_own(u + 1, 1 - s)
                if this:
                    c_y(u, s, 0)
                if has(u + 2, U4):
                    c_xt(u + 2, s)
                if nxt:
                    c_mt(u + 1)
                if this:
                    c_y(u, s, 1)
                    c_y(u, s, 2)
                if nxt:
                    c_pt(u + 1, 1 - s)
                if this:
                    c_y(u, s, 3)
                if nxt:
                    c_wt(u + 1)
                    c_hq(u + 1, 1 - s)
                    c_hc(u + 1, 1 - s)

            pipelined(pe, it_c, -3, 1, U4 - 3, U4 + 1)

            pe.wait_ge(S("c_x"), 1 + U4)
            pe.wait_ge(ld_f1, 48)

            def d_xt(u, s):
                pe.wait_ge(S("d_ln"), u + 1)
                transposes("d_xt", bank[0], lambda c: xn[:, s, c, :], 4)

            def d_lg(u, s):
                pe.wait_ge(S("d_xts"), u + 1)
                for c in range(4):
                    o = bank[7][:, E * c:E * (c + 1)]
                    mm(o, xT[:, s, P * c:P * (c + 1)], f1g_s[:], start=True, stop=False)
                    last = mm(o, ones[:], rowv[0:1, R_BG:R_BG + E], start=False, stop=True)
                last.then_inc(S("lgp"), 1)

            def d_h(u, s, k):
                pe.wait_ge(S("d_gelu"), 1 + u * 4 + max(k - 1, 0))
                mm(bank[1 + k % 2][:], xT[:, s, P * k:P * (k + 1)], f1w1_s[:], start=True, stop=True).then_inc(S("d_h"), 1)

            def d_ht(u, k):
                pe.wait_ge(S("d_hgg"), 1 + u * 4 + (k + 1))
                pe.wait_ge(S("d_hts"), 1 + u * 4 + max(k - 1, 0))
                transposes("d_ht", bank[3 + k % 2], lambda c: hgg[:, k % 2, P * c:P * (c + 1)], 4)

            def d_y(u, k):
                pe.wait_ge(S("d_hts"), 1 + u * 4 + (k + 1))
                pe.wait_ge(S("d_x"), 1 + u * 4 + max(k - 1, 0))
                for c in range(4):
                    last = mm(bank[5 + k % 2][:, 0:D], hT[:, k % 2, P * c:P * (c + 1)], f1w2_s[:, c, :],
                              start=c == 0, stop=c == 3)
                last.then_inc(S("d_y"), 1)

            d_xt(0, 0)
            d_lg(0, 0)

            def body_d(u, s, left):
                d_h(u, s, 0)
                d_h(u, s, 1)
                d_ht(u, 0)
                if left:
                    d_xt(u + 1, 1 - s)
                d_h(u, s, 2)
                d_ht(u, 1)
                d_y(u, 0)
                d_h(u, s, 3)
                d_ht(u, 2)
                d_y(u, 1)
                if left:
                    d_lg(u + 1, 1 - s)
                d_ht(u, 3)
                d_y(u, 2)
                d_y(u, 3)

            skewed(pe, U4, 0, 2, body_d)


def kernel(**inputs):
    import concourse.bacc as bacc
    from concourse.bass_utils import run_bass_kernel_spmd

    a = {k: np.asarray(v) for k, v in inputs.items()}
    consts, far = constants()
    lay = np.ascontiguousarray
    sim = a["L1_xattn_w_sim"].reshape(3, D)
    arrays = {
        "x": a["x"].reshape(TOKENS, D),
        "ctx_tok": a["ctx_1024"].reshape(TOKENS, D),
        "ctx_t": lay(a["ctx_1024"].reshape(TOKENS, D).T),
        "wq": lay(a["L0_xattn_wq_w"].T),
        "wk": lay(a["L0_xattn_wk_w"].T),
        "wv": lay(a["L0_xattn_wv_w"].T),
        "wo": lay(a["L0_xattn_wo_w"].T),
        "cols": lay(np.stack([a["L0_xattn_wq_b"], a["L0_xattn_wk_b"], a["L0_xattn_wv_b"], sim[0], sim[1], sim[2]], 1)),
        "rows": lay(np.concatenate([a["L0_xattn_wo_b"], a["L1_xattn_b_qv"], a["L1_ffn_bg"]])[None]),
        "gates": lay(np.concatenate([a["g_xattn"], a["g_ffn"], a["L1_xattn_b_sim"]])),
        "consts": consts,
        "far": far,
        "f0_wg": a["L0_ffn_Wg"],
        "f0_w12": lay(np.concatenate([a["L0_ffn_W1"], a["L0_ffn_W2"]], 2).transpose(1, 0, 2)),
        "f0_w3": lay(a["L0_ffn_W3"].reshape(E, 2, P, D).transpose(2, 0, 1, 3)),
        "wqv": lay(a["L1_xattn_W_qv"].reshape(4, D, D).transpose(1, 0, 2)),
        "f1_wg": lay(a["L1_ffn_Wg"].T),
        "f1_w1": lay(a["L1_ffn_W1"].reshape(E * R, D).T),
        "f1_w2": lay(a["L1_ffn_W2"].transpose(0, 2, 1).reshape(4, P, D).transpose(1, 0, 2)),
    }
    nc = bacc.Bacc("TRN2", target_bir_lowering=False, num_devices=1)
    args = {n: nc.dram_tensor(n + "_dram", v.shape, mybir.dt.from_np(v.dtype), kind="ExternalInput").ap()
            for n, v in arrays.items()}
    args["out"] = nc.dram_tensor("out_dram", (TOKENS, D), F32, kind="ExternalOutput").ap()
    flamingo(nc, **args)
    r = run_bass_kernel_spmd(nc, [{n + "_dram": v for n, v in arrays.items()}], core_ids=[0])
    return r.results[0]["out_dram"].reshape(a["x"].shape)
```

```python
from contextlib import ExitStack

import numpy as np

import concourse.bass as bass
from concourse import mybir

F32 = mybir.dt.float32
BF16 = mybir.dt.bfloat16
F32R = mybir.dt.float32r
U32 = mybir.dt.uint32
ACT = mybir.ActivationFunctionType
ALU = mybir.AluOpType
AX = mybir.AxisListType.X

P = 128
D = 128
L = 64
NH = 16
DH = D // NH
NG = 4
HG = NH // NG
E = 8
HID = 256
R = 64
SCALING = 2.0
TOKENS = 64 * L
EPS = 1e-5
REGION = TOKENS + P
TURN = 8
PACK = 10
RK = 2 * P + 2 * E
NB = 2 * TOKENS // P + E
WRITTEN = {1: "a_x", 2: "c_sum", 3: "c_x"}
WRITES = {1: 1, 2: 2, 3: 1}
FAR = -1e30
CH = TOKENS // P
UA = CH // 2
U4 = CH // 4
stats_units = {0: 0, 1: U4, 2: U4 + UA, 3: 0}
gated = {1: 0, 3: UA}

BQ, BK, BV, W1S, W2S, W3S = range(6)
C_ID, C_KM, C_VM, C_IO, C_BI, C_UP, C_RG, C_TR, C_P, C_BD = 0, 128, 132, 134, 142, 144, 272, 280, 344, 346
C_N = C_BD + 2 * NB
R_BO, R_BQV, R_BG = 0, 128, 256
R_N = 264


def constants():
    c = np.zeros((P, C_N), np.float32)
    p = np.arange(P)
    c[:, C_ID:C_ID + P] = np.eye(P)
    c[p, C_KM + (p % 32) // DH] = 1
    c[p, C_VM + p // L] = 1
    c[:, C_IO:C_IO + E] = np.arange(E)
    c[p, C_BI + p // L] = 1
    c[:, C_UP:C_UP + P] = p[:, None] < p[None, :]
    c[:, C_RG:C_RG + E] = np.arange(E) * REGION
    c[:, C_TR:C_TR + E * E] = (np.arange(E)[:, None] >= np.arange(E)[None, :]).reshape(-1)
    c[:, C_P] = p
    c[:, C_P + 1] = p * P
    ahead = p[:, None] - np.arange(NB)[None, :]
    half = PACK // 2
    for h in range(2):
        a = ahead - h * half
        c[:, C_BD + h * NB:C_BD + (h + 1) * NB] = np.where((a >= 0) & (a < half), float(E) ** a, 0)
    far = np.zeros((2, P + 4 * P), np.float32)
    far[0, :L] = FAR
    far[1, L:P] = FAR
    k = np.arange(4 * P) % P
    far[0, P:] = k >= L
    far[1, P:] = k < L
    return c, far


def flamingo(nc, x, ctx_tok, ctx_t, wq, wk, wv, wo, cols, rows, gates, consts, far,
             f0_wg, f0_w12, f0_w3, wqv, f1_wg, f1_w1, f1_w2, out):
    with ExitStack() as stack:
        def sb(name, shape, dt=F32):
            return stack.enter_context(nc.sbuf_tensor(name, shape, dt))

        def sem(name):
            return stack.enter_context(nc.semaphore(name))

        xs = sb("xs", [P, CH, D])
        ln = sb("ln", [P, CH, 2])
        cst = sb("cst", [P, C_N])
        colv = sb("colv", [P, 6])
        rowv = sb("rowv", [1, R_N])
        gate = sb("gate", [P, 5])
        tg = sb("tg", [P, 4])
        ones = sb("ones", [1, P])
        farf = sb("farf", [2, 5 * P])
        farb = sb("farb", [2, 5 * P], BF16)
        half = sb("half", [P, 4])
        stat = sb("stat", [P, 2, 4, 6])
        mv = sb("mv", [P, 2, 4, 2])
        ve = sb("ve", [P, 2, 4])

        wq_s, wk_s, wv_s, wo_s = (sb(n, [P, D]) for n in ("wq_s", "wk_s", "wv_s", "wo_s"))
        wv_eo = sb("wv_eo", [P, 2, D])
        bqs = sb("bqs", [P, 1])
        bkm = sb("bkm", [P, HG])
        row0 = sb("row0", [1, D])
        row1 = sb("row1", [1, D])
        xn = sb("xn", [P, 2, 4, D])
        cT = sb("cT", [P, 2, 4 * P])
        ctk = sb("ctk", [P, 2, 4, D])
        xT = sb("xT", [P, 2, 4 * P])
        QT = sb("QT", [P, 2, NG, 2 * P])
        Kb = sb("Kb", [P, 2, HG, 2 * P])
        Vb = sb("Vb", [P, 2, 4, NH // 2, 18])
        Pr = sb("Pr", [P, 2, NG, 512])
        PT = sb("PT", [P, NG, 512])
        mx = sb("mx", [P, NG, 8])
        rec = sb("rec", [P, NH, 2])
        att = sb("att", [P, 2 * D])
        attT = sb("attT", [P, 2 * P])

        f0g_s = sb("f0g_s", [P, E])
        f0w12_s = sb("f0w12_s", [P, E, 2 * HID])
        f0w3_s = sb("f0w3_s", [P, E, 2, D])
        sil = sb("sil", [P, 2, HID])
        act = sb("act", [P, 2, HID])
        aT = sb("aT", [P, 2, 2, P])
        xb = sb("xb", [P, 4, D])
        f0w12_h = sb("f0w12_h", [P, E, 2 * HID], F32R)
        f0w12_l = f0w12_s[:].bitcast(F32R)
        xbh = sb("xbh", [P, 2, P], F32R)
        xbl = sb("xbl", [P, 2, P], F32R)
        yb = sb("yb", [P, 4, D])
        zero = sb("zero", [P, D])
        xr = sb("xr", [P, 2, 2, D])
        upb = sb("upb", [P, P], BF16)
        onb = sb("onb", [P, P], BF16)
        chosen = sb("chosen", [P, 2, E], BF16)
        run = sb("run", [P, E])
        pos = sb("pos", [P, 2, E])
        ohp = sb("ohp", [P, 2, 2, E])
        row = sb("row", [P, 4])
        rowu = sb("rowu", [P, 2, 4], U32)
        kept_row = sb("kept_row", [P, UA, 4])
        kept_e = sb("kept_e", [P, UA, 4])
        kept_w = sb("kept_w", [P, UA, 4])
        back = sb("back", [P, UA, 4], U32)
        cnt = sb("cnt", [P, E], U32)
        cntf = sb("cntf", [P, E])
        nbf = sb("nbf", [P, E])
        trn = sb("trn", [P, E, E])
        cs = sb("cs", [P, E])
        shift = sb("shift", [P, E])
        ge = sb("ge", [P, E])
        ej = sb("ej", [P, 1])
        en = sb("en", [P, 1])
        cn = sb("cn", [P, 1])
        first_row = sb("first_row", [P, 1])
        table = sb("table", [1, 3, NB], U32)
        tail = sb("tail", [1, E], U32)
        eqd = sb("eqd", [P, 4 * UA, E])
        bkf = sb("bkf", [P, 4 * UA])
        gidx = sb("gidx", [P, 2, 8], U32)
        yg = sb("yg", [P, 2, 8, D])
        lg = sb("lg", [P, 4, E])
        top = sb("top", [P, 4, 8])
        idx = sb("idx", [P, 4, 8], U32)
        idf = sb("idf", [P, 4, 8])
        dif = sb("dif", [P, 4])
        pe2 = sb("pe2", [P, 4])
        den = sb("den", [P, 4])
        w1g = sb("w1g", [P, 4])
        w2g = sb("w2g", [P, 4])
        oh = sb("oh", [P, 2, 4, E])
        cmb = sb("cmb", [P, 2, 4, E])

        wqv_s = sb("wqv_s", [P, 4, D])
        wqv_g = sb("wqv_g", [P, 4, D])
        e3 = sb("e3", [P, 4 * P])
        rmx = sb("rmx", [P, 4])
        nmx = sb("nmx", [P, 4])
        Pc = sb("Pc", [P, 2, 4, P])
        sm = sb("sm", [P, 2, 4])
        rsm = sb("rsm", [P, 4])
        mcol = sb("mcol", [P, 4])
        bm = sb("bm", [4, 2])
        brow = sb("brow", [4, 2, L])
        bs = sb("bs", [4, 2])
        br = sb("br", [4, 2])
        wrow = sb("wrow", [4, P])
        wbd = sb("wbd", [P, 4, 2])
        hc = sb("hc", [P, 8])
        PcT = sb("PcT", [P, 4 * P])
        hqT = sb("hqT", [P, 4 * P])
        ehq = sb("ehq", [P, 4 * P])
        w1c = sb("w1c", [P, 4, 4])
        ehc = sb("ehc", [P, 2, 4 * P])

        f1g_s = sb("f1g_s", [P, E])
        f1w1_s = sb("f1w1_s", [P, E * R])
        f1w2_s = sb("f1w2_s", [P, 4, D])
        f1w1_h = sb("f1w1_h", [P, E * R], F32R)
        f1w1_l = sb("f1w1_l", [P, E * R], F32R)
        xTh = sb("xTh", [P, 2, 4 * P], F32R)
        xTl = sb("xTl", [P, 2, 4 * P], F32R)
        hg = sb("hg", [P, 2, E * R])
        hgg = sb("hgg", [P, 2, E * R])
        hT = PT[:, 0:2, :]

        ident = cst[:, C_ID:C_ID + P]
        iota = cst[:, C_IO:C_IO + E]

        bank = [stack.enter_context(nc.psum_tensor(f"bank{i}", [P, 512], F32)) for i in range(8)]

        sent = nc.dram_tensor("sent", (E * REGION + E * P, D), F32, kind="Internal").ap()
        done = nc.dram_tensor("done", (NB * P, D), F32, kind="Internal").ap()

        ld_x = [sem(f"ld_x{i}") for i in range(4)]
        ld_small, ld_attn, ld_f0g, ld_f0, ld_c, ld_f1 = (
            sem(n) for n in ("ld_small", "ld_attn", "ld_f0g", "ld_f0", "ld_c", "ld_f1"))
        ld_cT = [sem(f"ld_cT{i}") for i in range(2)]
        ld_cC = [sem(f"ld_cC{i}") for i in range(2)]
        sent_s = [sem(f"sent{i}") for i in range(2)]
        zeroed = sem("zeroed")
        ld_b = [sem(f"ld_b{i}") for i in range(4)]
        st_b = [sem(f"st_b{i}") for i in range(4)]
        back_s = [sem(f"back{i}") for i in range(2)]
        fill, prep, prep_pe, prep_act, prep_b0 = (
            sem(n) for n in ("fill", "prep", "prep_pe", "prep_act", "prep_b0"))
        names = {}

        def S(name):
            if name not in names:
                names[name] = sem(name)
            return names[name]

        START_AT_ONE = {
            "vector": ("a_x", "a_nrm", "c_x", "c_sum", "d_hgg", "d_x", "mv0", "mv1", "mv2", "mv3"),
            "scalar": ("a_pts", "d_gelu", "d_hts"),
            "tensor": ("a_pv", "d_ht", "d_y"),
            "gpsimd": ("ln0", "ln1", "ln2", "ln3"),
        }

        def start_at_one(eng, which):
            for name in START_AT_ONE[which]:
                eng.sem_inc(S(name), 1)

        block = stack.enter_context(nc.Block())
        x_v = x.rearrange("(t p) c -> p t c", p=P)
        out_v = out.rearrange("(t p) c -> p t c", p=P)
        ctx_v = ctx_tok.rearrange("(t p) c -> p t c", p=P)

        def wait_alone(eng, semaphore, value):
            if not isinstance(value, int):
                eng.compute_val(value)
            eng.wait_ge(ld_small, 80)
            eng.wait_ge(semaphore, value)

        def skewed(eng, units, first, ahead, body):
            turns = (units - first - ahead) // 2
            with eng.Fori(0, turns) as i:
                for s in range(2):
                    body(i * 2 + (first + s), s, ahead)
            for u in range(first + 2 * turns, units):
                body(u, (u - first) % 2, units - 1 - u)

        def has(u, units=UA):
            return not isinstance(u, int) or 0 <= u < units

        def pipelined(eng, it, first, loop, behind, end):
            for u in range(first, loop):
                it(u, u % 2)
            with eng.Fori(0, (behind - loop) // 2) as i:
                for k in range(2):
                    it(i * 2 + (loop + k), (loop + k) % 2)
            for u in range(behind, end):
                it(u, u % 2)

        def wait(eng, semaphore, value):
            if not isinstance(value, int) or value > 0:
                eng.wait_ge(semaphore, value)

        def blocks(eng, step, turn=lambda t, n: None):
            turn(0, TURN)
            for t in range(TURN):
                step(t, t, t, 4)
            with eng.Fori(0, NB // TURN - 1) as i:
                turn(i * TURN + (TURN - 3), PACK)
                for q in range(TURN):
                    step(i * TURN + (TURN + q), q, 8, 4)
            turn(NB - 3, 3)
            for t in range(NB, NB + 3):
                step(t, t % TURN, 8, NB - 1 - t)

        @block.sync
        def _(sp):
            sp.dma_start(cst[:], consts).then_inc(ld_small, 16)
            sp.dma_start(colv[:], cols).then_inc(ld_small, 16)
            sp.dma_start(rowv[:], rows).then_inc(ld_small, 16)
            sp.dma_start(gate[:], gates.partition_broadcast(P)).then_inc(ld_small, 16)
            sp.dma_start(farf[:], far).then_inc(ld_small, 16)
            for i in range(4):
                sp.dma_start(xs[:, 8 * i:8 * i + 8, :], x_v[:, 8 * i:8 * i + 8, :]).then_inc(ld_x[i], 16)
                if i == 0:
                    for s in range(2):
                        sp.dma_start(cT[:, s, 0:2 * P], ctx_t[:, 2 * P * s:2 * P * (s + 1)]).then_inc(ld_cT[s], 16)
            sp.dma_start(f0w12_s[:], f0_w12).then_inc(ld_f0, 16)
            sp.dma_start(f0w3_s[:], f0_w3).then_inc(ld_f0, 16)
            sp.dma_start(wqv_s[:], wqv).then_inc(ld_c, 16)
            sp.dma_start(f1g_s[:], f1_wg).then_inc(ld_f1, 16)
            sp.dma_start(f1w1_s[:], f1_w1).then_inc(ld_f1, 16)
            sp.dma_start(f1w2_s[:], f1_w2).then_inc(ld_f1, 16)
            with sp.Fori(0, UA // 2 - 1) as i:
                u = i * 2
                for s in range(2):
                    sp.wait_ge(S("a_v"), u + (s + 1))
                    sp.dma_start(cT[:, s, 0:2 * P], ctx_t[:, bass.ds((u + (s + 2)) * (2 * P), 2 * P)]).then_inc(ld_cT[s], 16)
            sp.wait_ge(fill, 11)
            for e in range(E):
                sp.dma_start(sent[E * REGION + P * e:E * REGION + P * (e + 1), :], zero[:]).then_inc(zeroed, 16)
            sp.wait_ge(S("tail"), 1)
            for e in range(E):
                r = sp.value_load(tail[0:1, e:e + 1], min_val=e * REGION, max_val=e * REGION + TOKENS)
                sp.dma_start(sent[bass.ds(r, P), :], zero[:]).then_inc(zeroed, 16)
            sp.wait_ge(zeroed, 32 * E)
            sp.wait_ge(S("table"), 2)
            for i in range(2):
                sp.wait_ge(sent_s[i], 64 * UA // 2)

            def b_load(t, k):
                r = sp.value_load(table[0:1, 1, bass.ds(t, 1)], min_val=0, max_val=E * REGION + (E - 1) * P)
                sp.dma_start(xb[:, k, :], sent[bass.ds(r, P), :]).then_inc(ld_b[k], 16)

            for t in range(4):
                b_load(t, t)
            with sp.Fori(0, NB // 4 - 1) as i:
                for k in range(4):
                    sp.wait_ge(S("b_xt"), i * 4 + (k + 1))
                    b_load(i * 4 + (k + 4), k)
            sp.wait_ge(S("a_v"), UA)
            for s in range(2):
                sp.dma_start(cT[:, s, :], ctx_t[:, 4 * P * s:4 * P * (s + 1)]).then_inc(ld_cC[s], 16)
                sp.dma_start(ctk[:, s], ctx_v[:, 4 * s:4 * s + 4, :]).then_inc(ld_cC[s], 16)
            with sp.Fori(0, U4 // 2 - 1) as i:
                u = i * 2
                for s in range(2):
                    sp.wait_ge(S("c_hq"), u + (s + 1))
                    sp.dma_start(cT[:, s, :], ctx_t[:, bass.ds((u + (s + 2)) * (4 * P), 4 * P)]).then_inc(ld_cC[s], 16)
                    sp.dma_start(ctk[:, s], ctx_v[:, bass.ds((u + (s + 2)) * 4, 4), :]).then_inc(ld_cC[s], 16)
            with sp.Fori(0, U4, 1) as u:
                sp.wait_ge(S("d_x"), 1 + u * 4 + 4)
                sp.dma_start(out_v[:, bass.ds(u * 4, 4), :], xs[:, bass.ds(u * 4, 4), :]).then_inc(S("stored"), 16)
            sp.wait_ge(S("stored"), 16 * U4)

        @block.gpsimd
        def _(pool):
            start_at_one(pool, "gpsimd")
            for c, value in enumerate((EPS, 1.0, -0.5, float(np.e))):
                nc.gpsimd.memset(half[:, c:c + 1], value).then_inc(fill, 1)
            nc.gpsimd.memset(ones[:], 1.0).then_inc(fill, 1)
            nc.gpsimd.memset(wv_eo[:], 0.0).then_inc(fill, 1)
            nc.gpsimd.memset(zero[:], 0.0).then_inc(fill, 1)
            nc.gpsimd.memset(onb[:], 1.0).then_inc(fill, 1)
            nc.gpsimd.memset(chosen[:], 0.0).then_inc(fill, 1)
            nc.gpsimd.memset(QT[:], 0.0).then_inc(fill, 1)
            nc.gpsimd.memset(w1c[:], 0.0).then_inc(fill, 1)
            pool.dma_start(f0g_s[:], f0_wg).then_inc(ld_f0g, 16)
            pool.wait_ge(fill, 11)

            def rstd(k, u, n):
                pool.wait_ge(S(f"mv{k}"), 1 + u * n + n)
                h = k % 2
                nc.gpsimd.tensor_tensor(ve[:, h, 0:n], mv[:, h, 0:n, 1], half[:, 0:1].to_broadcast([P, n]), ALU.add).then_inc(S(f"ve{k // 3}"), 1)
                pool.wait_ge(S(f"ve{k // 3}"), stats_units[k] + u + 1)
                nc.gpsimd.tensor_copy(ln[:, bass.ds(u * n, n), 0], mv[:, h, 0:n, 0])
                nc.gpsimd.tensor_tensor(ln[:, bass.ds(u * n, n), 1], ve[:, h, 0:n], half[:, 2:3].to_broadcast([P, n]), ALU.pow).then_inc(S(f"ln{k}"), 1)

            def second_weight(k, u, n):
                pool.wait_ge(S("dif"), gated[k] + u + 1)
                nc.gpsimd.tensor_tensor(pe2[:, 0:n], half[:, 3:4].to_broadcast([P, n]), dif[:, 0:n], ALU.pow).then_inc(S("second"), 1)

            def send(u, s):
                wait_alone(pool, S("r_row"), u + 1)
                for k in range(2):
                    for c in range(2):
                        nc.gpsimd.indirect_dma_start(sent, bass.IndirectOffsetOnAxis(ap=rowu[:, s, 2 * k + c:2 * k + c + 1], axis=0),
                                                     xr[:, s, c, :], None).then_inc(sent_s[s], 16)

            def fetch(u, s, columns=range(8)):
                if columns[0] == 0:
                    if not isinstance(u, int) or u >= 2:
                        wait_alone(pool, S("c_sum"), u * 2 - 1)
                    nc.gpsimd.tensor_copy(gidx[:, s, :].rearrange("p (a j) -> p a j", a=2), back[:, bass.ds(u * 2, 2), :]).then_inc(S("c_idx"), 1)
                    wait_alone(pool, S("c_idx"), u + 1)
                for j in columns:
                    nc.gpsimd.indirect_dma_start(yg[:, s, j, :], None, done,
                                                 bass.IndirectOffsetOnAxis(ap=gidx[:, s, j:j + 1], axis=0)).then_inc(back_s[s], 16)

            with pool.Fori(0, U4) as u:
                rstd(0, u, 4)
            rstd(1, 0, 2)

            def body_a(u, s, left):
                if left:
                    rstd(1, u + 1, 2)
                second_weight(1, u, 2)
                send(u, s)

            skewed(pool, UA, 0, 2, body_a)
            pool.wait_ge(S("back"), 1)
            with pool.Fori(0, NB // 4) as i:
                for k in range(4):
                    pool.wait_ge(S("b_ys"), i * 4 + (k + 1))
                    pool.dma_start(done[bass.ds(i * (4 * P) + k * P, P), :], yb[:, k, :]).then_inc(st_b[k], 16)
            for k in range(4):
                pool.wait_ge(st_b[k], 16 * (NB // 4))

            def it_c(u, s):
                if isinstance(u, int) and u == -3:
                    fetch(u + 4, s, range(5))
                    rstd(2, u + 3, 4)
                    fetch(u + 4, s, range(5, 8))
                    return
                if has(u + 4, U4):
                    fetch(u + 4, s)
                if has(u - 1, U4):
                    rstd(3, u - 1, 4)
                if has(u + 3, U4):
                    rstd(2, u + 3, 4)

            pipelined(pool, it_c, -4, 1, U4 - 5, U4 + 1)

            def it_d(u, s, left):
                pool.wait_ge(S("d_xhs"), u + 1)
                nc.gpsimd.tensor_tensor(xTl[:, s, :], xT[:, s, :], xTh[:, s, :], ALU.subtract).then_inc(S("d_xls"), 1)
                second_weight(3, u, 4)

            skewed(pool, U4, 0, 2, it_d)

        @block.scalar
        def _(a):
            start_at_one(a, "scalar")
            for w_s, w in ((wq_s, wq), (wk_s, wk), (wv_s, wv), (wo_s, wo)):
                a.dma_start(w_s[:], w).then_inc(ld_attn, 16)
            a.wait_ge(ld_small, 80)
            nc.scalar.activation(tg[:], gate[:, 0:4], ACT.Tanh).then_inc(prep_act, 1)
            nc.scalar.activation(bqs[:], colv[:, BQ:BQ + 1], ACT.Copy, scale=float(DH) ** -0.5).then_inc(prep_act, 1)

            def a_xts(u):
                a.wait_ge(S("a_xt"), u + 1)
                nc.scalar.activation(xT[:, 0, 0:2 * P], bank[4][:, 0:2 * P], ACT.Copy).then_inc(S("a_xts"), 1)

            def a_qks(u, s):
                a.wait_ge(S("a_qk"), u + 1)
                for g in range(NG):
                    rows_g = slice(32 * g, 32 * (g + 1))
                    nc.scalar.activation(QT[rows_g, s, g, :], bank[4][rows_g, 0:2 * P], ACT.Identity, bias=bqs[rows_g], scale=float(DH) ** -0.5)
                for j in range(HG):
                    last = nc.scalar.activation(Kb[:, s, j, :], bank[4][:, 2 * P:4 * P], ACT.Identity,
                                                bias=bkm[:, j:j + 1], scale=cst[:, C_KM + j:C_KM + j + 1])
                last.then_inc(S("a_qks"), 1)

            def a_exp(u, s, g):
                a.wait_ge(S("a_sub"), u * 4 + (g + 1))
                nc.scalar.activation(Pr[:, s, g, :], Pr[:, s, g, :], ACT.Exp).then_inc(S("a_exp"), 1)

            def a_pts(u, g):
                a.wait_ge(S("a_pt"), u * 4 + (g + 1))
                if g == 0:
                    a.wait_ge(S("a_pv"), 1 + u)
                nc.scalar.activation(PT[:, g, :], bank[6 + g % 2][:], ACT.Copy).then_inc(S("a_pts"), 1)

            def a_ats(u):
                a.wait_ge(S("a_at"), u + 1)
                nc.scalar.activation(attT[:], bank[2][:, 0:2 * P], ACT.Copy).then_inc(S("a_ats"), 1)

            a.wait_ge(prep, 3)
            a.wait_ge(fill, 11)
            def r_xts(v):
                a.wait_ge(S("r_xt"), v + 1)
                nc.scalar.activation(xT[:, 1, 0:2 * P], bank[3][:, 0:2 * P], ACT.Copy).then_inc(S("r_xts"), 1)

            def it_a(u, s):
                if isinstance(u, int) and 0 <= u - (UA - 3) < 4:
                    a.wait_ge(ld_f0, 32)
                    for e in range(2 * (u - (UA - 3)), 2 * (u - (UA - 3)) + 2):
                        nc.scalar.activation(f0w12_h[:, e, :], f0w12_s[:, e, :], ACT.Copy).then_inc(S("w12_h"), 1)
                if has(u):
                    a_pts(u, 0)
                    a_pts(u, 1)
                if has(u - 1):
                    a_ats(u - 1)
                if has(u + 2):
                    a_xts(u + 2)
                if has(u - 2):
                    r_xts(u - 2)
                if has(u):
                    a_pts(u, 2)
                    a_pts(u, 3)
                if has(u + 1):
                    for g in range(NG):
                        a_exp(u + 1, 1 - s, g)
                if has(u + 2):
                    a_qks(u + 2, s)

            pipelined(a, it_a, -3, 3, UA - 3, UA + 3)
            a.wait_ge(ld_f1, 48)
            nc.scalar.activation(f1w1_h[:], f1w1_s[:], ACT.Copy).then_inc(S("w1_h"), 1)

            def b_step(t, q, first, last):
                k = q % 2
                if last >= 0:
                    a.wait_ge(S("b_xt"), t + 1)
                    nc.scalar.activation(xbh[:, k, :], bank[k][:, 0:P], ACT.Copy).then_inc(S("b_xts"), 1)
                if first >= 1 and last >= -1:
                    a.wait_ge(S("b_hg"), t)
                    if first >= 3:
                        a.wait_ge(S("b_act"), t - 2)
                    nc.scalar.activation(sil[:, 1 - k, :], bank[3 - k][:, 0:HID], ACT.Silu).then_inc(S("b_sil"), 1)
                if first >= 2 and last >= -2:
                    a.wait_ge(S("b_at"), t - 1)
                    if first >= 4:
                        a.wait_ge(S("b_y"), t - 3)
                    nc.scalar.activation(aT[:, k], bank[4 + k][:, 0:2 * P].rearrange("p (j n) -> p j n", n=P), ACT.Copy).then_inc(S("b_ats"), 1)

            blocks(a, b_step)

            def c_xts(u, s):
                wait(a, S("c_y"), u - 1)
                nc.scalar.activation(xT[:, s, :], bank[0][:], ACT.Copy).then_inc(S("c_xts"), 1)

            def c_e3(u):
                a.wait_ge(S("c_xt"), u + 1)
                nc.scalar.activation(e3[:], bank[0][:], ACT.Identity, bias=colv[:, W2S:W2S + 1],
                                     scale=colv[:, W3S:W3S + 1]).then_inc(S("c_e3"), 1)

            def c_exp(u, s):
                a.wait_ge(S("c_nmx"), u + 1)
                for k in range(4):
                    last = nc.scalar.activation(Pc[:, s, k, :], bank[1][:, P * k:P * (k + 1)], ACT.Exp,
                                                bias=nmx[:, k:k + 1], accum_out=sm[:, s, k:k + 1])
                last.then_inc(S("c_exp"), 1)

            def c_nrm(u, s):
                a.wait_ge(S("c_rsm"), u + 1)
                for k in range(4):
                    last = nc.scalar.activation(Pc[:, s, k, :], Pc[:, s, k, :], ACT.Copy, scale=rsm[:, k:k + 1])
                last.then_inc(S("c_nrm"), 1)

            def c_bexp(u):
                a.wait_ge(S("c_bsub"), u + 1)
                nc.scalar.activation(brow[:], brow[:], ACT.Exp).then_inc(S("c_bexp"), 1)

            def c_pts(u):
                a.wait_ge(S("c_pt"), u + 1)
                nc.scalar.activation(PcT[:], bank[3][:], ACT.Copy).then_inc(S("c_pts"), 1)

            def c_hqs(u):
                a.wait_ge(S("c_hq"), u + 1)
                nc.scalar.activation(hqT[:], bank[4][:], ACT.Copy).then_inc(S("c_hqs"), 1)

            def it_c(u, s):
                if has(u + 1, U4):
                    c_xts(u + 1, 1 - s)
                if has(u, U4):
                    c_hqs(u)
                if has(u + 1, U4):
                    c_exp(u + 1, 1 - s)
                if has(u + 2, U4):
                    c_e3(u + 2)
                if has(u + 1, U4):
                    c_nrm(u + 1, 1 - s)
                    c_bexp(u + 1)
                    c_pts(u + 1)

            pipelined(a, it_c, -3, 1, U4 - 3, U4 + 1)

            def d_xts(u, s):
                a.wait_ge(S("d_xt"), u + 1)
                nc.scalar.activation(xT[:, s, :], bank[0][:], ACT.Copy).then_inc(S("d_xts"), 1)
                nc.scalar.activation(xTh[:, s, :], bank[0][:], ACT.Copy).then_inc(S("d_xhs"), 1)

            def d_gelu(u, k):
                a.wait_ge(S("d_h"), u * 4 + (k + 1))
                wait(a, S("d_hgg"), u * 4 + k)
                nc.scalar.activation(hg[:, k % 2, :], bank[1 + k % 2][:], ACT.Gelu).then_inc(S("d_gelu"), 1)

            def d_hts(u, k):
                a.wait_ge(S("d_ht"), 1 + u * 4 + (k + 1))
                wait(a, S("d_y"), u * 4 + k)
                nc.scalar.activation(hT[:, k % 2, :], bank[3 + k % 2][:], ACT.Copy).then_inc(S("d_hts"), 1)

            def it_d(u, s):
                this, nxt = has(u, U4), has(u + 1, U4)
                if nxt:
                    d_xts(u + 1, 1 - s)
                for k in range(4):
                    if has(u + k // 2, U4):
                        d_gelu(u + k // 2, (k + 2) % 4)
                    if this:
                        d_hts(u, k)

            pipelined(a, it_d, -2, 1, U4 - 3, U4 + 1)

        @block.vector
        def _(v):
            start_at_one(v, "vector")
            v.wait_ge(ld_small, 80)
            v.wait_ge(prep_act, 2)
            nc.vector.tensor_scalar(bkm[:], cst[:, C_KM:C_KM + HG], colv[:, BK:BK + 1], None, ALU.mult).then_inc(prep, 1)
            nc.vector.tensor_scalar(row1[:], rowv[:, R_BQV:R_BQV + D], tg[0:1, 1:2], None, ALU.mult).then_inc(prep, 1)
            for s in range(2):
                last = nc.vector.tensor_copy(Vb[:, s, :, :, 16:18],
                                             cst[:, C_VM:C_VM + 2].unsqueeze(1).unsqueeze(1).to_broadcast([P, 4, NH // 2, 2]))
            last.then_inc(prep, 1)
            nc.vector.tensor_copy(farb[:], farf[:]).then_inc(prep, 1)
            nc.vector.tensor_copy(upb[:], cst[:, C_UP:C_UP + P]).then_inc(S("r_prep"), 1)
            nc.vector.tensor_copy(run[:], cst[:, C_RG:C_RG + E]).then_inc(S("r_run"), 1)
            v.wait_ge(ld_attn, 64)
            v.wait_ge(fill, 11)
            nc.vector.tensor_scalar(wo_s[:], wo_s[:], tg[:, 0:1], None, ALU.mult).then_inc(prep, 1)
            nc.vector.tensor_scalar(rowv[:, R_BO:R_BO + D], rowv[:, R_BO:R_BO + D], tg[0:1, 0:1], None, ALU.mult).then_inc(prep, 1)
            for e in range(2):
                last = nc.vector.tensor_copy(wv_eo[:, e, :].rearrange("p (h e d) -> p h e d", e=2, d=DH)[:, :, e, :],
                                             wv_s[:].rearrange("p (h e d) -> p h e d", e=2, d=DH)[:, :, e, :])
            last.then_inc(prep, 1)
            nc.vector.tensor_copy(w1c[:].rearrange("p c m -> p (c m)")[:, 0:16:5], colv[:, W1S:W1S + 1].to_broadcast([P, 4])).then_inc(prep, 1)
            v.wait_ge(prep_pe, 1)
            nc.vector.tensor_copy(row0[:], bank[7][0:1, 0:D]).then_inc(prep_b0, 1)

            def sums(k, u, n):
                wait_alone(v, S(f"mv{k}"), 1 + u * n)
                if k:
                    wait_alone(v, S(WRITTEN[k]), 1 + (u + 1) * WRITES[k])
                for c in range(n):
                    nc.vector.bn_stats(stat[:, k % 2, c, :], xs[:, u * n + c, :]).then_inc(S(f"bn{k // 3}"), 1)

            def moments(k, u, n):
                wait_alone(v, S(f"ln{k}"), 1 + u)
                wait_alone(v, S(f"bn{k // 3}"), CH * (k % 3) + u * n + n)
                for c in range(n):
                    nc.vector.bn_aggr(mv[:, k % 2, c, :], stat[:, k % 2, c, :]).then_inc(S(f"mv{k}"), 1)

            def stats(k, u, n):
                sums(k, u, n)
                moments(k, u, n)

            def norm(u, n, dst, signal, k=0):
                if k:
                    v.wait_ge(S(f"ln{k}"), 2 + u)
                for c in range(n):
                    last = nc.vector.tensor_scalar(dst[:, c, :], xs[:, u * n + c, :], ln[:, u * n + c, 0:1],
                                                   ln[:, u * n + c, 1:2], ALU.subtract, ALU.mult)
                last.then_inc(S(signal), 1)

            def first_stats(u):
                v.wait_ge(ld_x[u // 2], 16)
                stats(0, u, 4)

            first_stats(0)

            def a_vs(u, s):
                v.wait_ge(S("a_v"), u + 1)
                nc.vector.tensor_copy(Vb[:, s, :, :, 0:16],
                                      bank[5][:].rearrange("p (b h d) -> p b h d", b=4, d=16)).then_inc(S("a_vs"), 1)

            def scores(g):
                return bank[g % 2][:].rearrange("p (m k) -> p m k", k=L)

            def a_max(u, g):
                v.wait_ge(S("a_s"), u * 4 + (g + 1))
                nc.vector.tensor_reduce(mx[:, g, :], scores(g), AX, ALU.max).then_inc(S("a_max"), 1)

            def a_sub(u, s, g):
                v.wait_ge(S("a_max"), u * 4 + (g + 1))
                nc.vector.tensor_tensor(Pr[:, s, g, :].rearrange("p (m k) -> p m k", k=L), scores(g),
                                        mx[:, g, :].unsqueeze(2).to_broadcast([P, 8, L]), ALU.subtract).then_inc(S("a_sub"), 1)

            def a_rec(u):
                v.wait_ge(S("a_pv"), 1 + u + 1)
                nc.vector.reciprocal(rec[:], bank[5][:, 0:NH * 18].rearrange("p (m c) -> p m c", c=18)[:, :, 16:18]).then_inc(S("a_rec"), 1)

            def a_nrm(u):
                v.wait_ge(S("a_rec"), u + 1)
                o = bank[5][:, 0:NH * 18].rearrange("p (m c) -> p m c", c=18)
                nc.vector.tensor_tensor(att[:].rearrange("p (m e d) -> p m e d", e=2, d=DH),
                                        o[:, :, 0:16].rearrange("p m (e d) -> p m e d", e=2),
                                        rec[:].unsqueeze(3).to_broadcast([P, NH, 2, DH]), ALU.mult).then_inc(S("a_nrm"), 1)

            def a_x(u):
                v.wait_ge(S("a_y"), u + 1)
                xu = xs[:, bass.ds(u * 2, 2), :] if not isinstance(u, int) else xs[:, 2 * u:2 * u + 2, :]
                nc.vector.tensor_tensor(xu, bank[2][:, 2 * P:4 * P].rearrange("p (c d) -> p c d", d=D), xu, ALU.add).then_inc(S("a_x"), 1)


            def logits(k, u, n, scores):
                v.wait_ge(S("lgp"), gated[k] + u + 1)
                nc.vector.tensor_copy(lg[:, 0:n, :], scores).then_inc(S("lgs"), 1)

            def largest(k, u, n):
                wait_alone(v, S("lgs"), gated[k] + u + 1)
                for c in range(n):
                    nc.vector.max(top[:, c, :], lg[:, c, :]).then_inc(S("top"), 1)

            def experts(k, u, n):
                v.wait_ge(S("top"), gated[k] * 2 + u * n + n)
                nc.vector.tensor_tensor(dif[:, 0:n], top[:, 0:n, 1], top[:, 0:n, 0], ALU.subtract).then_inc(S("dif"), 1)
                for c in range(n):
                    nc.vector.max_index(idx[:, c, :], top[:, c, :], lg[:, c, :]).then_inc(S("idx"), 1)

            def as_float(k, u, n):
                v.wait_ge(S("idx"), gated[k] * 2 + u * n + n)
                nc.vector.tensor_copy(idf[:, 0:n, :], idx[:, 0:n, :]).then_inc(S("idf"), 1)

            def one_hot(k, u, n):
                v.wait_ge(S("idf"), gated[k] + u + 1)
                for h in range(2):
                    nc.vector.tensor_tensor(oh[:, h, 0:n, :], iota.unsqueeze(1).to_broadcast([P, n, E]),
                                            idf[:, 0:n, h:h + 1].to_broadcast([P, n, E]), ALU.is_equal).then_inc(S("oh"), 1)

            def denominator(k, u, n):
                v.wait_ge(S("second"), gated[k] + u + 1)
                nc.vector.tensor_scalar(den[:, 0:n], pe2[:, 0:n], 1.0, None, ALU.add).then_inc(S("den"), 1)

            def inverse(k, u, n):
                v.wait_ge(S("den"), gated[k] * 2 + u * 2 + 1)
                nc.vector.reciprocal(den[:, 0:n], den[:, 0:n]).then_inc(S("den"), 1)

            def first_weight(k, u, n, g, factor, w1):
                v.wait_ge(S("den"), gated[k] * 2 + u * 2 + 2)
                nc.vector.tensor_scalar(w1, den[:, 0:n], tg[:, g:g + 1], factor, ALU.mult, ALU.mult).then_inc(S("w"), 1)

            def second_weight(k, u, n, w1, w2):
                v.wait_ge(S("w"), gated[k] * 2 + u * 2 + 1)
                nc.vector.tensor_tensor(w2, w1, pe2[:, 0:n], ALU.mult).then_inc(S("w"), 1)

            def r_ln(w, s):
                if not isinstance(w, int) or w >= 2:
                    v.wait_ge(sent_s[s], (w - s) * 32)
                norm(w, 2, xr[:, s], "r_ln", 1)

            def r_mask(w):
                v.wait_ge(S("oh"), w * 2 + 2)
                nc.vector.tensor_tensor(chosen[:], oh[:, 0, 0:2, :], oh[:, 1, 0:2, :], ALU.add).then_inc(S("r_m"), 1)

            def r_pos(w):
                v.wait_ge(S("r_rank"), w + 1)
                v.wait_ge(S("r_run"), w + 1)
                nc.vector.tensor_tensor(pos[:], bank[3][:, RK:RK + 2 * E].rearrange("p (c e) -> p c e", e=E),
                                        run[:].unsqueeze(1).to_broadcast([P, 2, E]), ALU.add).then_inc(S("r_pos"), 1)

            def r_own(w):
                v.wait_ge(S("r_pos"), w + 1)
                nc.vector.tensor_tensor(ohp[:], oh[:, :, 0:2, :], pos[:].unsqueeze(1).to_broadcast([P, 2, 2, E]), ALU.mult).then_inc(S("r_ohp"), 1)
                nc.vector.tensor_tensor(run[:], bank[3][:, RK + 2 * E:RK + 3 * E], run[:], ALU.add).then_inc(S("r_run"), 1)

            def r_sum(w):
                v.wait_ge(S("r_ohp"), w + 1)
                nc.vector.tensor_reduce(row[:], ohp[:].rearrange("p k c e -> p (k c) e"), AX, ALU.add).then_inc(S("r_red"), 1)

            def r_keep(w, s):
                v.wait_ge(S("r_red"), w + 1)
                nc.vector.tensor_copy(rowu[:, s, :], row[:]).then_inc(S("r_row"), 1)
                nc.vector.tensor_copy(kept_row[:, bass.ds(w, 1), :], row[:].unsqueeze(1)).then_inc(S("r_kept"), 1)
                nc.vector.tensor_copy(kept_e[:, bass.ds(w, 1), :].rearrange("p a (k c) -> p a k c", k=2),
                                      idf[:, 0:2, 0:2].rearrange("p c k -> p k c").unsqueeze(1)).then_inc(S("r_kept"), 1)

            def kept_weight(w, k):
                return kept_w[:, bass.ds(w, 1), 2 * k:2 * k + 2].rearrange("p a c -> p (a c)")

            def it_a(u, s):
                if has(u + 3):
                    wait(v, S("a_xt"), u + 2)
                    if isinstance(u, int):
                        v.wait_ge(S("ln0"), 2 + (u + 3) // 2 if u + 3 < 4 else 1 + U4)
                    norm(u + 3, 2, xn[:, 1 - s], "a_ln")
                if isinstance(u, int) and u + 3 < 4:
                    for group in ((1, 2), (3, 4), (5, 6), (7,))[u + 3]:
                        first_stats(group)
                if has(u - 3):
                    r_pos(u - 3)
                if has(u - 2):
                    r_ln(u - 2, s)
                if has(u - 3):
                    r_own(u - 3)
                if has(u):
                    a_vs(u, s)
                if has(u - 3):
                    r_sum(u - 3)
                if has(u + 1):
                    a_max(u + 1, 0)
                if has(u - 3):
                    r_keep(u - 3, 1 - s)
                if has(u + 1):
                    a_sub(u + 1, 1 - s, 0)
                if has(u - 3):
                    denominator(1, u - 3, 2)
                if has(u + 1):
                    a_max(u + 1, 1)
                if has(u - 3):
                    inverse(1, u - 3, 2)
                if has(u + 1):
                    a_sub(u + 1, 1 - s, 1)
                if has(u - 3):
                    first_weight(1, u - 3, 2, 2, 1.0, kept_weight(u - 3, 0))
                if has(u + 1):
                    a_max(u + 1, 2)
                if has(u - 3):
                    second_weight(1, u - 3, 2, kept_weight(u - 3, 0), kept_weight(u - 3, 1))
                if has(u + 1):
                    a_sub(u + 1, 1 - s, 2)
                if has(u - 1):
                    a_x(u - 1)
                if has(u - 2):
                    logits(1, u - 2, 2, bank[3][:, 2 * P:2 * P + 2 * E].rearrange("p (c e) -> p c e", e=E))
                if has(u - 1):
                    sums(1, u - 1, 2)
                if has(u - 2):
                    largest(1, u - 2, 2)
                if has(u + 1):
                    a_max(u + 1, 3)
                if has(u - 2):
                    experts(1, u - 2, 2)
                if has(u - 1):
                    moments(1, u - 1, 2)
                if has(u + 1):
                    a_sub(u + 1, 1 - s, 3)
                if has(u - 2):
                    as_float(1, u - 2, 2)
                    one_hot(1, u - 2, 2)
                    r_mask(u - 2)
                if isinstance(u, int) and 0 <= u - (UA - 3) < 4:
                    for e in range(2 * (u - (UA - 3)), 2 * (u - (UA - 3)) + 2):
                        v.wait_ge(S("w12_h"), e + 1)
                        nc.vector.tensor_tensor(f0w12_l[:, e, :], f0w12_s[:, e, :], f0w12_h[:, e, :], ALU.subtract).then_inc(S("w12_l"), 1)
                if has(u):
                    a_rec(u)
                    a_nrm(u)

            pipelined(v, it_a, -3, 3, UA - 3, UA + 3)

            n_table = [0]

            def then(ins):
                n_table[0] += 1
                ins.then_inc(S("steps"), 1)
                v.wait_ge(S("steps"), n_table[0])

            v.wait_ge(S("r_run"), UA + 1)
            nc.vector.tensor_copy(tail[:], run[0:1, :]).then_inc(S("tail"), 1)
            then(nc.vector.tensor_tensor(cntf[:], run[:], cst[:, C_RG:C_RG + E], ALU.subtract))
            then(nc.vector.tensor_scalar(cnt[:], cntf[:], float(P - 1), None, ALU.add))
            then(nc.vector.tensor_scalar(cnt[:], cnt[:], 7, None, ALU.logical_shift_right))
            then(nc.vector.tensor_copy(nbf[:], cnt[:]))
            then(nc.vector.tensor_tensor(trn[:], nbf[:].unsqueeze(1).to_broadcast([P, E, E]),
                                         cst[:, C_TR:C_TR + E * E].rearrange("p (e f) -> p e f", f=E), ALU.mult))
            then(nc.vector.tensor_reduce(cs[:], trn[:], AX, ALU.add))
            then(nc.vector.tensor_tensor(ge[:], cst[:, C_P:C_P + 1].to_broadcast([P, E]), cs[:], ALU.is_ge))
            then(nc.vector.tensor_reduce(ej[:], ge[:], AX, ALU.add))
            nc.vector.tensor_scalar(en[:], ej[:], float(E - 1), None, ALU.min).then_inc(S("t_col"), 1)
            then(nc.vector.tensor_tensor(ge[:], ge[:], nbf[:], ALU.mult))
            then(nc.vector.tensor_reduce(cn[:], ge[:], AX, ALU.add))
            then(nc.vector.scalar_tensor_tensor(cn[:], cn[:], -float(P), cst[:, C_P + 1:C_P + 2], ALU.mult, ALU.add))
            nc.vector.scalar_tensor_tensor(first_row[:], ej[:], float(REGION), cn[:], ALU.mult, ALU.add).then_inc(S("t_col"), 1)
            v.wait_ge(S("t_row"), 1)
            then(nc.vector.tensor_copy(table[:].rearrange("p k j -> p (k j)"), bank[0][0:1, 0:3 * NB]))
            then(nc.vector.tensor_scalar(table[:, 2, :], table[:, 2, :], 3 * PACK // 2, None, ALU.logical_shift_left))
            nc.vector.tensor_tensor(table[:, 0, :], table[:, 0, :], table[:, 2, :], ALU.bitwise_or).then_inc(S("table"), 2)
            then(nc.vector.tensor_tensor(cs[:], cs[:], nbf[:], ALU.subtract))
            then(nc.vector.scalar_tensor_tensor(shift[:], cs[:], float(P), cst[:, C_RG:C_RG + E], ALU.mult, ALU.subtract))
            v.wait_ge(S("r_kept"), 2 * UA)
            then(nc.vector.tensor_tensor(eqd[:], kept_e[:].rearrange("p a j -> p (a j)").unsqueeze(2).to_broadcast([P, 4 * UA, E]),
                                         iota.unsqueeze(1).to_broadcast([P, 4 * UA, E]), ALU.is_equal))
            then(nc.vector.tensor_tensor(eqd[:], eqd[:], shift[:].unsqueeze(1).to_broadcast([P, 4 * UA, E]), ALU.mult))
            then(nc.vector.tensor_reduce(bkf[:], eqd[:], AX, ALU.add))
            nc.vector.tensor_tensor(back[:].rearrange("p a j -> p (a j)"), kept_row[:].rearrange("p a j -> p (a j)"),
                                    bkf[:], ALU.add).then_inc(S("back"), 1)

            def b_step(t, q, first, last):
                k = q % 2
                if last >= 0:
                    v.wait_ge(S("b_xts"), t + 1)
                    nc.vector.tensor_tensor(xbl[:, k, :], bank[k][:, 0:P], xbh[:, k, :], ALU.subtract).then_inc(S("b_xls"), 1)
                if first >= 1 and last >= -1:
                    v.wait_ge(S("b_sil"), t)
                    if first >= 3:
                        v.wait_ge(S("b_at"), t - 2)
                    nc.vector.tensor_tensor(act[:, 1 - k, :], sil[:, 1 - k, :], bank[3 - k][:, HID:2 * HID], ALU.mult).then_inc(S("b_act"), 1)
                if first >= 3:
                    v.wait_ge(S("b_y"), t - 2)
                    slot = (q + 1) % 4
                    if first >= 7:
                        v.wait_ge(st_b[slot], (t - (3 + slot)) * 4)
                    nc.vector.tensor_copy(yb[:, slot, :], bank[7 - k][:, 0:D]).then_inc(S("b_ys"), 1)

            blocks(v, b_step)
            v.wait_ge(S("w1_h"), 1)
            nc.vector.tensor_tensor(f1w1_l[:], f1w1_s[:], f1w1_h[:], ALU.subtract).then_inc(prep, 1)
            v.wait_ge(ld_c, 16)
            nc.vector.tensor_scalar(wqv_g[:], wqv_s[:], tg[:, 1:2], None, ALU.mult).then_inc(prep, 1)

            def comb(u, s, k, a):
                if k == 0 and a == 0:
                    v.wait_ge(back_s[s], (u - s) * 64 + 128)
                if k == 1 and a == 0:
                    v.wait_ge(S("c_sum"), 1 + u * 2 + 1)
                for c in range(2):
                    xk = xs[:, u * 4 + (2 * a + c), :]
                    last = nc.vector.scalar_tensor_tensor(xk, yg[:, s, 4 * a + 2 * k + c, :],
                                                          kept_w[:, u * 2 + a, 2 * k + c:2 * k + c + 1], xk, ALU.mult, ALU.add)
                if a == 1:
                    last.then_inc(S("c_sum"), 1)

            def c_rmx(u):
                v.wait_ge(S("c_s"), u + 1)
                nc.vector.tensor_reduce(rmx[:], bank[1][:].rearrange("p (c k) -> p c k", k=P), AX, ALU.max).then_inc(S("c_rmx"), 1)

            def c_nmx(u):
                v.wait_ge(S("c_rmx"), u + 1)
                nc.vector.tensor_scalar(nmx[:], rmx[:], -1.0, None, ALU.mult).then_inc(S("c_nmx"), 1)
                nc.vector.tensor_scalar(mcol[:], rmx[:], gate[:, 4:5], None, ALU.add).then_inc(S("c_mcol"), 1)

            def maxima():
                return bank[2][0:4, P:2 * P].rearrange("p (b l) -> p b l", l=L)

            def c_bm(u):
                v.wait_ge(S("c_mt"), u + 1)
                nc.vector.tensor_reduce(bm[:], maxima(), AX, ALU.max).then_inc(S("c_bm"), 1)

            def c_bsub(u):
                v.wait_ge(S("c_bm"), u + 1)
                nc.vector.tensor_tensor(brow[:], maxima(), bm[:].unsqueeze(2).to_broadcast([4, 2, L]), ALU.subtract).then_inc(S("c_bsub"), 1)

            def c_bs(u):
                v.wait_ge(S("c_bexp"), u + 1)
                nc.vector.tensor_reduce(bs[:], brow[:], AX, ALU.add).then_inc(S("c_bs"), 1)

            def c_br(u):
                v.wait_ge(S("c_bs"), u * 2 + 1)
                nc.vector.reciprocal(br[:], bs[:]).then_inc(S("c_bs"), 1)

            def c_wrow(u):
                v.wait_ge(S("c_bs"), u * 2 + 2)
                nc.vector.tensor_tensor(wrow[:].rearrange("p (b l) -> p b l", l=L), brow[:],
                                        br[:].unsqueeze(2).to_broadcast([4, 2, L]), ALU.mult).then_inc(S("c_wrow"), 1)

            def c_wbd(u):
                v.wait_ge(S("c_wt"), u + 1)
                nc.vector.tensor_tensor(wbd[:], bank[2][:, 4:8].unsqueeze(2).to_broadcast([P, 4, 2]),
                                        cst[:, C_BI:C_BI + 2].unsqueeze(1).to_broadcast([P, 4, 2]), ALU.mult).then_inc(S("c_wbd"), 1)

            def c_hcs(u):
                v.wait_ge(S("c_hc"), u + 1)
                nc.vector.tensor_copy(hc[:], bank[2][:, 8:16]).then_inc(S("c_hcs"), 1)

            def c_ehc(u, s):
                v.wait_ge(S("c_hcs"), u + 1)
                nc.vector.tensor_tensor(ehc[:, s, :].rearrange("p (b l) -> p b l", l=L),
                                        xT[:, s, :].rearrange("p (b l) -> p b l", l=L),
                                        hc[:].unsqueeze(2).to_broadcast([P, 8, L]), ALU.mult).then_inc(S("c_ehc"), 1)

            def c_rsm(u, s):
                v.wait_ge(S("c_exp"), u + 1)
                nc.vector.reciprocal(rsm[:], sm[:, s, :]).then_inc(S("c_rsm"), 1)

            def c_ehq(u, s):
                v.wait_ge(S("c_hqs"), u + 1)
                nc.vector.tensor_tensor(ehq[:], hqT[:], xT[:, s, :], ALU.mult).then_inc(S("c_ehq"), 1)

            def c_x(u, s):
                v.wait_ge(S("c_y"), u + 1)
                xu = xs[:, bass.ds(u * 4, 4), :] if not isinstance(u, int) else xs[:, 4 * u:4 * u + 4, :]
                nc.vector.tensor_tensor(xu, bank[5 + s][:].rearrange("p (c d) -> p c d", d=D), xu, ALU.add).then_inc(S("c_x"), 1)

            def it_c(u, s):
                this, nxt, got, was = has(u, U4), has(u + 1, U4), has(u + 3, U4), has(u - 1, U4)
                if this:
                    c_ehq(u, s)
                if nxt:
                    c_rmx(u + 1)
                    c_nmx(u + 1)
                if was:
                    c_x(u - 1, 1 - s)
                if has(u + 2, U4):
                    wait(v, S("c_hc"), u + 1)
                    norm(u + 2, 4, xn[:, s], "c_ln", 2)
                if was:
                    sums(3, u - 1, 4)
                if nxt:
                    c_rsm(u + 1, 1 - s)
                    c_bm(u + 1)
                if got:
                    comb(u + 3, 1 - s, 0, 0)
                if nxt:
                    c_bsub(u + 1)
                if got:
                    comb(u + 3, 1 - s, 0, 1)
                if nxt:
                    c_bs(u + 1)
                if was:
                    moments(3, u - 1, 4)
                if nxt:
                    c_br(u + 1)
                if got:
                    comb(u + 3, 1 - s, 1, 0)
                if nxt:
                    c_wrow(u + 1)
                if got:
                    comb(u + 3, 1 - s, 1, 1)
                if nxt:
                    c_wbd(u + 1)
                if got:
                    sums(2, u + 3, 4)
                if nxt:
                    c_hcs(u + 1)
                if got:
                    moments(2, u + 3, 4)
                if nxt:
                    c_ehc(u + 1, 1 - s)

            pipelined(v, it_c, -3, 1, U4 - 3, U4 + 1)

            def d_gate(u, s, k):
                v.wait_ge(S("d_gelu"), 1 + u * 4 + (k + 1))
                if k == 0:
                    v.wait_ge(S("cmb"), u + 1)
                wait(v, S("d_ht"), u * 4 + k)
                nc.vector.tensor_tensor(hgg[:, k % 2, :].rearrange("p (e r) -> p e r", r=R),
                                        hg[:, k % 2, :].rearrange("p (e r) -> p e r", r=R),
                                        cmb[:, s, k, :].unsqueeze(2).to_broadcast([P, E, R]), ALU.mult).then_inc(S("d_hgg"), 1)

            def d_acc(u, k):
                v.wait_ge(S("d_y"), 1 + u * 4 + (k + 1))
                xk = xs[:, u * 4 + k, :]
                nc.vector.tensor_tensor(xk, bank[5 + k % 2][:, 0:D], xk, ALU.add).then_inc(S("d_x"), 1)

            def d_share(u):
                v.wait_ge(S("oh"), UA * 2 + u * 2 + 2)
                v.wait_ge(S("w"), UA * 2 + u * 2 + 2)
                for h, w in enumerate((w1g, w2g)):
                    nc.vector.tensor_tensor(oh[:, h], oh[:, h], w[:].unsqueeze(2).to_broadcast([P, 4, E]), ALU.mult).then_inc(S("ohw"), 1)

            def d_cmb(u, s):
                v.wait_ge(S("ohw"), u * 2 + 2)
                nc.vector.tensor_tensor(cmb[:, s], oh[:, 0], oh[:, 1], ALU.add).then_inc(S("cmb"), 1)

            def it_d(u, s):
                this, nxt = has(u, U4), has(u + 1, U4)
                if this:
                    d_gate(u, s, 1)
                if has(u + 2, U4):
                    wait(v, S("d_xt"), u + 1)
                    norm(u + 2, 4, xn[:, s], "d_ln", 3)
                if has(u - 1, U4):
                    d_acc(u - 1, 3)
                if this:
                    d_gate(u, s, 2)
                if nxt:
                    logits(3, u + 1, 4, bank[7][:, 0:4 * E].rearrange("p (c e) -> p c e", e=E))
                    largest(3, u + 1, 4)
                    experts(3, u + 1, 4)
                if this:
                    d_gate(u, s, 3)
                if nxt:
                    as_float(3, u + 1, 4)
                if this:
                    d_acc(u, 0)
                if nxt:
                    one_hot(3, u + 1, 4)
                    denominator(3, u + 1, 4)
                    inverse(3, u + 1, 4)
                    first_weight(3, u + 1, 4, 3, SCALING, w1g[:])
                if this:
                    d_acc(u, 1)
                if nxt:
                    second_weight(3, u + 1, 4, w1g[:], w2g[:])
                    d_share(u + 1)
                    d_cmb(u + 1, 1 - s)
                    d_gate(u + 1, 1 - s, 0)
                if this:
                    d_acc(u, 2)

            pipelined(v, it_d, -2, 1, U4 - 3, U4 + 1)

        @block.tensor
        def _(pe):
            start_at_one(pe, "tensor")
            mm = nc.tensor.matmul

            pe.wait_ge(prep, 7)
            mm(bank[7][0:1, 0:D], colv[:, BV:BV + 1], wo_s[:], start=True, stop=False)
            mm(bank[7][0:1, 0:D], ones[0:1, 0:1], rowv[0:1, R_BO:R_BO + D], start=False, stop=True).then_inc(prep_pe, 1)

            def transposes(done, dst, src, n):
                for c in range(n):
                    last = nc.tensor.transpose(dst[:, P * c:P * (c + 1)], src(c), ident)
                last.then_inc(S(done), 1)

            def a_xt(u, s):
                pe.wait_ge(S("a_ln"), u + 1)
                wait(pe, S("a_qks"), u)
                transposes("a_xt", bank[4], lambda c: xn[:, s, c, :], 2)

            def a_v(u, s):
                pe.wait_ge(S("a_nrm"), 1 + u)
                for b in range(4):
                    for e in range(2):
                        last = mm(bank[5][L * e:L * (e + 1), P * b:P * (b + 1)], cT[:, s, L * b:L * (b + 1)],
                                  wv_eo[:, e, :], start=True, stop=True)
                last.then_inc(S("a_v"), 1)

            def a_qk(u, s):
                pe.wait_ge(S("a_xts"), u + 1)
                pe.wait_ge(ld_cT[s], (u - s) * 8 + 16)
                mm(bank[4][:, 0:2 * P], wq_s[:], xT[:, 0, 0:2 * P], start=True, stop=True)
                mm(bank[4][:, 2 * P:4 * P], wk_s[:], cT[:, s, 0:2 * P], start=True, stop=True).then_inc(S("a_qk"), 1)

            def a_s(u, s, g):
                if g == 0:
                    pe.wait_ge(S("a_qks"), u + 1)
                wait(pe, S("a_sub"), u * 4 + (g - 1))
                for p in range(2):
                    for b in range(2):
                        t = P * p + L * b
                        last = mm(bank[g % 2][L * b:L * (b + 1), 256 * p:256 * (p + 1)], QT[:, s, g, t:t + L],
                                  Kb[:, s, :, t:t + L], start=True, stop=True)
                last.then_inc(S("a_s"), 1)

            def a_pt(u, s, g):
                pe.wait_ge(S("a_exp"), u * 4 + (g + 1))
                wait(pe, S("a_pts"), u * 4 + g)
                transposes("a_pt", bank[6 + g % 2], lambda c: Pr[:, s, g, P * c:P * (c + 1)], 4)

            def a_pv(u, s, g):
                pe.wait_ge(S("a_pts"), 1 + u * 4 + (g + 1))
                if g == 0:
                    pe.wait_ge(S("a_vs"), u + 1)
                for p in range(2):
                    for h in range(2):
                        for b in range(2):
                            m = (p * 8 + 2 * g + h) * 18
                            c = P * (2 * p + h) + L * b
                            last = mm(bank[5][L * b:L * (b + 1), m:m + 18], PT[:, g, c:c + L],
                                      Vb[:, s, 2 * p + b, 2 * g + h, :], start=True, stop=True)
                if g == NG - 1:
                    last.then_inc(S("a_pv"), 1)

            def a_at(u):
                pe.wait_ge(S("a_nrm"), 1 + u + 1)
                pe.wait_ge(S("a_x"), 1 + u)
                transposes("a_at", bank[2], lambda c: att[:, D * c:D * (c + 1)], 2)

            def a_y(u):
                pe.wait_ge(S("a_ats"), u + 1)
                for c in range(2):
                    o = bank[2][:, P * (2 + c):P * (3 + c)]
                    mm(o, attT[:, P * c:P * (c + 1)], wo_s[:], start=True, stop=False)
                    last = mm(o, ones[:], row0[:], start=False, stop=True)
                last.then_inc(S("a_y"), 1)

            pe.wait_ge(prep_b0, 1)

            def r_x(w, s):
                pe.wait_ge(S("r_ln"), w + 1)
                pe.wait_ge(S("r_run"), w + 1)
                transposes("r_xt", bank[3], lambda c: xr[:, s, c, :], 2)

            def r_lg(w):
                pe.wait_ge(S("r_xts"), w + 1)
                for c in range(2):
                    last = mm(bank[3][:, 2 * P + E * c:2 * P + E * (c + 1)], xT[:, 1, P * c:P * (c + 1)], f0g_s[:], start=True, stop=True)
                last.then_inc(S("lgp"), 1)

            def r_rank(w):
                pe.wait_ge(S("r_m"), w + 1)
                of = [bank[3][:, RK + E * c:RK + E * (c + 1)] for c in range(3)]
                mm(of[0], upb[:], chosen[:, 0, :], start=True, stop=True)
                mm(of[1], onb[:], chosen[:, 0, :], start=True, stop=False)
                mm(of[1], upb[:], chosen[:, 1, :], start=False, stop=True)
                mm(of[2], onb[:], chosen[:, 0, :], start=True, stop=False)
                mm(of[2], onb[:], chosen[:, 1, :], start=False, stop=True).then_inc(S("r_rank"), 1)

            pe.wait_ge(S("r_prep"), 1)
            pe.wait_ge(ld_f0g, 16)

            def it_a(u, s):
                if has(u):
                    a_pt(u, s, 0)
                    a_pt(u, s, 1)
                    a_v(u, s)
                if has(u + 1):
                    a_s(u + 1, 1 - s, 0)
                if has(u - 1):
                    a_at(u - 1)
                if has(u + 2):
                    a_xt(u + 2, s)
                if has(u + 1):
                    a_s(u + 1, 1 - s, 1)
                if has(u - 2):
                    r_x(u - 2, s)
                if has(u):
                    a_pt(u, s, 2)
                if has(u + 1):
                    a_s(u + 1, 1 - s, 2)
                if has(u):
                    a_pt(u, s, 3)
                if has(u - 1):
                    a_y(u - 1)
                if has(u - 2):
                    r_lg(u - 2)
                if has(u + 1):
                    a_s(u + 1, 1 - s, 3)
                if has(u):
                    a_pv(u, s, 0)
                    a_pv(u, s, 1)
                if has(u + 2):
                    a_qk(u + 2, s)
                if has(u):
                    a_pv(u, s, 2)
                    a_pv(u, s, 3)
                if has(u - 2):
                    r_rank(u - 2)

            pipelined(pe, it_a, -3, 3, UA - 3, UA + 3)

            pe.wait_ge(S("t_col"), 2)
            for h in range(2):
                mm(bank[0][0:1, 2 * h * NB:(2 * h + 1) * NB], en[:], cst[:, C_BD + h * NB:C_BD + (h + 1) * NB], start=True, stop=True)
            mm(bank[0][0:1, NB:2 * NB], first_row[:], cst[:, C_ID:C_ID + NB], start=True, stop=True).then_inc(S("t_row"), 1)
            pe.wait_ge(S("table"), 2)
            pe.wait_ge(ld_f0, 32)
            pe.wait_ge(S("w12_l"), E)

            experts_of = {}

            def load_experts(t, n):
                experts_of.clear()
                for j in range(0, n, PACK):
                    w = pe.value_load(table[0:1, 0, bass.ds(t + j, 1)], min_val=0, max_val=E ** PACK - 1)
                    for k in range(min(PACK, n - j)):
                        experts_of[(t if isinstance(t, int) else -3) + j + k] = (w >> (3 * k)) & (E - 1)

            def expert(t, q, behind):
                return experts_of[(t if isinstance(t, int) else q) - behind]

            def b_step(t, q, first, last):
                k = q % 2
                if last >= 0:
                    pe.wait_ge(ld_b[q % 4], (t - q % 4) * 4 + 16)
                    transposes("b_xt", bank[k], lambda c: xb[:, q % 4, :], 1)
                if first >= 1 and last >= -1:
                    e = expert(t, q, 1)
                    pe.wait_ge(S("b_xls"), t)
                    high, low = (w[:, bass.ds(e, 1), :].rearrange("p e n -> p (e n)") for w in (f0w12_h, f0w12_l))
                    mm(bank[3 - k][:], xbh[:, 1 - k, :], high, start=True, stop=False)
                    mm(bank[3 - k][:], xbh[:, 1 - k, :], low, start=False, stop=False)
                    mm(bank[3 - k][:], xbl[:, 1 - k, :], high, start=False, stop=True).then_inc(S("b_hg"), 1)
                if first >= 2 and last >= -2:
                    pe.wait_ge(S("b_act"), t - 1)
                    transposes("b_at", bank[4 + k], lambda c: act[:, k, P * c:P * (c + 1)], 2)
                if first >= 3:
                    e = expert(t, q, 3)
                    pe.wait_ge(S("b_ats"), t - 2)
                    if first >= 5:
                        pe.wait_ge(S("b_ys"), t - 4)
                    for j in range(2):
                        last_mm = mm(bank[7 - k][:, 0:D], aT[:, 1 - k, j, :],
                                     f0w3_s[:, bass.ds(e, 1), j, :].rearrange("p e n -> p (e n)"), start=j == 0, stop=j == 1)
                    last_mm.then_inc(S("b_y"), 1)

            blocks(pe, b_step, load_experts)

            pe.wait_ge(S("b_ys"), NB)
            pe.wait_ge(prep, 10)

            def c_xt(u, s):
                pe.wait_ge(S("c_ln"), u + 1)
                transposes("c_xt", bank[0], lambda c: xn[:, s, c, :], 4)

            def c_s(u, s):
                pe.wait_ge(ld_cC[s], (u - s) * 16 + 32)
                pe.wait_ge(S("c_e3"), u + 1)
                mm(bank[1][:], farb[:, 0:P], farb[:, P:5 * P], start=True, stop=False, skip_group_check=True)
                for c in range(4):
                    last = mm(bank[1][:, P * c:P * (c + 1)], e3[:, P * c:P * (c + 1)], cT[:, s, P * c:P * (c + 1)],
                              start=False, stop=True, skip_group_check=True)
                last.then_inc(S("c_s"), 1)

            def c_own(u, s):
                pe.wait_ge(S("c_xts"), u + 1)
                wait(pe, S("c_hcs"), u)
                for c in range(4):
                    mm(bank[2][0:4, P:2 * P], w1c[:, c, :], xT[:, s, P * c:P * (c + 1)], start=c == 0, stop=False)

            def c_mt(u):
                pe.wait_ge(S("c_mcol"), u + 1)
                mm(bank[2][0:4, P:2 * P], mcol[:], ident, start=False, stop=True).then_inc(S("c_mt"), 1)

            def c_wt(u):
                wait_alone(pe, S("c_wrow"), u + 1)
                nc.tensor.transpose(bank[2][:, 4:8], wrow[:], cst[0:4, C_ID:C_ID + 4]).then_inc(S("c_wt"), 1)

            def c_hc(u, s):
                pe.wait_ge(S("c_wbd"), u + 1)
                for c in range(4):
                    last = mm(bank[2][:, 8 + 2 * c:10 + 2 * c], xn[:, s, c, :], wbd[:, c, :], start=True, stop=True)
                last.then_inc(S("c_hc"), 1)

            def c_pt(u, s):
                pe.wait_ge(S("c_nrm"), u + 1)
                transposes("c_pt", bank[3], lambda c: Pc[:, s, c, :], 4)

            def c_hq(u, s):
                pe.wait_ge(S("c_pts"), u + 1)
                wait(pe, S("c_hqs"), u)
                for c in range(4):
                    last = mm(bank[4][:, P * c:P * (c + 1)], ctk[:, s, c, :], PcT[:, P * c:P * (c + 1)], start=True, stop=True)
                last.then_inc(S("c_hq"), 1)

            def c_y(u, s, c):
                if c == 0:
                    pe.wait_ge(S("c_ehq"), u + 1)
                    pe.wait_ge(S("c_ehc"), u + 1)
                    wait(pe, S("c_x"), u)
                o = bank[5 + s][:, P * c:P * (c + 1)]
                tok = slice(P * c, P * (c + 1))
                for i, f in enumerate((xT[:, s, tok], hqT[:, tok], ehq[:, tok], ehc[:, s, tok])):
                    mm(o, f, wqv_g[:, i, :], start=i == 0, stop=False)
                last = mm(o, ones[:], row1[:], start=False, stop=True)
                if c == 3:
                    last.then_inc(S("c_y"), 1)

            def it_c(u, s):
                this, nxt = has(u, U4), has(u + 1, U4)
                if nxt:
                    c_s(u + 1, 1 - s)
                    c_own(u + 1, 1 - s)
                if this:
                    c_y(u, s, 0)
                if has(u + 2, U4):
                    c_xt(u + 2, s)
                if nxt:
                    c_mt(u + 1)
                if this:
                    c_y(u, s, 1)
                    c_y(u, s, 2)
                if nxt:
                    c_pt(u + 1, 1 - s)
                if this:
                    c_y(u, s, 3)
                if nxt:
                    c_wt(u + 1)
                    c_hq(u + 1, 1 - s)
                    c_hc(u + 1, 1 - s)

            pipelined(pe, it_c, -3, 1, U4 - 3, U4 + 1)

            pe.wait_ge(S("c_x"), 1 + U4)
            pe.wait_ge(ld_f1, 48)

            def d_xt(u, s):
                pe.wait_ge(S("d_ln"), u + 1)
                transposes("d_xt", bank[0], lambda c: xn[:, s, c, :], 4)

            def d_lg(u, s):
                pe.wait_ge(S("d_xts"), u + 1)
                for c in range(4):
                    o = bank[7][:, E * c:E * (c + 1)]
                    mm(o, xT[:, s, P * c:P * (c + 1)], f1g_s[:], start=True, stop=False)
                    last = mm(o, ones[:], rowv[0:1, R_BG:R_BG + E], start=False, stop=True)
                last.then_inc(S("lgp"), 1)

            def d_h(u, s, k):
                wait(pe, S("d_gelu"), u * 4 + k)
                if k == 0:
                    pe.wait_ge(S("d_xls"), u + 1)
                o, high, low = bank[1 + k % 2][:], xTh[:, s, P * k:P * (k + 1)], xTl[:, s, P * k:P * (k + 1)]
                mm(o, high, f1w1_h[:], start=True, stop=False)
                mm(o, high, f1w1_l[:], start=False, stop=False)
                mm(o, low, f1w1_h[:], start=False, stop=True).then_inc(S("d_h"), 1)

            def d_ht(u, k):
                pe.wait_ge(S("d_hgg"), 1 + u * 4 + (k + 1))
                wait(pe, S("d_hts"), u * 4 + k)
                transposes("d_ht", bank[3 + k % 2], lambda c: hgg[:, k % 2, P * c:P * (c + 1)], 4)

            def d_y(u, k):
                pe.wait_ge(S("d_hts"), 1 + u * 4 + (k + 1))
                wait(pe, S("d_x"), u * 4 + k)
                for c in range(4):
                    last = mm(bank[5 + k % 2][:, 0:D], hT[:, k % 2, P * c:P * (c + 1)], f1w2_s[:, c, :],
                              start=c == 0, stop=c == 3)
                last.then_inc(S("d_y"), 1)

            def it_d(u, s):
                this, nxt = has(u, U4), has(u + 1, U4)
                if nxt:
                    d_xt(u + 1, 1 - s)
                for k in range(4):
                    if k < 2 and this:
                        d_h(u, s, k + 2)
                    if k >= 2 and nxt:
                        d_h(u + 1, 1 - s, k - 2)
                    if this:
                        d_ht(u, k)
                    if k == 0 and has(u - 1, U4):
                        d_y(u - 1, 3)
                    if k == 0 and nxt:
                        d_lg(u + 1, 1 - s)
                    if k > 0 and this:
                        d_y(u, k - 1)

            pipelined(pe, it_d, -2, 1, U4 - 3, U4 + 1)


def kernel(**inputs):
    import concourse.bacc as bacc
    from concourse.bass_utils import run_bass_kernel_spmd

    a = {k: np.asarray(v) for k, v in inputs.items()}
    consts, far = constants()
    lay = np.ascontiguousarray
    sim = a["L1_xattn_w_sim"].reshape(3, D)
    arrays = {
        "x": a["x"].reshape(TOKENS, D),
        "ctx_tok": a["ctx_1024"].reshape(TOKENS, D),
        "ctx_t": lay(a["ctx_1024"].reshape(TOKENS, D).T),
        "wq": lay(a["L0_xattn_wq_w"].T),
        "wk": lay(a["L0_xattn_wk_w"].T),
        "wv": lay(a["L0_xattn_wv_w"].T),
        "wo": lay(a["L0_xattn_wo_w"].T),
        "cols": lay(np.stack([a["L0_xattn_wq_b"], a["L0_xattn_wk_b"], a["L0_xattn_wv_b"], sim[0], sim[1], sim[2]], 1)),
        "rows": lay(np.concatenate([a["L0_xattn_wo_b"], a["L1_xattn_b_qv"], a["L1_ffn_bg"]])[None]),
        "gates": lay(np.concatenate([a["g_xattn"], a["g_ffn"], a["L1_xattn_b_sim"]])),
        "consts": consts,
        "far": far,
        "f0_wg": a["L0_ffn_Wg"],
        "f0_w12": lay(np.concatenate([a["L0_ffn_W1"], a["L0_ffn_W2"]], 2).transpose(1, 0, 2)),
        "f0_w3": lay(a["L0_ffn_W3"].reshape(E, 2, P, D).transpose(2, 0, 1, 3)),
        "wqv": lay(a["L1_xattn_W_qv"].reshape(4, D, D).transpose(1, 0, 2)),
        "f1_wg": lay(a["L1_ffn_Wg"].T),
        "f1_w1": lay(a["L1_ffn_W1"].reshape(E * R, D).T),
        "f1_w2": lay(a["L1_ffn_W2"].transpose(0, 2, 1).reshape(4, P, D).transpose(1, 0, 2)),
    }
    nc = bacc.Bacc("TRN2", target_bir_lowering=False, num_devices=1)
    args = {n: nc.dram_tensor(n + "_dram", v.shape, mybir.dt.from_np(v.dtype), kind="ExternalInput").ap()
            for n, v in arrays.items()}
    args["out"] = nc.dram_tensor("out_dram", (TOKENS, D), F32, kind="ExternalOutput").ap()
    flamingo(nc, **args)
    r = run_bass_kernel_spmd(nc, [{n + "_dram": v for n, v in arrays.items()}], core_ids=[0])
    return r.results[0]["out_dram"].reshape(a["x"].shape)
```
